# Optimizing a Trainium2 kernel written in Bass

```python
import numpy as np
import jax
import jax.numpy as jnp

def _softmax(x, axis=-1):
    return jax.nn.softmax(x, axis=axis)

def _gelu(x):
    return jax.nn.gelu(x, approximate=True)

def _silu(x):
    return jax.nn.silu(x)

def _sigmoid(x):
    return jax.nn.sigmoid(x)

def _layernorm(x, axis=-1, eps=1e-05):
    m = jnp.mean(x, axis=axis, keepdims=True)
    v = jnp.var(x, axis=axis, keepdims=True)
    return (x - m) / jnp.sqrt(v + eps)

def _scatter_add(tgt, idx, src, axis=0):
    return tgt.at[idx].add(src)

def _segment_sum(src, seg, n):
    return jax.ops.segment_sum(src, seg, n)
kernel_name = 'mk_xattn_ffn_d2_seqx_r4_82f186'

def setup_inputs(seed: int=0):
    np.random.seed(seed)
    _w = jnp.asarray

    def _rec_inputs():
        import jax
        import jax.numpy as jnp
        _rk = jax.random.key(seed)
        x = -0.0002928 + 1 * jax.random.normal(jax.random.fold_in(_rk, 1), (4, 1024, 256), jnp.float32)
        _lenS = 1024 - jax.random.randint(jax.random.fold_in(_rk, 7), (4,), 0, max(1, 1024 // 4) + 1, jnp.int32)
        _lenS2 = 77 - jax.random.randint(jax.random.fold_in(_rk, 8), (4,), 0, max(1, 77 // 4) + 1, jnp.int32)
        _ctx_1024P = jax.random.normal(jax.random.fold_in(_rk, 11), (4, 16, 256), jnp.float32)
        _ctx_1024c = jax.random.dirichlet(jax.random.fold_in(_rk, 511), 0.3 * jnp.ones((16,), jnp.float32), (4, 77))
        _ctx_1024t = jnp.einsum('bsk,bkd->bsd', _ctx_1024c, _ctx_1024P)
        _ctx_1024t = _ctx_1024t * jax.lax.rsqrt(jnp.mean(jnp.square(_ctx_1024t)) + 1e-12) * 0.953939
        ctx_1024 = -1.39393e-06 + 0.999914 * (_ctx_1024t + 0.3 * jax.random.normal(jax.random.fold_in(_rk, 611), (4, 77, 256), jnp.float32))
        _validS = jnp.arange(1024)[None, :] < _lenS[:, None]
        _validS2 = jnp.arange(77)[None, :] < _lenS2[:, None]
        _causal = jnp.tril(jnp.ones((1024, 1024), dtype=bool))
        mask_BxS2_ik0 = jnp.where(jnp.broadcast_to(_validS2[:, :], (4, 77)), 0, 1).astype(jnp.int32)
        return (x, ctx_1024, mask_BxS2_ik0)
    x, ctx_1024, mask_BxS2_ik0 = _rec_inputs()

    def _L0_xattn_setup():
        import jax, jax.numpy as jnp
        import numpy as np
        D_MODEL = 256
        N_HEADS = 16
        D_K = D_MODEL // N_HEADS
        key = jax.random.key(seed)
        ks = jax.random.split(key, 11)
        B, L, S = (2, 512, 512)
        scale = 1.0 / np.sqrt(D_MODEL)
        return {'x_q': jax.random.normal(ks[0], (B, L, D_MODEL), jnp.float32), 'x_k': jax.random.normal(ks[1], (B, S, D_MODEL), jnp.float32), 'x_v': jax.random.normal(ks[2], (B, S, D_MODEL), jnp.float32), 'W_Q': jax.random.normal(ks[3], (D_MODEL, D_MODEL), jnp.float32) * scale, 'b_Q': jax.random.normal(ks[4], (D_MODEL,), jnp.float32) * 0.01, 'W_K': jax.random.normal(ks[5], (D_MODEL, D_MODEL), jnp.float32) * scale, 'b_K': jax.random.normal(ks[6], (D_MODEL,), jnp.float32) * 0.01, 'W_V': jax.random.normal(ks[7], (D_MODEL, D_MODEL), jnp.float32) * scale, 'b_V': jax.random.normal(ks[8], (D_MODEL,), jnp.float32) * 0.01, 'W_O': jax.random.normal(ks[9], (D_MODEL, D_MODEL), jnp.float32) * scale, 'b_O': jax.random.normal(ks[10], (D_MODEL,), jnp.float32) * 0.01}
    _L0_xattn_all = _L0_xattn_setup()
    _L0_xattn_in = {k: v for k, v in _L0_xattn_all.items() if k in ('W_Q', 'b_Q', 'W_K', 'b_K', 'W_V', 'b_V', 'W_O', 'b_O')}
    del _L0_xattn_all

    def _L0_ffn_setup():
        import jax, jax.numpy as jnp
        import numpy as np
        LATENT = 256
        LEAF_W = 64
        DEPTH = 4
        N_LEAVES = 2 ** DEPTH
        N_NODES = 2 ** DEPTH - 1
        B, S = (4, 512)

        def _fff_params(key, prefix):
            ks = jax.random.split(key, 4)
            d, h, l, n = (LATENT, LEAF_W, N_LEAVES, N_NODES)
            s_in = 1.0 / np.sqrt(d).astype(np.float32)
            s_h = 1.0 / np.sqrt(h).astype(np.float32)
            return {f'{prefix}_node_w': jax.random.normal(ks[0], (n, d), jnp.float32) * s_in, f'{prefix}_node_b': jax.random.normal(ks[1], (n,), jnp.float32) * s_in, f'{prefix}_w1': jax.random.normal(ks[2], (l, d, h), jnp.float32) * s_in, f'{prefix}_b1': jnp.zeros((l, h), jnp.float32), f'{prefix}_w2': jax.random.normal(ks[3], (l, h, d), jnp.float32) * s_h, f'{prefix}_b2': jnp.zeros((l, d), jnp.float32)}

        def _fff(x, node_w, node_b, w1, b1, w2, b2):
            Bx, Sx, D = x.shape
            xf = x.reshape(-1, D)
            N = xf.shape[0]
            cur = jnp.zeros((N,), jnp.int32)
            for _ in range(DEPTH):
                pw = node_w[cur]
                score = jnp.einsum('nd,nd->n', xf, pw) + node_b[cur]
                cur = 2 * cur + 1 + (score >= 0).astype(jnp.int32)
            leaf = cur - N_NODES
            sel = jax.nn.one_hot(leaf, N_LEAVES, dtype=xf.dtype)
            hidden_all = jax.nn.relu(jnp.einsum('nd,ldh->lnh', xf, w1) + b1[:, None, :])
            hidden = hidden_all * sel.T[:, :, None]
            out = jnp.einsum('lnh,lho->no', hidden, w2) + sel @ b2
            return out.reshape(Bx, Sx, D)
        key = jax.random.key(seed)
        kx, kq, kk, kv = jax.random.split(key, 4)
        inp = {'x': jax.random.normal(kx, (B, S, LATENT), jnp.float32)}
        inp.update(_fff_params(kq, 'q'))
        inp.update(_fff_params(kk, 'k'))
        inp.update(_fff_params(kv, 'v'))
        return inp
    _L0_ffn_all = _L0_ffn_setup()
    _L0_ffn_in = {k: v for k, v in _L0_ffn_all.items() if k in ('q_node_w', 'q_node_b', 'q_w1', 'q_b1', 'q_w2', 'q_b2', 'k_node_w', 'k_node_b', 'k_w1', 'k_b1', 'k_w2', 'k_b2', 'v_node_w', 'v_node_b', 'v_w1', 'v_b1', 'v_w2', 'v_b2')}
    del _L0_ffn_all

    def _L1_xattn_setup():
        import jax, jax.numpy as jnp
        import numpy as np
        B, LQ, LK, D = (4, 512, 512, 256)
        H = 16
        HD = D // H

        def _split_heads(x):
            b, l, _ = x.shape
            return x.reshape(b, l, H, HD).transpose(0, 2, 1, 3)
        key = jax.random.key(seed)
        ks = jax.random.split(key, 10)
        s = 0.02
        return {'hidden_states': jax.random.normal(ks[0], (B, LQ, D), jnp.float32), 'context': jax.random.normal(ks[1], (B, LK, D), jnp.float32), 'attention_mask': jax.random.randint(ks[2], (B, LK), 0, 2, jnp.int32), 'q_w': jax.random.normal(ks[3], (D, D), jnp.float32) * s, 'q_b': jnp.zeros((D,), jnp.float32), 'k_w': jax.random.normal(ks[4], (D, D), jnp.float32) * s, 'k_b': jnp.zeros((D,), jnp.float32), 'v_w': jax.random.normal(ks[5], (D, D), jnp.float32) * s, 'v_b': jnp.zeros((D,), jnp.float32)}
    _L1_xattn_all = _L1_xattn_setup()
    _L1_xattn_in = {k: v for k, v in _L1_xattn_all.items() if k in ('q_w', 'q_b', 'k_w', 'k_b', 'v_w', 'v_b')}
    del _L1_xattn_all

    def _L1_ffn_setup():
        import jax, jax.numpy as jnp
        import numpy as np
        B, T, C = (8, 512, 256)
        H = 1024
        E = 8
        K = 2
        LOAD_FACTOR = 1.2
        N_LAYER = 12

        def _get_expert_inputs(x, logits, expert_capacity):
            Tt = logits.shape[0]
            Cc = x.shape[1]
            top_k_logits, expert_indices = jax.lax.top_k(logits, K)
            expert_probs = jax.nn.softmax(top_k_logits, axis=-1)
            ei = jnp.swapaxes(expert_indices, 0, 1).ravel()
            one_hot = jax.nn.one_hot(ei, E, dtype=jnp.int32)
            pos = jnp.cumsum(one_hot, axis=0) * one_hot - 1
            pos = pos.reshape(-1, Tt, E)
            pos = jnp.swapaxes(pos, 0, 1)
            pos = jnp.max(pos, axis=2)
            ei = jnp.swapaxes(ei.reshape(-1, Tt), 0, 1)
            buf = jnp.zeros((E, expert_capacity, Cc), x.dtype)
            xr = jnp.repeat(x, K, axis=0)
            expert_inputs = buf.at[ei.ravel(), pos.ravel()].add(xr)
            return (expert_probs, pos, ei, expert_inputs)
        key = jax.random.key(seed)
        ks = jax.random.split(key, 9)
        std = 0.02
        proj_std = 0.02 * (2 * N_LAYER) ** (-0.5)
        return {'x': jax.random.normal(ks[0], (B, T, C), jnp.float32), 'router_w': jax.random.normal(ks[1], (C, E), jnp.float32) * std, 'router_b': jnp.zeros((E,), jnp.float32), 'w_c_fc': jax.random.normal(ks[2], (E, C, H), jnp.float32) * std, 'b_c_fc': jnp.zeros((E, 1, H), jnp.float32), 'w_gate': jax.random.normal(ks[3], (E, C, H), jnp.float32) * std, 'b_gate': jnp.zeros((E, 1, H), jnp.float32), 'w_c_proj': jax.random.normal(ks[4], (E, H, C), jnp.float32) * proj_std, 'b_c_proj': jnp.zeros((E, 1, C), jnp.float32)}
    _L1_ffn_all = _L1_ffn_setup()
    _L1_ffn_in = {k: v for k, v in _L1_ffn_all.items() if k in ('router_w', 'router_b', 'w_c_fc', 'b_c_fc', 'w_gate', 'b_gate', 'w_c_proj', 'b_c_proj')}
    del _L1_ffn_all
    return {'x': x, 'ctx_1024': ctx_1024, 'mask_BxS2_ik0': mask_BxS2_ik0, 'L0_xattn_W_Q': _L0_xattn_in['W_Q'], 'L0_xattn_b_Q': _L0_xattn_in['b_Q'], 'L0_xattn_W_K': _L0_xattn_in['W_K'], 'L0_xattn_b_K': _L0_xattn_in['b_K'], 'L0_xattn_W_V': _L0_xattn_in['W_V'], 'L0_xattn_b_V': _L0_xattn_in['b_V'], 'L0_xattn_W_O': _L0_xattn_in['W_O'], 'L0_xattn_b_O': _L0_xattn_in['b_O'], 'L0_ffn_q_node_w': _L0_ffn_in['q_node_w'], 'L0_ffn_q_node_b': _L0_ffn_in['q_node_b'], 'L0_ffn_q_w1': _L0_ffn_in['q_w1'], 'L0_ffn_q_b1': _L0_ffn_in['q_b1'], 'L0_ffn_q_w2': _L0_ffn_in['q_w2'], 'L0_ffn_q_b2': _L0_ffn_in['q_b2'], 'L0_ffn_k_node_w': _L0_ffn_in['k_node_w'], 'L0_ffn_k_node_b': _L0_ffn_in['k_node_b'], 'L0_ffn_k_w1': _L0_ffn_in['k_w1'], 'L0_ffn_k_b1': _L0_ffn_in['k_b1'], 'L0_ffn_k_w2': _L0_ffn_in['k_w2'], 'L0_ffn_k_b2': _L0_ffn_in['k_b2'], 'L0_ffn_v_node_w': _L0_ffn_in['v_node_w'], 'L0_ffn_v_node_b': _L0_ffn_in['v_node_b'], 'L0_ffn_v_w1': _L0_ffn_in['v_w1'], 'L0_ffn_v_b1': _L0_ffn_in['v_b1'], 'L0_ffn_v_w2': _L0_ffn_in['v_w2'], 'L0_ffn_v_b2': _L0_ffn_in['v_b2'], 'L1_xattn_q_w': _L1_xattn_in['q_w'], 'L1_xattn_q_b': _L1_xattn_in['q_b'], 'L1_xattn_k_w': _L1_xattn_in['k_w'], 'L1_xattn_k_b': _L1_xattn_in['k_b'], 'L1_xattn_v_w': _L1_xattn_in['v_w'], 'L1_xattn_v_b': _L1_xattn_in['v_b'], 'L1_ffn_router_w': _L1_ffn_in['router_w'], 'L1_ffn_router_b': _L1_ffn_in['router_b'], 'L1_ffn_w_c_fc': _L1_ffn_in['w_c_fc'], 'L1_ffn_b_c_fc': _L1_ffn_in['b_c_fc'], 'L1_ffn_w_gate': _L1_ffn_in['w_gate'], 'L1_ffn_b_gate': _L1_ffn_in['b_gate'], 'L1_ffn_w_c_proj': _L1_ffn_in['w_c_proj'], 'L1_ffn_b_c_proj': _L1_ffn_in['b_c_proj']}

def reference(x, ctx_1024, mask_BxS2_ik0, L0_xattn_W_Q, L0_xattn_b_Q, L0_xattn_W_K, L0_xattn_b_K, L0_xattn_W_V, L0_xattn_b_V, L0_xattn_W_O, L0_xattn_b_O, L0_ffn_q_node_w, L0_ffn_q_node_b, L0_ffn_q_w1, L0_ffn_q_b1, L0_ffn_q_w2, L0_ffn_q_b2, L0_ffn_k_node_w, L0_ffn_k_node_b, L0_ffn_k_w1, L0_ffn_k_b1, L0_ffn_k_w2, L0_ffn_k_b2, L0_ffn_v_node_w, L0_ffn_v_node_b, L0_ffn_v_w1, L0_ffn_v_b1, L0_ffn_v_w2, L0_ffn_v_b2, L1_xattn_q_w, L1_xattn_q_b, L1_xattn_k_w, L1_xattn_k_b, L1_xattn_v_w, L1_xattn_v_b, L1_ffn_router_w, L1_ffn_router_b, L1_ffn_w_c_fc, L1_ffn_b_c_fc, L1_ffn_w_gate, L1_ffn_b_gate, L1_ffn_w_c_proj, L1_ffn_b_c_proj):
    import jax
    import jax.numpy as jnp

    def _L0_xattn_ref(x_q, x_k, x_v, W_Q, b_Q, W_K, b_K, W_V, b_V, W_O, b_O):
        import jax, jax.numpy as jnp
        import numpy as np
        D_MODEL = 256
        N_HEADS = 16
        D_K = D_MODEL // N_HEADS
        B, L, _ = x_q.shape
        S = x_k.shape[1]
        H, dk = (N_HEADS, D_K)
        Q = (x_q @ W_Q + b_Q).reshape(B, L, H, dk).transpose(0, 2, 1, 3)
        K = (x_k @ W_K + b_K).reshape(B, S, H, dk).transpose(0, 2, 1, 3)
        V = (x_v @ W_V + b_V).reshape(B, S, H, dk).transpose(0, 2, 1, 3)
        scores = jnp.einsum('bhld,bhsd->bhls', Q, K) / jnp.sqrt(jnp.float32(dk))
        attn = jax.nn.softmax(scores, axis=-1)
        ctx = jnp.einsum('bhls,bhsd->bhld', attn, V)
        ctx = ctx.transpose(0, 2, 1, 3).reshape(B, L, H * dk)
        out = ctx @ W_O + b_O
        return out

    def _L0_ffn_ref(x, q_node_w, q_node_b, q_w1, q_b1, q_w2, q_b2, k_node_w, k_node_b, k_w1, k_b1, k_w2, k_b2, v_node_w, v_node_b, v_w1, v_b1, v_w2, v_b2):
        import jax, jax.numpy as jnp
        import numpy as np
        LATENT = 256
        LEAF_W = 64
        DEPTH = 4
        N_LEAVES = 2 ** DEPTH
        N_NODES = 2 ** DEPTH - 1
        B, S = (4, 512)

        def _fff_params(key, prefix):
            ks = jax.random.split(key, 4)
            d, h, l, n = (LATENT, LEAF_W, N_LEAVES, N_NODES)
            s_in = 1.0 / np.sqrt(d).astype(np.float32)
            s_h = 1.0 / np.sqrt(h).astype(np.float32)
            return {f'{prefix}_node_w': jax.random.normal(ks[0], (n, d), jnp.float32) * s_in, f'{prefix}_node_b': jax.random.normal(ks[1], (n,), jnp.float32) * s_in, f'{prefix}_w1': jax.random.normal(ks[2], (l, d, h), jnp.float32) * s_in, f'{prefix}_b1': jnp.zeros((l, h), jnp.float32), f'{prefix}_w2': jax.random.normal(ks[3], (l, h, d), jnp.float32) * s_h, f'{prefix}_b2': jnp.zeros((l, d), jnp.float32)}

        def _fff(x, node_w, node_b, w1, b1, w2, b2):
            Bx, Sx, D = x.shape
            xf = x.reshape(-1, D)
            N = xf.shape[0]
            cur = jnp.zeros((N,), jnp.int32)
            for _ in range(DEPTH):
                pw = node_w[cur]
                score = jnp.einsum('nd,nd->n', xf, pw) + node_b[cur]
                cur = 2 * cur + 1 + (score >= 0).astype(jnp.int32)
            leaf = cur - N_NODES
            sel = jax.nn.one_hot(leaf, N_LEAVES, dtype=xf.dtype)
            hidden_all = jax.nn.relu(jnp.einsum('nd,ldh->lnh', xf, w1) + b1[:, None, :])
            hidden = hidden_all * sel.T[:, :, None]
            out = jnp.einsum('lnh,lho->no', hidden, w2) + sel @ b2
            return out.reshape(Bx, Sx, D)
        q = _fff(x, q_node_w, q_node_b, q_w1, q_b1, q_w2, q_b2)
        k = _fff(x, k_node_w, k_node_b, k_w1, k_b1, k_w2, k_b2)
        v = _fff(x, v_node_w, v_node_b, v_w1, v_b1, v_w2, v_b2)
        scale = 1.0 / np.sqrt(LATENT).astype(np.float32)
        attn = jax.nn.softmax(jnp.einsum('bqd,bkd->bqk', q, k) * scale, axis=-1)
        return jnp.einsum('bqk,bkd->bqd', attn, v)

    def _L1_xattn_ref(hidden_states, context, attention_mask, q_w, q_b, k_w, k_b, v_w, v_b):
        import jax, jax.numpy as jnp
        import numpy as np
        B, LQ, LK, D = (4, 512, 512, 256)
        H = 16
        HD = D // H

        def _split_heads(x):
            b, l, _ = x.shape
            return x.reshape(b, l, H, HD).transpose(0, 2, 1, 3)
        q = _split_heads(hidden_states @ q_w.T + q_b)
        k = _split_heads(context @ k_w.T + k_b)
        v = _split_heads(context @ v_w.T + v_b)
        scores = jnp.einsum('bhqd,bhkd->bhqk', q, k) / jnp.sqrt(jnp.float32(HD))
        mask = (attention_mask > 0)[:, None, None, :]
        scores = jnp.where(mask, -jnp.inf, scores)
        probs = jax.nn.softmax(scores, axis=-1)
        ctx = jnp.einsum('bhqk,bhkd->bhqd', probs, v)
        ctx = ctx.transpose(0, 2, 1, 3).reshape(ctx.shape[0], ctx.shape[2], H * HD)
        return ctx

    def _L1_ffn_ref(x, router_w, router_b, w_c_fc, b_c_fc, w_gate, b_gate, w_c_proj, b_c_proj):
        import jax, jax.numpy as jnp
        import numpy as np
        B, T, C = (8, 512, 256)
        H = 1024
        E = 8
        K = 2
        LOAD_FACTOR = 1.2
        N_LAYER = 12

        def _get_expert_inputs(x, logits, expert_capacity):
            Tt = logits.shape[0]
            Cc = x.shape[1]
            top_k_logits, expert_indices = jax.lax.top_k(logits, K)
            expert_probs = jax.nn.softmax(top_k_logits, axis=-1)
            ei = jnp.swapaxes(expert_indices, 0, 1).ravel()
            one_hot = jax.nn.one_hot(ei, E, dtype=jnp.int32)
            pos = jnp.cumsum(one_hot, axis=0) * one_hot - 1
            pos = pos.reshape(-1, Tt, E)
            pos = jnp.swapaxes(pos, 0, 1)
            pos = jnp.max(pos, axis=2)
            ei = jnp.swapaxes(ei.reshape(-1, Tt), 0, 1)
            buf = jnp.zeros((E, expert_capacity, Cc), x.dtype)
            xr = jnp.repeat(x, K, axis=0)
            expert_inputs = buf.at[ei.ravel(), pos.ravel()].add(xr)
            return (expert_probs, pos, ei, expert_inputs)
        Bb, Tt, Cc = x.shape
        logits = jnp.einsum('btc,ce->bte', x, router_w) + router_b
        cap = int(LOAD_FACTOR * K * Tt // E)
        probs, pos, idx, einp = jax.vmap(lambda xb, lb: _get_expert_inputs(xb, lb, cap))(x, logits)
        if Bb % E == 0:
            t = einp.reshape(E, Bb // E, E, cap, Cc)
            t = jnp.swapaxes(t, 0, 2)
        else:
            t = jnp.swapaxes(einp, 0, 1)
        einp2 = t.reshape(E, Bb * cap, Cc)
        h = jnp.einsum('eti,eih->eth', einp2, w_c_fc) + b_c_fc
        g = jnp.einsum('eti,eih->eth', einp2, w_gate) + b_gate
        o = jnp.einsum('eth,eho->eto', jax.nn.silu(h * g), w_c_proj) + b_c_proj
        if Bb % E == 0:
            o = o.reshape(E, Bb // E, E, cap, Cc)
            o = jnp.swapaxes(o, 0, 2)
            o = o.reshape(Bb, E, cap, Cc)
        else:
            o = o.reshape(E, Bb, cap, Cc)
            o = jnp.swapaxes(o, 0, 1)

        def collect(eo, i, p, pr):
            sel = eo[i, p]
            return jnp.sum(pr[..., None] * sel, axis=1)
        return jax.vmap(collect)(o, idx, pos, probs)
    x = x + _L0_xattn_ref(_layernorm(x, axis=-1), ctx_1024, ctx_1024, L0_xattn_W_Q, L0_xattn_b_Q, L0_xattn_W_K, L0_xattn_b_K, L0_xattn_W_V, L0_xattn_b_V, L0_xattn_W_O, L0_xattn_b_O)
    x = x + _L0_ffn_ref(_layernorm(x, axis=-1), L0_ffn_q_node_w, L0_ffn_q_node_b, L0_ffn_q_w1, L0_ffn_q_b1, L0_ffn_q_w2, L0_ffn_q_b2, L0_ffn_k_node_w, L0_ffn_k_node_b, L0_ffn_k_w1, L0_ffn_k_b1, L0_ffn_k_w2, L0_ffn_k_b2, L0_ffn_v_node_w, L0_ffn_v_node_b, L0_ffn_v_w1, L0_ffn_v_b1, L0_ffn_v_w2, L0_ffn_v_b2)
    x = x + _L1_xattn_ref(_layernorm(x, axis=-1), ctx_1024, mask_BxS2_ik0, L1_xattn_q_w, L1_xattn_q_b, L1_xattn_k_w, L1_xattn_k_b, L1_xattn_v_w, L1_xattn_v_b)
    x = x + _L1_ffn_ref(_layernorm(x, axis=-1), L1_ffn_router_w, L1_ffn_router_b, L1_ffn_w_c_fc, L1_ffn_b_c_fc, L1_ffn_w_gate, L1_ffn_b_gate, L1_ffn_w_c_proj, L1_ffn_b_c_proj)
    return x

_drawn_inputs = setup_inputs


def setup_inputs(seed=0):
    import zlib

    import numpy as np

    out = dict(_drawn_inputs(seed))
    spreads = {'L0_ffn_q_b1': (0.0, 0.8),
     'L0_ffn_q_b2': (0.0, 0.8),
     'L0_ffn_k_b1': (0.0, 0.8),
     'L0_ffn_k_b2': (0.0, 0.8),
     'L0_ffn_v_b1': (0.0, 0.492),
     'L0_ffn_v_b2': (0.0, 0.293),
     'L1_xattn_q_b': (0.0, 0.8),
     'L1_xattn_k_b': (0.0, 2.0),
     'L1_xattn_v_b': (0.0, 0.1),
     'L1_ffn_router_b': (0.0, 0.1),
     'L1_ffn_b_c_fc': (0.0, 0.8),
     'L1_ffn_b_gate': (0.0, 0.8),
     'L1_ffn_b_c_proj': (0.0, 0.456)}
    factors = {'L0_xattn_b_Q': 8.0,
     'L0_xattn_b_K': 64.0,
     'L0_xattn_b_V': 5.748,
     'L0_xattn_b_O': 5.343,
     'L0_ffn_q_node_w': 4.884,
     'L0_ffn_q_node_b': 8.0,
     'L0_ffn_q_w1': 5.429,
     'L0_ffn_q_w2': 4.817,
     'L0_ffn_k_node_w': 4.796,
     'L0_ffn_k_node_b': 8.0,
     'L0_ffn_k_w1': 5.44,
     'L0_ffn_k_w2': 4.707,
     'L0_ffn_v_node_b': 3.504,
     'L1_xattn_q_w': 8.0,
     'L1_xattn_k_w': 7.931,
     'L1_ffn_w_c_fc': 8.0,
     'L1_ffn_w_gate': 8.0,
     'L1_ffn_w_c_proj': 8.0}
    for name, (base, spread) in spreads.items():
        noise = np.random.default_rng([zlib.crc32(name.encode()), seed]).standard_normal(out[name].shape)
        drawn = base * np.exp(spread * noise) if base else spread * noise
        out[name] = jnp.asarray(drawn.astype(out[name].dtype))
    for name, factor in factors.items():
        out[name] = (out[name] * factor).astype(out[name].dtype)
    return out
```

```python
import concourse.bass as bass
from concourse import mybir
from contextlib import ExitStack

F32 = mybir.dt.float32
BF16 = mybir.dt.bfloat16
I32 = mybir.dt.int32
U32 = mybir.dt.uint32
ALU = mybir.AluOpType
ACT = mybir.ActivationFunctionType
AX = mybir.AxisListType

P = 128
B, SEQ, D = 4, 1024, 256
NT = B * SEQ // P
TPB = SEQ // P
GT = 4
DC = D // P
HEADS, DK, CTX = 16, 16, 77
HH = HEADS // 2
HQ = HH // 2
HW = HH * CTX
VW = DK + 1
EPS = 1e-5
NEG = -1e30
STEPS = 2 * TPB
DRAIN = 6

LEAVES, DEPTH, LEAF_W = 16, 4, 64
NODES = LEAVES - 1
NODES3, LEAVES3 = 3 * NODES, 3 * LEAVES
SET_TILES = NT + LEAVES
SET_ROWS = SET_TILES * P
FS = 8
GB = 2
WS = 4
IT_SET = SET_TILES // FS
W1W = DC * LEAF_W + 2
ZR = 16
SA_SCALE = D ** -0.5
EXPERTS, TOPK = 8, 2
CAP = int(1.2 * TOPK * SEQ // EXPERTS)
SLOTS = B * CAP
ROW_TRASH = EXPERTS * SLOTS
SLOT_ROWS = ROW_TRASH + TOPK * NT * P
SLOT_FILL = 10240
HID = 1024
YS = 5
GS = 4


class Link:

    def __init__(self, eng, sem):
        self.eng, self.sem, self.base, self.n = eng, sem, 0, 0

    def restart(self, base):
        self.base, self.n = base, 0

    def count(self, ins):
        self.n += 1
        ins.then_inc(self.sem, 1)

    def wait(self):
        self.eng.wait_ge(self.sem, self.base + self.n)

    def __call__(self, ins):
        self.count(ins)
        self.wait()


def xattn_ffn_kernel(nc, x_in, ctx_in, mask_in, xa, ffn, moe, out):
    es = ExitStack()
    with es:
        def sb(name, shape, dt=F32, scope=es):
            return scope.enter_context(nc.sbuf_tensor(name, shape, dt))

        def pb(name, shape, dt=F32, scope=es):
            return scope.enter_context(nc.psum_tensor(name, shape, dt))

        def sem(name):
            return es.enter_context(nc.semaphore(name))

        x = sb("x", [P, NT, D])
        ident = sb("ident", [P, P])
        stat = sb("stat", [P, TPB, 6])
        mean = sb("mean", [P, TPB])
        rstd = sb("rstd", [P, TPB])
        nw = sb("nw", [P, 2, TPB])
        x_v = x_in.rearrange("b (t p) d -> p (b t) d", p=P)
        out_v = out.rearrange("b (t p) d -> p (b t) d", p=P)

        kb, vb = {}, {}
        kb["c"] = sb("kb_c", [P, B, DC, HH, CTX])
        vb["c"] = sb("vb_c", [CTX, B, HEADS, VW])
        neg = sb("neg", [P, B, CTX], BF16)
        mean128 = sb("mean128", [P, P], BF16)
        wq = {L: sb(f"wq_{L}", [P, DC, D]) for L in "ac"}
        bq = {L: sb(f"bq_{L}", [P, DC]) for L in "ac"}
        bk = {L: sb(f"bk_{L}", [P, DC]) for L in "ac"}
        wo = sb("wo", [P, DC, D])
        bo_bc = sb("bo_bc", [P, D])

        zq = sb("zq", [P, NT, D])
        nodew = sb("nodew", [P, DC, NODES3])
        nodeb = sb("nodeb", [P, NODES3])
        bits = sb("bits", [P, TPB * NODES3])
        path = [sb(f"path{l}", [P, TPB * 3, 2 ** (l + 1)]) for l in range(DEPTH - 1)]
        onehot = sb("onehot", [P, NT, LEAVES3], BF16)
        before = sb("before", [P, NT + 1, LEAVES3], BF16)
        tri = sb("tri", [P, P], BF16)
        ones_bf = sb("ones_bf", [P, P], BF16)
        ones_row = sb("ones_row", [P, LEAVES])
        set_leaf0 = sb("set_leaf0", [1, 3, SET_TILES])
        tile_row = sb("tile_row", [1, SET_TILES])
        expert_id = sb("expert_id", [P, EXPERTS])
        trash = sb("trash", [P, TOPK * TPB, B])
        cnt_i = sb("cnt_i", [P, LEAVES3], I32)
        padded, incl, base = (sb(n, [P, LEAVES3]) for n in ("padded", "incl", "base"))
        rowt = sb("rowt", [P, TPB, LEAVES3])
        rowf = sb("rowf", [P, 3, TPB])
        row_i = sb("row_i", [P, 3, NT], U32)
        leaff = sb("leaff", [1, 3, SET_TILES])
        leaf_i = sb("leaf_i", [1, 3 * SET_TILES], I32)

        routerw = sb("routerw", [P, DC, EXPERTS])
        routerb = sb("routerb", [P, EXPERTS])
        logit = sb("logit", [P, NT, EXPERTS])
        best = sb("best", [P, NT, 8])
        best_i = sb("best_i", [P, NT, 8], U32)
        choice = sb("choice", [P, NT, TOPK])
        prob = sb("prob", [P, TOPK, NT])
        ohs = sb("ohs", [P, TOPK * TPB, B, EXPERTS], BF16)
        ohb = sb("ohb", [P, TOPK * TPB, B, EXPERTS], BF16)
        xrow = sb("xrow", [P, TOPK * TPB, B])
        rankt = sb("rankt", [P, TOPK * TPB, B, EXPERTS])
        rankf = sb("rankf", [P, TOPK * TPB, B])
        read_i = sb("read_i", [P, TOPK * TPB, B], U32)
        write_i = sb("write_i", [P, TOPK * TPB, B], U32)
        batch0 = sb("batch0", [P, B])

        sorted_in, sorted_out = ([nc.dram_tensor(f"sorted_{d}{s}", [SET_ROWS, D], F32, kind="Internal").ap()
                                  for s in range(3)] for d in ("in", "out"))
        slots_in = nc.dram_tensor("slots_in", [SLOT_ROWS, D], F32, kind="Internal").ap()
        slots_out = nc.dram_tensor("slots_out", [EXPERTS * SLOTS, D], F32, kind="Internal").ap()

        with ExitStack() as r1:
            kb["a"] = sb("kb_a", [P, B, DC, HH, CTX], scope=r1)
            vb["a"] = sb("vb_a", [CTX, B, HEADS, VW], scope=r1)
            ctx_sb = sb("ctx_sb", [CTX, B, D], scope=r1)
            ctxT = sb("ctxT", [P, DC, B * CTX], scope=r1)
            wk = {L: sb(f"wk_{L}", [P, DC, D], scope=r1) for L in "ac"}
            wv = {L: sb(f"wv_{L}", [P, DC, D], scope=r1) for L in "ac"}
            kT = {L: sb(f"kT_{L}", [P, DC, B * CTX], scope=r1) for L in "ac"}
            bv_bc = {L: sb(f"bv_{L}", [CTX, D], scope=r1) for L in "ac"}
            mask_sb = sb("mask_sb", [P, B * CTX], I32, scope=r1)
            headsel = sb("headsel", [P, HH], scope=r1)
            sa = {
                "y": sb("y", [P, 2, D], scope=r1),
                "yT": sb("yT", [P, DC, GT * P], scope=r1),
                "qT": sb("qT", [P, 2, DC, GT * P], scope=r1),
                "mx": sb("mx", [P, 2, HH], scope=r1),
                "pr": sb("pr", [P, 2, HH, CTX], scope=r1),
                "prT": sb("prT", [CTX, 2, HH, P], scope=r1),
                "rinv": sb("rinv", [P, 2, HH], scope=r1),
                "o": sb("o", [P, 2, D], scope=r1),
                "oT": sb("oT", [P, DC, P], scope=r1),
            }
        with ExitStack() as r2:
            kg = sb("kg", [P, TPB, D], scope=r2)
            with ExitStack() as r3:
                vg = sb("vg", [P, 2, TPB, D], scope=r3)
            with ExitStack() as r4:
                ends = sb("ends", [1, 3, SET_TILES, LEAVES], scope=r4)
            with ExitStack() as r3:
                zt = sb("zt", [P, FS, D], scope=r3)
                yt = sb("yt", [P, FS, D], scope=r3)
                with ExitStack() as r4:
                    w1_all = sb("w1_all", [P, 2, LEAVES, W1W], scope=r4)
                    w2_all = sb("w2_all", [LEAF_W + 1, 2, LEAVES, D], scope=r4)
                    w1s = sb("w1s", [P, WS, W1W], scope=r4)
                    w2s = sb("w2s", [LEAF_W + 1, WS, D], scope=r4)
                    zT = sb("zT", [P, 2, DC, P], scope=r4)
                    hT = sb("hT", [LEAF_W + 1, 2, P], scope=r4)
                kTs = sb("kTs", [P, 2, DC, SEQ], scope=r3)
                qTs = sb("qTs", [P, 2, DC, P], scope=r3)
                pg = sb("pg", [P, 2, SEQ], scope=r3)
                pgT = sb("pgT", [P, 2, TPB, P], scope=r3)
                smax, nmax, rsum = (sb(n, [P, 2], scope=r3) for n in ("smax", "nmax", "rsum"))
                psum_exp = sb("psum_exp", [P, 4], scope=r3)

        with ExitStack() as r5:
            wc = sb("wc", [P, 2, DC, HID], scope=r5)
            wg = sb("wg", [P, 2, DC, HID], scope=r5)
            wp = sb("wp", [P, 2, HID // P, D], scope=r5)
            bcg = sb("bcg", [P, 2, 2 * HID // P], scope=r5)
            bp = sb("bp", [P, 2, D], scope=r5)
            xr = sb("xr", [P, 2, -(-SLOTS // P), D], scope=r5)
            xT = sb("xT", [P, 2, DC, 512], scope=r5)
            hb = sb("hb", [P, 2, 512], scope=r5)
            hg = sb("hg", [P, 2, 512], scope=r5)
        dead = kb["c"][:].rearrange("p b j h s -> p (b j h s)")
        yo = dead[:, 0:YS * D].rearrange("p (u d) -> p u d", u=YS)
        zT_of = {"b": zT, "d": dead[:, 4096:4096 + 2 * DC * P].rearrange("p (u c t) -> p u c t", u=2, c=DC)}
        yg = dead[:, YS * D:(YS + GS * TOPK) * D].rearrange("p (u k d) -> p u k d", u=GS, k=TOPK)
        st = zq[:].rearrange("p t d -> p (t d)").rearrange("p (a m w) -> p a m w", a=2, m=HID // P)

        psS = pb("psS", [P, 2, 2, 512])
        psT = pb("psT", [P, 2, 512])
        psO = pb("psO", [P, 512])
        psM = pb("psM", [P, 512])

        s_x0 = sem("x_batch0_loaded")
        s_ctx, s_x, s_w, s_mask = sem("ctx_loaded"), sem("x_loaded"), sem("weights_loaded"), sem("mask_loaded")
        s_ident, s_const, s_hs = sem("ident_ready"), sem("consts_ready"), sem("headsel_ready")
        s_poolc = sem("pool_chain")
        p_ctxT, p_ctxTc, p_k, p_kc, p_v, p_vc = (sem(n) for n in
            ("ctxT_done", "ctxT_copied", "k_done", "k_copied", "v_done", "v_copied"))
        s_kb = {L: sem(f"kb_ready_{L}") for L in "ac"}
        s_neg = sem("neg_ready")
        s_out = sem("out_stored")
        s_dve = sem("dve_chain")

        N_ = {}
        for L in "ac":
            for n in ("yT_done", "yT_copied", "q_done", "q_copied", "scores_done", "shifted", "exp_done",
                      "prT_done", "prT_copied", "pv_done", "o_ready", "oT_done", "oT_copied", "wo_done",
                      "y_ready", "x_biased", "x_updated", "chain"):
                N_[L, n] = sem(f"{L}_{n}")

        for L in "bd":
            for n in ("z_ready", "zT_done", "zT_copied", "node_done", "scores_used", "rank_done", "chain"):
                N_[L, n] = sem(f"{L}_{n}")
        for n in ("zT_done", "zT_copied", "w_copied", "h_done", "h_copied", "y_done", "y_copied"):
            N_["f", n] = sem(f"f_{n}")
        for n in ("tr_done", "tr_copied", "scores_done", "bias_ready", "exp_done", "pT_done", "pT_copied", "pv_done",
                  "x_updated", "chain"):
            N_["g", n] = sem(f"g_{n}")
        s_node, s_zeros, s_zfill, s_tables = sem("node_loaded"), sem("zeros_ready"), sem("zero_filled"), sem("tables_ready")
        for n in ("xT_done", "xT_copied", "hg_done", "h_ready", "gated", "silu_done", "o_done", "o_copied"):
            N_["e", n] = sem(f"e_{n}")
        s_ohs, s_xrank, s_gap, s_gexp, s_disp, s_half, s_fin = (sem(n) for n in (
            "onehots_ready", "slot_ranks_done", "gap_ready", "gap_exp_done", "dispatched", "first_added", "x_final"))
        s_wload = [sem(f"expert_loaded{q}") for q in range(2)]
        s_xload = [sem(f"slots_loaded{q}") for q in range(2)]
        s_ostore = [sem(f"o_stored{u}") for u in range(YS)]
        s_yload = [sem(f"outputs_gathered{u}") for u in range(GS)]
        s_rows, s_leaf = sem("rows_ready"), sem("leaf_table_ready")
        s_scat = [sem(f"scattered{s}") for s in range(3)]
        s_qgath, s_kgath, s_vgath = sem("queries_gathered"), sem("keys_gathered"), sem("values_gathered")
        s_leafw = [sem(f"leaf_weights_loaded{s}") for s in range(3)]
        s_zload = [sem(f"tiles_loaded{g}") for g in range(FS // GB)]
        s_ystore = [sem(f"y_stored{g}") for g in range(FS // GB)]

        def prep_sync(sp):
            sp.dma_start(ctx_sb[:], ctx_in.rearrange("b s d -> s b d")).then_inc(s_ctx, 16)
            for L in "ac":
                sp.dma_start(wk[L][:], xa[L]["wk"].rearrange("(c p) n -> p c n", p=P)).then_inc(s_w, 16)
                sp.dma_start(wv[L][:], xa[L]["wv"].rearrange("(c p) n -> p c n", p=P)).then_inc(s_w, 16)
                sp.dma_start(wq[L][:], xa[L]["wq"].rearrange("(c p) n -> p c n", p=P)).then_inc(s_w, 16)
            sp.dma_start(wo[:], xa["a"]["wo"].rearrange("(c p) n -> p c n", p=P)).then_inc(s_w, 16)

        def prep_loads_act(act):
            act.dma_start(x[:, 0:TPB, :], x_v[:, 0:TPB, :]).then_inc(s_x0, 16)
            for L in "ac":
                act.dma_start(bq[L][:], xa[L]["bq"]).then_inc(s_w, 16)
                act.dma_start(bk[L][:], xa[L]["bk"]).then_inc(s_w, 16)
                act.dma_start(bv_bc[L][:], xa[L]["bv"].partition_broadcast(CTX)).then_inc(s_w, 16)
            act.dma_start(bo_bc[:], xa["a"]["bo"].partition_broadcast(P)).then_inc(s_w, 16)
            act.dma_start(mask_sb[:], mask_in.rearrange("b s -> (b s)").partition_broadcast(P)).then_inc(s_mask, 16)
            act.dma_start(x[:, TPB:NT, :], x_v[:, TPB:NT, :]).then_inc(s_x, 16)

        N_W = 14

        def prep_pool(pool):
            ch = Link(pool, s_poolc)
            ch(nc.gpsimd.memset(ident[:], 0.0))
            nc.gpsimd.affine_select(out=ident[:], in_=ident[:], compare_op=ALU.not_equal, fill=1.0, base=0,
                                    pattern=[[-1, P]], channel_multiplier=1).then_inc(s_ident, 1)
            ch(nc.gpsimd.memset(headsel[:], 1.0 / DK ** 0.5))
            ch(nc.gpsimd.affine_select(out=headsel[:], in_=headsel[:], compare_op=ALU.is_ge, fill=0.0, base=0,
                                       pattern=[[-DK, HH]], channel_multiplier=1))
            nc.gpsimd.affine_select(out=headsel[:], in_=headsel[:], compare_op=ALU.is_ge, fill=0.0, base=DK - 1,
                                    pattern=[[DK, HH]], channel_multiplier=-1).then_inc(s_hs, 1)
            nc.gpsimd.memset(mean128[:], 1.0 / P).then_inc(s_const, 1)
            for L in "ac":
                nc.gpsimd.memset(vb[L][:, :, :, DK:VW], 1.0).then_inc(s_const, 1)
            consts_pool(pool, ch)
            pool.wait_ge(s_hs, 1)
            key_blocks(pool, nc.gpsimd, "c", 2 * DC)

        def key_blocks(eng, e, L, copied):
            eng.wait_ge(p_kc, copied)
            for b in range(B):
                for j in range(DC):
                    e.tensor_tensor(
                        out=kb[L][:, b, j],
                        in0=kT[L][:, j, b * CTX:(b + 1) * CTX].unsqueeze(1).broadcast_to([P, HH, CTX]),
                        in1=headsel[:].unsqueeze(2).broadcast_to([P, HH, CTX]),
                        op=ALU.mult).then_inc(s_kb[L], 1)

        def prep_pe(pe):
            pe.wait_ge(s_ident, 1)
            pe.wait_ge(s_ctx, 16)
            for b in range(B):
                for c in range(DC):
                    i = nc.tensor.transpose(psS[:, c, 0, b * CTX:(b + 1) * CTX], ctx_sb[:, b, c * P:(c + 1) * P],
                                            ident[0:CTX, 0:CTX])
                    if b == B - 1:
                        i.then_inc(p_ctxT, 1)
            pe.wait_ge(s_w, 16 * N_W)
            pe.wait_ge(p_ctxTc, DC)
            for n, (L, j) in enumerate((L, j) for L in "ac" for j in range(DC)):
                for c in range(DC):
                    i = nc.tensor.matmul(psS[:, n // 2, n % 2, 0:B * CTX], wk[L][:, c, j * P:(j + 1) * P],
                                         ctxT[:, c, :], start=(c == 0), stop=(c == DC - 1))
                i.then_inc(p_k, 1)
            for n, (L, b) in enumerate((L, b) for L in "ac" for b in range(B)):
                if n >= 2:
                    pe.wait_ge(p_vc, n - 1)
                for c in range(DC):
                    i = nc.tensor.matmul(psT[0:CTX, n % 2, 0:D], ctxT[:, c, b * CTX:(b + 1) * CTX],
                                         wv[L][:, c, :], start=(c == 0), stop=(c == DC - 1))
                i.then_inc(p_v, 1)

        def prep_act(act):
            for c in range(DC):
                act.wait_ge(p_ctxT, c + 1)
                nc.scalar.copy(ctxT[:, c, :], psS[:, c, 0, 0:B * CTX]).then_inc(p_ctxTc, 1)
            act.wait_ge(s_w, 16 * N_W)
            for n, (L, j) in enumerate((L, j) for L in "ac" for j in range(DC)):
                act.wait_ge(p_k, n + 1)
                nc.scalar.activation(kT[L][:, j, :], psS[:, n // 2, n % 2, 0:B * CTX], ACT.Identity,
                                     bias=bk[L][:, j:j + 1]).then_inc(p_kc, 1)

        def prep_dve(dve):
            dve.wait_ge(s_mask, 16)
            nc.vector.tensor_scalar(neg[:].rearrange("p b s -> p (b s)"), mask_sb[:], 0, NEG,
                                    ALU.is_gt, ALU.mult).then_inc(s_neg, 1)
            dve.wait_ge(s_w, 16 * N_W)
            for n, (L, b) in enumerate((L, b) for L in "ac" for b in range(B)):
                dve.wait_ge(p_v, n + 1)
                nc.vector.tensor_tensor(
                    out=vb[L][:, b, :, 0:DK],
                    in0=psT[0:CTX, n % 2, 0:D].rearrange("p (h d) -> p h d", h=HEADS),
                    in1=bv_bc[L][:].rearrange("p (h d) -> p h d", h=HEADS), op=ALU.add).then_inc(p_vc, 1)
            dve.wait_ge(s_hs, 1)
            key_blocks(dve, nc.vector, "a", DC)

        def bodies(eng, step, chain=None, per=0):
            for k in range(STEPS):
                step(0, k, True, False)
            done = chain.base + chain.n if chain else 0
            with eng.Fori(1, B - 1) as b:
                if chain:
                    chain.restart(b * per + (done - per))
                for k in range(STEPS):
                    step(b, k, False, False)
                assert not chain or chain.n == per
            if chain:
                chain.restart(done + (B - 2) * per)
            for k in range(STEPS + DRAIN):
                step(B - 1, k, False, True)

        def front_use(k):
            return {1: [(1, "y", 0)], 3: [(0, "y", 1), (1, "y", 2)], 5: [(0, "y", 3), (1, "q", 0)],
                    7: [(0, "q", 1)]}.get(k % 8, [])

        def front_pe(pe, L, b, g, kind, i):
            G = 2 * b + g
            if kind == "y":
                T = GT * G + i
                pe.wait_ge(N_[L, "y_ready"], T + 1)
                for c in range(DC):
                    m = nc.tensor.transpose(psM[:, c * P:(c + 1) * P], sa["y"][:, i % 2, c * P:(c + 1) * P], ident[:])
                m.then_inc(N_[L, "yT_done"], 1)
            else:
                pe.wait_ge(N_[L, "yT_copied"], GT * G + GT)
                for c in range(DC):
                    m = nc.tensor.matmul(psM[:], wq[L][:, c, i * P:(i + 1) * P], sa["yT"][:, c, :],
                                         start=(c == 0), stop=(c == DC - 1))
                m.then_inc(N_[L, "q_done"], 1)

        def front_act(act, L, b, g, kind, i):
            G = 2 * b + g
            if kind == "y":
                T = GT * G + i
                act.wait_ge(N_[L, "yT_done"], T + 1)
                nc.scalar.copy(sa["yT"][:, :, i * P:(i + 1) * P],
                               psM[:, 0:D].rearrange("p (c t) -> p c t", c=DC)).then_inc(N_[L, "yT_copied"], 1)
            else:
                act.wait_ge(N_[L, "q_done"], 2 * G + i + 1)
                nc.scalar.activation(sa["qT"][:, g % 2, i, :], psM[:], ACT.Identity,
                                     bias=bq[L][:, i:i + 1]).then_inc(N_[L, "q_copied"], 1)

        def xattn_pe(pe, L):
            def m_free(front_y, front_q, outs):
                if front_y is not None:
                    pe.wait_ge(N_[L, "yT_copied"], front_y)
                if front_q is not None:
                    pe.wait_ge(N_[L, "q_copied"], front_q)
                if outs is not None:
                    pe.wait_ge(N_[L, "x_updated"], outs)

            def step(b, k, first, last):
                n = STEPS * b + k
                drain = k >= STEPS
                if not drain:
                    g = k // 8
                    if k % 8 == 0:
                        pe.wait_ge(N_[L, "q_copied"], 2 * (2 * b + g) + 2)
                    if not (first and k < 2):
                        pe.wait_ge(N_[L, "shifted"], n - 1)
                    for q in range(2):
                        o = psS[:, k % 2, q, 0:HQ * CTX].rearrange("p (h s) -> p h s", h=HQ)
                        j = k % 2
                        lhs = sa["qT"][:, g, j, ((k // 2) % GT) * P:((k // 2) % GT + 1) * P]
                        m = nc.tensor.matmul(o, lhs, kb[L][:, b, j, q * HQ:(q + 1) * HQ, :],
                                             start=True, stop=(L == "a"))
                        if L == "c":
                            m = nc.tensor.matmul(o, mean128[:], neg[:, b, :].unsqueeze(1).broadcast_to([P, HQ, CTX]),
                                                 start=False, stop=True)
                    m.then_inc(N_[L, "scores_done"], 1)
                fronts = [] if (last and k >= 8) else front_use(k)

                def slot(s):
                    for sl, kind, i in fronts:
                        if sl == s:
                            G = 2 * b + k // 8 + 1
                            if kind == "y" and i > 0:
                                m_free(GT * G + i, None, None)
                            if kind == "q" and i == 1:
                                m_free(None, 2 * G + 1, None)
                            if L == "a" and not (first and k < 7):
                                m_free(None, None, TPB * b + (k - 1 - 6) // 2 + 1)
                            front_pe(pe, L, b, k // 8 + 1, kind, i)
                    if L == "a" and k % 2 == 0 and not (first and k < 6) :
                        T = TPB * b + (k - 6) // 2
                        if s == 0:
                            if not (last and k >= 10):
                                G = 2 * b + (k - 1) // 8 + 1
                                kk = (k - 1) % 8
                                if kk == 7:
                                    m_free(None, 2 * G + 2, None)
                                elif kk == 5:
                                    m_free(None, 2 * G + 1, None)
                                else:
                                    m_free(GT * G + (1 if kk == 1 else 3), None, None)
                            if not (first and k < 8):
                                m_free(None, None, T)
                            pe.wait_ge(N_[L, "o_ready"], 2 * T + 2)
                            for c in range(DC):
                                m = nc.tensor.transpose(psM[:, c * P:(c + 1) * P],
                                                        sa["o"][:, ((k - 6) // 2) % 2, c * P:(c + 1) * P], ident[:])
                            m.then_inc(N_[L, "oT_done"], 1)
                        else:
                            pe.wait_ge(N_[L, "oT_copied"], T + 1)
                            for c in range(DC):
                                m = nc.tensor.matmul(psM[:, 0:D], sa["oT"][:, c, :], wo[:, c, :],
                                                     start=(c == 0), stop=(c == DC - 1))
                            m.then_inc(N_[L, "wo_done"], 1)

                slot(0)
                if k - 1 < STEPS and not (first and k < 1):
                    pe.wait_ge(N_[L, "exp_done"], n)
                    for q in range(2):
                        if not (first and k < 2):
                            pe.wait_ge(N_[L, "prT_copied"], 2 * (n - 2) + q + 1)
                        for h in range(HQ):
                            m = nc.tensor.transpose(psT[0:CTX, q, h * P:(h + 1) * P],
                                                    sa["pr"][:, (k - 1) % 2, q * HQ + h, :], ident[:])
                        m.then_inc(N_[L, "prT_done"], 1)
                if k - 2 < STEPS and not (first and k < 2):
                    pe.wait_ge(N_[L, "prT_copied"], 2 * (n - 2) + 2)
                    if not (first and k < 3):
                        pe.wait_ge(N_[L, "o_ready"], n - 2)
                    bb = b if k >= 2 else b - 1
                    for h in range(HH):
                        m = nc.tensor.matmul(psO[:, h * VW:(h + 1) * VW], sa["prT"][:, k % 2, h, :],
                                             vb[L][:, bb, (k % 2) * HH + h, :], start=True, stop=True)
                    m.then_inc(N_[L, "pv_done"], 1)
                slot(1)

            if L == "a":
                pe.wait_ge(s_ident, 1)
            else:
                pe.wait_ge(N_["g", "tr_copied"], TPB + 2 * NT)
            for i in range(GT):
                if i:
                    m_free(i, None, None)
                front_pe(pe, L, 0, 0, "y", i)
            for i in range(DC):
                if i:
                    m_free(None, 1, None)
                front_pe(pe, L, 0, 0, "q", i)
            pe.wait_ge(s_kb[L], B * DC)
            pe.wait_ge(p_vc, 2 * B)
            pe.wait_ge(s_const, 3)
            pe.wait_ge(s_neg, 1)
            pe.wait_ge(N_[L, "q_copied"], DC)
            bodies(pe, step)

        def xattn_act(act, L):
            def step(b, k, first, last):
                n = STEPS * b + k
                if k - 1 < STEPS and not (first and k < 1):
                    act.wait_ge(N_[L, "shifted"], n)
                    pr = sa["pr"][:, (k - 1) % 2].rearrange("p h s -> p (h s)")
                    nc.scalar.activation(pr, pr, ACT.Exp).then_inc(N_[L, "exp_done"], 1)

                def slot(s):
                    for sl, kind, i in ([] if (last and k >= 8) else front_use(k)):
                        if sl == s:
                            front_act(act, L, b, k // 8 + 1, kind, i)
                    if s == 0 and L == "a" and k % 2 == 0 and not (first and k < 6):
                        T = TPB * b + (k - 6) // 2
                        act.wait_ge(N_[L, "oT_done"], T + 1)
                        nc.scalar.copy(sa["oT"][:], psM[:, 0:D].rearrange("p (c t) -> p c t", c=DC))\
                            .then_inc(N_[L, "oT_copied"], 1)
                slot(0)
                if k - 1 < STEPS and not (first and k < 1):
                    if not (first and k < 3):
                        act.wait_ge(N_[L, "pv_done"], n - 2)
                    for q in range(2):
                        act.wait_ge(N_[L, "prT_done"], 2 * (n - 1) + q + 1)
                        nc.scalar.copy(sa["prT"][:, (k - 1) % 2, q * HQ:(q + 1) * HQ, :],
                                       psT[0:CTX, q, :].rearrange("p (h t) -> p h t", h=HQ))\
                            .then_inc(N_[L, "prT_copied"], 1)
                slot(1)

            act.wait_ge(s_w, 16 * N_W)
            for i in range(GT):
                front_act(act, L, 0, 0, "y", i)
            for i in range(DC):
                front_act(act, L, 0, 0, "q", i)
            bodies(act, step)

        def tile_stats(ch, T, i):
            ch.count(nc.vector.bn_stats(stat[:, i, :], x[:, T, :]))

        def batch_rstd(ch):
            ch.wait()
            m_even, q_even, m_odd, q_odd = (stat[:, :, i] for i in (1, 2, 4, 5))
            v, t, r = nw[:, 0], nw[:, 1], rstd[:]
            ch.count(nc.vector.tensor_tensor(out=mean[:], in0=m_even, in1=m_odd, op=ALU.add))
            ch.count(nc.vector.tensor_tensor(out=t, in0=m_even, in1=m_odd, op=ALU.subtract))
            ch(nc.vector.tensor_tensor(out=v, in0=q_even, in1=q_odd, op=ALU.add))
            ch.count(nc.vector.tensor_scalar(mean[:], mean[:], 0.5, None, ALU.mult))
            ch(nc.vector.tensor_tensor(out=t, in0=t, in1=t, op=ALU.mult))
            ch(nc.vector.scalar_tensor_tensor(v, t, D / 4.0, v, ALU.mult, ALU.add))
            ch(nc.vector.tensor_scalar(v, v, 1.0 / D, EPS, ALU.mult, ALU.add))
            ch(nc.vector.tensor_scalar(r.bitcast(I32), v.bitcast(I32), -0.5, float(0x5F3759DF), ALU.mult, ALU.add))
            for _ in range(3):
                ch(nc.vector.tensor_tensor(out=t, in0=r, in1=r, op=ALU.mult))
                ch(nc.vector.scalar_tensor_tensor(t, t, -0.5, v, ALU.mult, ALU.mult))
                ch(nc.vector.scalar_tensor_tensor(r, t, 1.5, r, ALU.add, ALU.mult))
        LN_CHAIN = TPB + 8 + 9

        def normalise(dst, T, i):
            return nc.vector.tensor_scalar(dst, x[:, T, :], mean[:, i:i + 1], rstd[:, i:i + 1], ALU.subtract, ALU.mult)

        def xattn_dve(dve, L):
            ch = Link(dve, N_[L, "chain"])

            def norm_tile(b, g, i):
                T = GT * (2 * b + g) + i
                if not (isinstance(b, int) and b == 0 and g == 0 and i < 2):
                    dve.wait_ge(N_[L, "yT_done"], T - 1)
                normalise(sa["y"][:, i % 2, :], T, GT * (g % 2) + i).then_inc(N_[L, "y_ready"], 1)

            def step(b, k, first, last):
                n = STEPS * b + k
                if 3 <= k + (0 if first else 3) and k - 3 < STEPS:
                    par, tp, j = (k - 3) % 2, ((k - 3) // 2) % 2, (k - 3) % 2
                    dve.wait_ge(N_[L, "pv_done"], n - 2)
                    pv = psO[:, 0:HH * VW].rearrange("p (h d) -> p h d", h=HH)
                    ch(nc.vector.reciprocal(sa["rinv"][:, par, :], pv[:, :, DK]))
                    if j == 0 and not (first and k < 7):
                        dve.wait_ge(N_[L, "oT_done" if L == "a" else "x_updated"], TPB * b + (k - 3) // 2 - 1)
                    nc.vector.tensor_tensor(
                        out=sa["o"][:, tp, j * P:(j + 1) * P].rearrange("p (h d) -> p h d", h=HH),
                        in0=pv[:, :, 0:DK], in1=sa["rinv"][:, par, :].unsqueeze(2).broadcast_to([P, HH, DK]),
                        op=ALU.mult).then_inc(N_[L, "o_ready"], 1)
                if k < STEPS:
                    dve.wait_ge(N_[L, "scores_done"], n + 1)
                    s = psS[:, k % 2, :, 0:HQ * CTX].rearrange("p q (h s) -> p q h s", h=HQ)
                    mx = sa["mx"][:, k % 2, :].rearrange("p (q h) -> p q h", q=2)
                    ch(nc.vector.tensor_reduce(mx, s, AX.X, ALU.max))
                    if not (first and k < 2):
                        dve.wait_ge(N_[L, "prT_done"], 2 * (n - 2) + 2)
                    nc.vector.tensor_tensor(
                        out=sa["pr"][:, k % 2].rearrange("p (q h) s -> p q h s", q=2), in0=s,
                        in1=mx.unsqueeze(3).broadcast_to([P, 2, HQ, CTX]), op=ALU.subtract)\
                        .then_inc(N_[L, "shifted"], 1)
                if L == "a" and k % 2 == 1 and not (first and k < 7):
                    T = TPB * b + (k - 7) // 2
                    dve.wait_ge(N_[L, "wo_done"], T + 1)
                    dve.wait_ge(N_[L, "x_biased"], T + 1)
                    nc.vector.tensor_tensor(out=x[:, T, :], in0=psM[:, 0:D], in1=x[:, T, :], op=ALU.add)\
                        .then_inc(N_[L, "x_updated"], 1)
                if k < TPB and not last:
                    if L == "a" and k == 0:
                        dve.wait_ge(s_x, 16)
                    tile_stats(ch, TPB * (b + 1) + k, k)
                if k == TPB - 1 and not last:
                    batch_rstd(ch)
                if k % 8 < GT and not (last and k >= 8):
                    norm_tile(b, k // 8 + 1, k % 8)

            if L == "a":
                dve.wait_ge(s_x0, 16)
            else:
                dve.wait_ge(N_["g", "x_updated"], NT)
            for T in range(TPB):
                tile_stats(ch, T, T)
            batch_rstd(ch)
            for i in range(GT):
                norm_tile(0, 0, i)
            bodies(dve, step, ch, per=2 * STEPS + LN_CHAIN)

        def xattn_pool(pool, L):
            if L == "a":
                with pool.Fori(0, NT) as T:
                    pool.wait_ge(N_["a", "y_ready"], T + 1)
                    nc.gpsimd.tensor_tensor(out=x[:, T, :], in0=x[:, T, :], in1=bo_bc[:], op=ALU.add)\
                        .then_inc(N_["a", "x_biased"], 1)
            else:
                with pool.Fori(0, NT // 2) as t2:
                    for u in range(2):
                        pool.wait_ge(N_["c", "o_ready"], 4 * t2 + 2 * u + 2)
                        nc.gpsimd.tensor_tensor(out=x[:, 2 * t2 + u, :], in0=x[:, 2 * t2 + u, :],
                                                in1=sa["o"][:, u, :], op=ALU.add).then_inc(N_["c", "x_updated"], 1)

        def route_sync(sp):
            sp.dma_start(nodew[:], ffn["node_w"].rearrange("(c p) n -> p c n", p=P)).then_inc(s_node, 16)
            sp.dma_start(nodeb[:], ffn["node_b"].partition_broadcast(P)).then_inc(s_node, 16)
            sp.dma_start(routerw[:], moe["router_w"].rearrange("(c p) n -> p c n", p=P)).then_inc(s_node, 16)
            sp.dma_start(routerb[:], moe["router_b"].partition_broadcast(P)).then_inc(s_node, 16)
            sp.wait_ge(s_zeros, 1)
            rows = zq[:, 0:ZR, :]
            n = P * ZR
            for buf in (*sorted_in, slots_in[0:SLOT_FILL, :]):
                for i in range(buf.shape[0] // n):
                    sp.dma_start(buf[i * n:(i + 1) * n, :].rearrange("(p r) d -> p r d", p=P), rows)\
                        .then_inc(s_zfill, 16)
        N_ZFILL = 16 * (3 * SET_ROWS + SLOT_FILL) // (P * ZR)

        def consts_pool(pool, ch):
            nc.gpsimd.memset(zq[:, 0:ZR, :], 0.0).then_inc(s_zeros, 1)
            ch(nc.gpsimd.memset(tri[:], 1.0))
            ch(nc.gpsimd.affine_select(out=tri[:], in_=tri[:], compare_op=ALU.is_ge, fill=0.0, base=0,
                                       pattern=[[1, P]], channel_multiplier=-1))
            ch(nc.gpsimd.memset(ones_bf[:], 1.0))
            ch(nc.gpsimd.memset(before[:, 0, :], 0.0))
            ch(nc.gpsimd.memset(ones_row[:], 1.0))
            for s in range(3):
                ch(nc.gpsimd.memset(set_leaf0[:, s, :], float(s % 2 * LEAVES)))
            ch(nc.gpsimd.iota(tile_row[:], pattern=[[P, SET_TILES]], base=0, channel_multiplier=0,
                              allow_small_or_imprecise_dtypes=True))
            ch(nc.gpsimd.iota(batch0[:], pattern=[[CAP, B]], base=0, channel_multiplier=0,
                              allow_small_or_imprecise_dtypes=True))
            ch(nc.gpsimd.iota(expert_id[:], pattern=[[1, EXPERTS]], base=0, channel_multiplier=0,
                              allow_small_or_imprecise_dtypes=True))
            nc.gpsimd.iota(trash[:], pattern=[[P * B, TOPK * TPB], [P, B]], base=ROW_TRASH, channel_multiplier=1,
                           allow_small_or_imprecise_dtypes=True).then_inc(s_tables, 1)

        def transposed_z(pe, L, T, k):
            for c in range(DC):
                m = nc.tensor.transpose(psT[:, k % 2, c * P:(c + 1) * P], zq[:, T, c * P:(c + 1) * P], ident[:])
            m.then_inc(N_[L, "zT_done"], 1)

        def route_pe(pe, L, w, width, wait_w):
            wait_w(pe)

            def scores(b, k, first):
                T = TPB * b + k
                pe.wait_ge(N_[L, "zT_copied"], T + 1)
                if k == 0 and not first:
                    pe.wait_ge(N_[L, "scores_used"], b)
                for c in range(DC):
                    m = nc.tensor.matmul(psO[:, k * width:(k + 1) * width], zT_of[L][:, k % 2, c, :], w[:, c, :],
                                         start=(c == 0), stop=(c == DC - 1))
                m.then_inc(N_[L, "node_done"], 1)

            def body(b, first):
                for k in range(TPB):
                    T = TPB * b + k
                    pe.wait_ge(N_[L, "z_ready"], T + 1)
                    if not (first and k < 2):
                        pe.wait_ge(N_[L, "zT_copied"], T - 1)
                    transposed_z(pe, L, T, k)
                    if k:
                        scores(b, k - 1, first)
                scores(b, TPB - 1, first)
            for b in range(B):
                body(b, b == 0)

        def route_act(act, L):
            def body(b, first):
                for k in range(TPB):
                    T = TPB * b + k
                    act.wait_ge(N_[L, "zT_done"], T + 1)
                    if not (first and k < 2):
                        act.wait_ge(N_[L, "node_done"], T - 1)
                    nc.scalar.copy(zT_of[L][:, k % 2], psT[:, k % 2, 0:D].rearrange("p (c t) -> p c t", c=DC))\
                        .then_inc(N_[L, "zT_copied"], 1)
            body(0, True)
            with act.Fori(1, B) as b:
                body(b, False)

        def route_norm(dve, ch, L, b):
            for k in range(TPB):
                tile_stats(ch, TPB * b + k, k)
            batch_rstd(ch)
            for k in range(TPB):
                normalise(zq[:, TPB * b + k, :], TPB * b + k, k).then_inc(N_[L, "z_ready"], 1)

        TREE_CHAIN = LN_CHAIN + 1 + 2 + 2 * (DEPTH - 1) + TPB - 1

        def tree_dve(dve):
            ch = Link(dve, N_["b", "chain"])
            dve.wait_ge(s_node, 64)
            dve.wait_ge(s_zfill, N_ZFILL)
            dve.wait_ge(N_["a", "x_updated"], NT)
            dve.wait_ge(s_tables, 1)
            ch(nc.vector.tensor_scalar(nodeb[:], nodeb[:], -1.0, None, ALU.mult))

            def body(b, first):
                route_norm(dve, ch, "b", b)
                dve.wait_ge(N_["b", "node_done"], TPB * (b + 1))
                ch(nc.vector.tensor_tensor(
                    out=bits[:].rearrange("p (t n) -> p t n", t=TPB),
                    in0=psO[:, 0:TPB * NODES3].rearrange("p (t n) -> p t n", t=TPB),
                    in1=nodeb[:].unsqueeze(1).broadcast_to([P, TPB, NODES3]), op=ALU.is_ge))
                bv = bits[:].rearrange("p (m n) -> p m n", n=NODES)
                p1 = path[0][:]
                ch.count(nc.vector.tensor_scalar(p1[:, :, 0], bv[:, :, 0], -1.0, 1.0, ALU.mult, ALU.add))
                ch(nc.vector.tensor_scalar(p1[:, :, 1], bv[:, :, 0], 1.0, None, ALU.mult))
                for l in range(1, DEPTH):
                    w = 2 ** l
                    src = path[l - 1][:]
                    if l < DEPTH - 1:
                        dst = path[l][:].rearrange("p m (w two) -> p m w two", two=2)
                    else:
                        dst = onehot[:, bass.ds(b * TPB, TPB), :].rearrange("p t (m w two) -> p (t m) w two", m=3, two=2)
                    ch(nc.vector.tensor_tensor(out=dst[:, :, :, 1], in0=src, in1=bv[:, :, w - 1:2 * w - 1], op=ALU.mult))
                    ch(nc.vector.tensor_tensor(out=dst[:, :, :, 0], in0=src, in1=dst[:, :, :, 1], op=ALU.subtract))
                if not first:
                    dve.wait_ge(N_["b", "scores_used"], b)
                for k in range(TPB):
                    T = TPB * b + k
                    i = nc.vector.tensor_tensor(out=before[:, T + 1, :], in0=before[:, T, :], in1=onehot[:, T, :], op=ALU.add)
                    if k < TPB - 1:
                        ch(i)
                    else:
                        i.then_inc(N_["b", "scores_used"], 1)

            ch.restart(1)
            body(0, True)
            with dve.Fori(1, B) as b:
                ch.restart(b * TREE_CHAIN + 1)
                body(b, False)
                assert ch.n == TREE_CHAIN, ch.n
            ch.restart(B * TREE_CHAIN + 1)
            dve.wait_ge(N_["b", "rank_done"], 1)
            ch(nc.vector.tensor_scalar(cnt_i[:], psO[:, 0:LEAVES3], float(P - 1), None, ALU.add))
            ch(nc.vector.tensor_scalar(cnt_i[:], cnt_i[:], 7, 7, ALU.arith_shift_right, ALU.logical_shift_left))
            ch(nc.vector.tensor_copy(padded[:], cnt_i[:]))
            for s in range(3):
                r = slice(s * LEAVES, (s + 1) * LEAVES)
                ch(nc.vector.tensor_tensor_scan(incl[:, r], ones_row[:, 0:LEAVES], padded[:, r], 0.0, ALU.mult, ALU.add))
            ch(nc.vector.tensor_tensor(out=base[:], in0=incl[:], in1=padded[:], op=ALU.subtract))
            ch(nc.vector.tensor_scalar(base[:], base[:], -1.0, None, ALU.add))
            for b in range(B):
                dve.wait_ge(N_["b", "rank_done"], 2 + b)
                r = psS[:, b // 2, b % 2, 0:TPB * LEAVES3].rearrange("p (t m) -> p t m", t=TPB)
                ch(nc.vector.tensor_tensor(out=rowt[:], in0=r, in1=base[:].unsqueeze(1).broadcast_to([P, TPB, LEAVES3]),
                                           op=ALU.add))
                ch(nc.vector.tensor_tensor(out=rowt[:], in0=rowt[:], in1=onehot[:, b * TPB:(b + 1) * TPB, :], op=ALU.mult))
                ch(nc.vector.tensor_reduce(rowf[:], rowt[:].rearrange("p t (s l) -> p s t l", s=3), AX.X, ALU.add))
                nc.vector.tensor_copy(row_i[:, :, b * TPB:(b + 1) * TPB], rowf[:]).then_inc(s_rows, 1)
            ch(nc.vector.tensor_tensor(
                out=ends[:], in0=incl[0:1].rearrange("p (s l) -> p s l", s=3).unsqueeze(2).broadcast_to([1, 3, SET_TILES, LEAVES]),
                in1=tile_row[:].unsqueeze(1).unsqueeze(3).broadcast_to([1, 3, SET_TILES, LEAVES]), op=ALU.is_le))
            ch(nc.vector.tensor_reduce(leaff[:], ends[:], AX.X, ALU.add))
            ch(nc.vector.tensor_scalar(leaff[:], leaff[:], float(LEAVES - 1), None, ALU.min))
            nc.vector.tensor_tensor(out=leaf_i[:].rearrange("p (s t) -> p s t", s=3), in0=leaff[:],
                                    in1=set_leaf0[:], op=ALU.add).then_inc(s_leaf, 1)

        def rank_pe(pe):
            pe.wait_ge(N_["b", "scores_used"], B)
            nc.tensor.matmul(psO[:, 0:LEAVES3], ones_bf[:], before[:, NT, :], start=True, stop=True)\
                .then_inc(N_["b", "rank_done"], 1)
            for b in range(B):
                o = psS[:, b // 2, b % 2, 0:TPB * LEAVES3]
                r = slice(b * TPB, (b + 1) * TPB)
                nc.tensor.matmul(o, tri[:], onehot[:, r, :].rearrange("p t m -> p (t m)"), start=True, stop=False)
                nc.tensor.matmul(o, ones_bf[:], before[:, r, :].rearrange("p t m -> p (t m)"), start=False, stop=True)\
                    .then_inc(N_["b", "rank_done"], 1)

        def scatter_pool(pool):
            pool.wait_ge(s_zfill, N_ZFILL)
            pool.wait_ge(N_["b", "z_ready"], NT)
            pool.wait_ge(s_rows, B)
            for s in range(3):
                for T in range(NT):
                    nc.gpsimd.indirect_dma_start(
                        out=sorted_in[s][:, :], out_offset=bass.IndirectOffsetOnAxis(ap=row_i[:, s, T:T + 1], axis=0),
                        in_=zq[:, T, :], in_offset=None).then_inc(s_scat[s], 16)

        def gather(pool, dst, s, T, done):
            nc.gpsimd.indirect_dma_start(
                out=dst, out_offset=None, in_=sorted_out[s][:, :],
                in_offset=bass.IndirectOffsetOnAxis(ap=row_i[:, s, T:T + 1], axis=0)).then_inc(done, 16)

        def gather_pool(pool):
            for s in range(3):
                pool.wait_ge(s_scat[s], 16 * NT)

            def rows_stored(s):
                for g in range(FS // GB):
                    pool.wait_ge(s_ystore[g], 16 * IT_SET * (s + 1))

            def query(b, k):
                gather(pool, zq[:, k, :], 0, b * TPB + k, s_qgath)

            def key(b, k):
                gather(pool, kg[:, k, :], 1, b * TPB + k, s_kgath)

            def values(b):
                for k in range(TPB):
                    gather(pool, vg[:, b % 2, k, :], 2, b * TPB + k, s_vgath)

            rows_stored(0)
            for k in range(TPB):
                query(0, k)
            rows_stored(1)
            for k in range(TPB):
                key(0, k)
            rows_stored(2)
            pool.wait_ge(N_["f", "y_done"], 3 * SET_TILES)
            values(0)
            for k in range(TPB):
                pool.wait_ge(N_["g", "tr_done"], k + 1)
                key(1, k)
            pool.wait_ge(s_vgath, 16 * TPB)
            values(1)
            for b in range(B - 1):
                for k in range(TPB):
                    pool.wait_ge(N_["g", "tr_done"], TPB + 1 + 2 * (TPB * b + k) + 1)
                    if b + 2 < B:
                        key(b + 2, k)
                    query(b + 1, k)
                if b + 2 < B:
                    pool.wait_ge(N_["g", "pv_done"], TPB * (b + 1))
                    pool.wait_ge(s_vgath, 16 * TPB * (b + 2))
                    values(b + 2)

        def leaf_weights_sync(sp, s):
            r = slice(s * LEAVES, (s + 1) * LEAVES)
            sp.dma_start(w1_all[:, s % 2], ffn["w1b"][r].rearrange("l p n -> p l n")).then_inc(s_leafw[s], 16)
            sp.dma_start(w2_all[:, s % 2], ffn["w2b"][r].rearrange("l p n -> p l n")).then_inc(s_leafw[s], 16)

        def ffn_sync(sp):
            def rows(buf, it, g):
                return buf[bass.ds((it * FS + g * GB) * P, GB * P), :].rearrange("(u p) d -> p u d", p=P)

            def load(s, it, g):
                sp.dma_start(zt[:, g * GB:(g + 1) * GB, :], rows(sorted_in[s], it, g)).then_inc(s_zload[g], 16)

            def store(s, it, g):
                sp.wait_ge(N_["f", "y_copied"], s * SET_TILES + (it * FS + (g + 1) * GB))
                sp.dma_start(rows(sorted_out[s], it, g), yt[:, g * GB:(g + 1) * GB, :]).then_inc(s_ystore[g], 16)

            sp.wait_ge(N_["a", "x_updated"], NT)
            leaf_weights_sync(sp, 0)
            leaf_weights_sync(sp, 1)
            sp.wait_ge(s_leaf, 1)
            for s in range(3):
                sp.wait_ge(s_leafw[s], 32)
                sp.wait_ge(s_scat[s], 16 * NT)
                for g in range(FS // GB):
                    if s:
                        sp.wait_ge(N_["f", "zT_done"], s * SET_TILES - FS + (g + 1) * GB)
                    load(s, 0, g)
                    if s:
                        store(s - 1, IT_SET - 1, g)
                if s == 1:
                    leaf_weights_sync(sp, 2)
                with sp.Fori(1, IT_SET) as it:
                    for g in range(FS // GB):
                        sp.wait_ge(N_["f", "zT_done"], it * FS + (s * SET_TILES - FS + (g + 1) * GB))
                        load(s, it, g)
                        store(s, it - 1, g)
            for g in range(FS // GB):
                store(2, IT_SET - 1, g)

        def ffn_turns(eng, step):
            for it in range(2):
                for u in range(FS):
                    step(it, u, it == 0, False)
            with eng.Fori(2, 3 * IT_SET - 1) as it:
                for u in range(FS):
                    step(it, u, False, False)
            for u in range(FS + 2):
                step(3 * IT_SET - 1, u, False, True)

        def ffn_pe(pe):
            def step(it, u, first, last):
                i = it * FS + u
                if u < FS:
                    if u % GB == 0:
                        pe.wait_ge(s_zload[u // GB], 16 * (it + 1))
                    if not (first and u < 2):
                        pe.wait_ge(N_["f", "zT_copied"], i - 1)
                    for c in range(DC):
                        m = nc.tensor.transpose(psT[:, u % 2, c * P:(c + 1) * P], zt[:, u, c * P:(c + 1) * P], ident[:])
                    m.then_inc(N_["f", "zT_done"], 1)
                if u - 1 < FS and not (first and u < 1):
                    v = (u - 1) % WS
                    pe.wait_ge(N_["f", "w_copied"], i)
                    if not (first and u < 3):
                        pe.wait_ge(N_["f", "h_copied"], i - 2)
                    for c in range(DC):
                        m = nc.tensor.matmul(psS[0:LEAF_W, 0, (u - 1) % 2, 0:P], w1s[:, v, c * LEAF_W:(c + 1) * LEAF_W],
                                             zT[:, (u - 1) % 2, c, :], start=(c == 0), stop=(c == DC - 1))
                    m.then_inc(N_["f", "h_done"], 1)
                if u - 2 < FS and not (first and u < 2):
                    v = (u - 2) % WS
                    pe.wait_ge(N_["f", "h_copied"], i - 1)
                    if not (first and u < 4):
                        pe.wait_ge(N_["f", "y_copied"], i - 3)
                    nc.tensor.matmul(psS[:, 1, u % 2, 0:D], hT[:, u % 2, :], w2s[:, v, :], start=True, stop=True)\
                        .then_inc(N_["f", "y_done"], 1)
            ffn_turns(pe, step)

        def ffn_act(act):
            def step(it, u, first, last):
                i = it * FS + u
                if u < FS:
                    act.wait_ge(N_["f", "zT_done"], i + 1)
                    if not (first and u < 2):
                        act.wait_ge(N_["f", "h_done"], i - 1)
                    nc.scalar.copy(zT[:, u % 2], psT[:, u % 2, 0:D].rearrange("p (c t) -> p c t", c=DC))\
                        .then_inc(N_["f", "zT_copied"], 1)
                    if not (first and u < WS):
                        act.wait_ge(N_["f", "y_done"], i - WS + 1)
                    r = act.value_load(leaf_i[0:1, bass.ds(i, 1)], min_val=0, max_val=2 * LEAVES - 1)
                    nc.scalar.copy(w1s[:, u % WS, :], w1_of[:, bass.ds(r, 1), :].rearrange("p o n -> p (o n)"))
                    nc.scalar.copy(w2s[:, u % WS, :], w2_of[:, bass.ds(r, 1), :].rearrange("p o n -> p (o n)"))\
                        .then_inc(N_["f", "w_copied"], 1)
            w1_of = w1_all[:].rearrange("p s l n -> p (s l) n")
            w2_of = w2_all[:].rearrange("p s l n -> p (s l) n")
            act.wait_ge(s_leaf, 1)
            ffn_turns(act, step)

        def ffn_dve(dve):
            def step(it, u, first, last):
                i = it * FS + u
                if u - 1 < FS and not (first and u < 1):
                    v = (u - 1) % WS
                    dve.wait_ge(N_["f", "h_done"], i)
                    if not (first and u < 3):
                        dve.wait_ge(N_["f", "y_done"], i - 2)
                    nc.vector.tensor_scalar(hT[0:LEAF_W, (u - 1) % 2, :], psS[0:LEAF_W, 0, (u - 1) % 2, 0:P],
                                            w1s[0:LEAF_W, v, DC * LEAF_W:DC * LEAF_W + 1], 0.0, ALU.add, ALU.max)\
                        .then_inc(N_["f", "h_copied"], 1)
                if u - 2 < FS and not (first and u < 2):
                    v = (u - 2) % FS
                    dve.wait_ge(N_["f", "y_done"], i - 1)
                    n = it if u >= 2 else it - 1
                    if not (isinstance(n, int) and n == 0):
                        dve.wait_ge(s_ystore[v // GB], 16 * n)
                    nc.vector.tensor_copy(yt[:, v, :], psS[:, 1, u % 2, 0:D]).then_inc(N_["f", "y_copied"], 1)
            nc.vector.memset(hT[LEAF_W:LEAF_W + 1, :, :], 1.0)
            ffn_turns(dve, step)

        def sa_bodies(eng, step, chain=None, per=0):
            for k in range(TPB):
                step(0, k, True, False)
            done = chain.base + chain.n if chain else 0
            with eng.Fori(1, B - 1) as b:
                if chain:
                    chain.restart(b * per + (done - per))
                for k in range(TPB):
                    step(b, k, False, False)
                assert not chain or chain.n == per
            if chain:
                chain.restart(done + (B - 2) * per)
            for k in range(TPB + 2):
                step(B - 1, k, False, True)

        def sa_pe(pe):
            def transpose_tile(src, count_free):
                if count_free is not None:
                    pe.wait_ge(N_["g", "tr_copied"], count_free)
                for c in range(DC):
                    m = nc.tensor.transpose(psM[:, c * P:(c + 1) * P], src[:, c * P:(c + 1) * P], ident[:])
                m.then_inc(N_["g", "tr_done"], 1)

            def step(b, k, first, last):
                n = TPB * b + k
                if k < TPB:
                    pe.wait_ge(N_["g", "tr_copied"], 2 * n + TPB + 1)
                    if not (first and k < 2):
                        pe.wait_ge(N_["g", "exp_done"], n - 1)
                    for h in range(2):
                        for c in range(DC):
                            m = nc.tensor.matmul(psS[:, k % 2, h, :], qTs[:, k % 2, c, :],
                                                 kTs[:, b % 2, c, h * 512:(h + 1) * 512],
                                                 start=(c == 0), stop=(c == DC - 1))
                    m.then_inc(N_["g", "scores_done"], 1)
                    if k == 0 and not last:
                        pe.wait_ge(s_kgath, 16 * TPB * (b + 2))
                    transpose_tile(kg[:, k, :], 2 * n + TPB + 1)
                    if not (last and k == TPB - 1):
                        if k == TPB - 1:
                            pe.wait_ge(s_qgath, 16 * TPB * (b + 2))
                        transpose_tile(zq[:, (k + 1) % TPB, :], 2 * n + TPB + 2)
                if k - 1 < TPB and not (first and k < 1):
                    pe.wait_ge(N_["g", "exp_done"], n)
                    for h in range(2):
                        if not (first and k < 2):
                            pe.wait_ge(N_["g", "pT_copied"], 2 * (n - 2) + h + 1)
                        for q in range(4):
                            m = nc.tensor.transpose(psT[:, h, q * P:(q + 1) * P],
                                                    pg[:, (k - 1) % 2, (4 * h + q) * P:(4 * h + q + 1) * P], ident[:])
                        m.then_inc(N_["g", "pT_done"], 1)
                if k - 2 < TPB and not (first and k < 2):
                    pe.wait_ge(N_["g", "pT_copied"], 2 * (n - 2) + 2)
                    if not (first and k < 3):
                        pe.wait_ge(N_["g", "x_updated"], n - 2)
                    bb = b if k >= 2 else b - 1
                    if k == 2:
                        pe.wait_ge(s_vgath, 16 * TPB * (b + 1))
                    for q in range(8):
                        m = nc.tensor.matmul(psO[:, 0:D], pgT[:, k % 2, q, :], vg[:, bb % 2, q, :],
                                             start=(q == 0), stop=(q == 7))
                    m.then_inc(N_["g", "pv_done"], 1)

            pe.wait_ge(s_kgath, 16 * TPB)
            pe.wait_ge(s_qgath, 16 * TPB)
            for k in range(TPB):
                transpose_tile(kg[:, k, :], k if k else None)
            transpose_tile(zq[:, 0, :], TPB)
            sa_bodies(pe, step)

        def sa_act(act):
            def copy_key(b, k, n):
                act.wait_ge(N_["g", "tr_done"], n)
                nc.scalar.copy(kTs[:, b % 2, :, k * P:(k + 1) * P],
                               psM[:, 0:D].rearrange("p (c t) -> p c t", c=DC)).then_inc(N_["g", "tr_copied"], 1)

            def copy_query(par, n):
                act.wait_ge(N_["g", "tr_done"], n)
                nc.scalar.copy(qTs[:, par], psM[:, 0:D].rearrange("p (c t) -> p c t", c=DC))\
                    .then_inc(N_["g", "tr_copied"], 1)

            def step(b, k, first, last):
                n = TPB * b + k
                if k - 1 < TPB and not (first and k < 1):
                    act.wait_ge(N_["g", "bias_ready"], n)
                    if not (first and k < 3):
                        act.wait_ge(N_["g", "pT_done"], 2 * (n - 3) + 2)
                    nc.scalar.activation(pg[:, (k - 1) % 2, :], psS[:, (k - 1) % 2].rearrange("p h s -> p (h s)"),
                                         ACT.Exp, bias=nmax[:, (k - 1) % 2:(k - 1) % 2 + 1], scale=SA_SCALE,
                                         accum_out=psum_exp[:, (k - 1) % 4:(k - 1) % 4 + 1])\
                        .then_inc(N_["g", "exp_done"], 1)
                if k < TPB:
                    copy_key(b + 1, k, 2 * n + TPB + 2)
                    if not (last and k == TPB - 1):
                        copy_query((k + 1) % 2, 2 * n + TPB + 3)
                if k - 1 < TPB and not (first and k < 1):
                    if not (first and k < 3):
                        act.wait_ge(N_["g", "pv_done"], n - 2)
                    for h in range(2):
                        act.wait_ge(N_["g", "pT_done"], 2 * (n - 1) + h + 1)
                        nc.scalar.copy(pgT[:, (k - 1) % 2, 4 * h:4 * h + 4, :],
                                       psT[:, h, :].rearrange("p (q t) -> p q t", q=4)).then_inc(N_["g", "pT_copied"], 1)

            for k in range(TPB):
                copy_key(0, k, k + 1)
            copy_query(0, TPB + 1)
            sa_bodies(act, step)

        def sa_dve(dve):
            ch = Link(dve, N_["g", "chain"])

            def step(b, k, first, last):
                n = TPB * b + k
                if k < TPB:
                    dve.wait_ge(N_["g", "scores_done"], n + 1)
                    par = k % 2
                    ch(nc.vector.tensor_reduce(smax[:, par:par + 1], psS[:, par].rearrange("p h s -> p (h s)"),
                                               AX.X, ALU.max))
                    if not (first and k < 2):
                        dve.wait_ge(N_["g", "exp_done"], n - 1)
                    nc.vector.tensor_scalar(nmax[:, par:par + 1], smax[:, par:par + 1], -SA_SCALE, None, ALU.mult)\
                        .then_inc(N_["g", "bias_ready"], 1)
                if k - 2 < TPB and not (first and k < 2):
                    T = TPB * b + k - 2
                    dve.wait_ge(N_["g", "pv_done"], n - 1)
                    ch(nc.vector.reciprocal(rsum[:, k % 2:k % 2 + 1], psum_exp[:, (k - 2) % 4:(k - 2) % 4 + 1]))
                    nc.vector.scalar_tensor_tensor(x[:, T, :], psO[:, 0:D], rsum[:, k % 2:k % 2 + 1], x[:, T, :],
                                                   ALU.mult, ALU.add).then_inc(N_["g", "x_updated"], 1)
            sa_bodies(dve, step, ch, per=2 * TPB)

        def topk_pe(pe):
            pe.wait_ge(s_ohs, 1)
            nc.tensor.matmul(psS[:, 0, 0, :], tri[:], ohs[:].rearrange("p q b e -> p (q b e)"), start=True, stop=False)
            nc.tensor.matmul(psS[:, 0, 0, :], ones_bf[:], ohb[:].rearrange("p q b e -> p (q b e)"), start=False, stop=True)\
                .then_inc(s_xrank, 1)

        def topk_act(act):
            act.wait_ge(s_gap, 1)
            nc.scalar.activation(prob[:, 1, :], prob[:, 1, :], ACT.Exp).then_inc(s_gexp, 1)

        def topk_dve(dve):
            ch = Link(dve, N_["d", "chain"])
            dve.wait_ge(N_["c", "x_updated"], NT)
            dve.wait_ge(s_node, 16 * 4)

            def body(b):
                route_norm(dve, ch, "d", b)
                dve.wait_ge(N_["d", "node_done"], TPB * (b + 1))
                nc.vector.tensor_tensor(
                    out=logit[:, bass.ds(b * TPB, TPB), :],
                    in0=psO[:, 0:TPB * EXPERTS].rearrange("p (t e) -> p t e", t=TPB),
                    in1=routerb[:].unsqueeze(1).broadcast_to([P, TPB, EXPERTS]), op=ALU.add)\
                    .then_inc(N_["d", "scores_used"], 1)

            with dve.Fori(0, B) as b:
                ch.restart(b * LN_CHAIN)
                body(b)
                assert ch.n == LN_CHAIN
            ch.restart(B * LN_CHAIN)
            dve.wait_ge(N_["d", "scores_used"], B)
            for T in range(NT):
                ch.count(nc.vector.max(best[:, T, :], logit[:, T, :]))
            ch.wait()
            for T in range(NT):
                ch.count(nc.vector.max_index(best_i[:, T, :], best[:, T, :], logit[:, T, :]))
            nc.vector.tensor_tensor(out=prob[:, 1, :], in0=best[:, :, 1], in1=best[:, :, 0], op=ALU.subtract)\
                .then_inc(s_gap, 1)
            ch.wait()
            ch(nc.vector.tensor_copy(choice[:], best_i[:, :, 0:TOPK]))
            for k in range(TOPK):
                ch.count(nc.vector.tensor_tensor(
                    out=ohs[:, k * TPB:(k + 1) * TPB],
                    in0=choice[:, :, k].rearrange("p (b t) -> p t b", b=B).unsqueeze(3).broadcast_to([P, TPB, B, EXPERTS]),
                    in1=expert_id[:].unsqueeze(1).unsqueeze(1).broadcast_to([P, TPB, B, EXPERTS]), op=ALU.is_equal))
            ch(nc.vector.memset(ohb[:, 0], 0.0))
            for q in range(TOPK * TPB - 1):
                i = nc.vector.tensor_tensor(out=ohb[:, q + 1], in0=ohb[:, q], in1=ohs[:, q], op=ALU.add)
                if q < TOPK * TPB - 2:
                    ch(i)
                else:
                    i.then_inc(s_ohs, 1)
            dve.wait_ge(s_gexp, 1)
            ch(nc.vector.tensor_scalar(prob[:, 0, :], prob[:, 1, :], 1.0, None, ALU.add))
            ch(nc.vector.reciprocal(prob[:, 0, :], prob[:, 0, :]))
            ch(nc.vector.tensor_tensor(out=prob[:, 1, :], in0=prob[:, 1, :], in1=prob[:, 0, :], op=ALU.mult))
            for k in range(TOPK):
                ch.count(nc.vector.tensor_scalar(xrow[:, k * TPB:(k + 1) * TPB],
                                                 choice[:, :, k].rearrange("p (b t) -> p t b", b=B),
                                                 float(SLOTS), -1.0, ALU.mult, ALU.add))
            ch.wait()
            ch(nc.vector.tensor_tensor(out=xrow[:], in0=xrow[:], in1=batch0[:].unsqueeze(1).broadcast_to([P, TOPK * TPB, B]),
                                       op=ALU.add))
            dve.wait_ge(s_xrank, 1)
            ch(nc.vector.tensor_tensor(out=rankt[:].rearrange("p q b e -> p (q b e)"), in0=psS[:, 0, 0, :],
                                       in1=ohs[:].rearrange("p q b e -> p (q b e)"), op=ALU.mult))
            ch(nc.vector.tensor_reduce(rankf[:], rankt[:], AX.X, ALU.add))
            ch(nc.vector.scalar_tensor_tensor(xrow[:], rankf[:], float(CAP), xrow[:], ALU.min, ALU.add))
            nc.vector.tensor_copy(read_i[:], xrow[:]).then_inc(s_rows, 1)
            ch(nc.vector.tensor_scalar(rankf[:], rankf[:], float(CAP), None, ALU.is_le))
            ch(nc.vector.tensor_tensor(out=xrow[:], in0=xrow[:], in1=trash[:], op=ALU.subtract))
            ch(nc.vector.tensor_tensor(out=xrow[:], in0=xrow[:], in1=rankf[:], op=ALU.mult))
            nc.vector.tensor_tensor(out=write_i[:], in0=xrow[:], in1=trash[:], op=ALU.add).then_inc(s_rows, 1)

        def dispatch_pool(pool):
            pool.wait_ge(s_rows, B + 2)
            for k in range(TOPK):
                for T in range(NT):
                    nc.gpsimd.indirect_dma_start(
                        out=slots_in[:, :],
                        out_offset=bass.IndirectOffsetOnAxis(ap=write_i[:, k * TPB + T % TPB, T // TPB:T // TPB + 1], axis=0),
                        in_=zq[:, T, :], in_offset=None).then_inc(s_disp, 16)

        EP = EXPERTS // 2
        ROWT = -(-SLOTS // P)
        BLOCKS = [(c, min(512, SLOTS - c)) for c in range(0, SLOTS, 512)]
        HCH = HID // P

        def rows_of(i):
            return min(P, SLOTS - i * P)

        def turns(eng, body):
            body(0, True, False)
            with eng.Fori(1, EP - 1) as t:
                body(t, False, False)
            body(EP - 1, False, True)

        def moe_sync(sp):
            def load(e, q):
                sp.dma_start(wc[:, q], moe["w_c"][e].rearrange("(c p) h -> p c h", p=P)).then_inc(s_wload[q], 16)
                sp.dma_start(wg[:, q], moe["w_g"][e].rearrange("(c p) h -> p c h", p=P)).then_inc(s_wload[q], 16)
                sp.dma_start(bcg[:, q], moe["b_cg"][e]).then_inc(s_wload[q], 16)
                sp.dma_start(wp[:, q], moe["w_p"][e].rearrange("(m p) n -> p m n", p=P)).then_inc(s_wload[q], 16)
                sp.dma_start(bp[:, q], moe["b_p"][e].partition_broadcast(P)).then_inc(s_wload[q], 16)

            def load_x(e, q):
                n = (ROWT - 1) * P
                sp.dma_start(xr[:, q, 0:ROWT - 1, :], slots_in[bass.ds(e * SLOTS, n), :].rearrange("(i p) d -> p i d", p=P))\
                    .then_inc(s_xload[q], 16)
                sp.dma_start(xr[0:SLOTS - n, q, ROWT - 1, :], slots_in[bass.ds(e * SLOTS + n, SLOTS - n), :])\
                    .then_inc(s_xload[q], 16)

            sp.wait_ge(N_["c", "x_updated"], NT)
            for q in range(2):
                load(q, q)
            sp.wait_ge(s_disp, 16 * TOPK * NT)
            for q in range(2):
                load_x(q, q)
            with sp.Fori(1, EP) as t:
                for q in range(2):
                    sp.wait_ge(N_["e", "o_copied"], t * (2 * ROWT) + (q - 1) * ROWT)
                    load(2 * t + q, q)
                    load_x(2 * t + q, q)

        def moe_pe(pe):
            NB = len(BLOCKS)

            def transposes(t, q, blk, first):
                if blk == 0:
                    pe.wait_ge(s_xload[q], 32 * (t + 1))
                for i in range(blk * 4, min(blk * 4 + 4, ROWT)):
                    n = t * (2 * ROWT) + (q * ROWT + i)
                    if not (first and n < 2):
                        pe.wait_ge(N_["e", "xT_copied"], n - 1)
                    r = rows_of(i)
                    for c in range(DC):
                        m = nc.tensor.transpose(psT[:, i % 2, c * P:c * P + r], xr[0:r, q, i, c * P:(c + 1) * P], ident[0:r, 0:r])
                    m.then_inc(N_["e", "xT_done"], 1)

            def outputs(t, q, blk, first):
                for i in range(blk * 4, min(blk * 4 + 4, ROWT)):
                    n = t * (2 * ROWT) + (q * ROWT + i)
                    r = rows_of(i)
                    if i == blk * 4:
                        pe.wait_ge(N_["e", "silu_done"], ((t * 2 + q) * NB + blk + 1) * HCH)
                    if not (first and n < 2):
                        pe.wait_ge(N_["e", "o_copied"], n - 1)
                    par = (q * NB + blk) % 2
                    po = (psO, psM)[i % 2]
                    for m_ in range(HCH):
                        m = nc.tensor.matmul(po[0:r, 0:D], st[:, par, m_, (i % 4) * P:(i % 4) * P + r], wp[:, q, m_, :],
                                             start=(m_ == 0), stop=(m_ == HCH - 1))
                    m.then_inc(N_["e", "o_done"], 1)

            def body(t, first, last):
                for q in range(2):
                    for blk, (c0, w) in enumerate(BLOCKS):
                        pos = q * NB + blk
                        par = pos % 2
                        if blk == 0:
                            pe.wait_ge(s_wload[q], 80 * (t + 1))
                        pe.wait_ge(N_["e", "xT_copied"], t * (2 * ROWT) + (q * ROWT + min(blk * 4 + 4, ROWT)))
                        for m_ in range(HCH):
                            n = (t * 2 * NB + pos) * HCH + m_
                            if not (first and pos == 0 and m_ < 2):
                                pe.wait_ge(N_["e", "gated"], n - 1)
                            for which, wt in enumerate((wc, wg)):
                                for c in range(DC):
                                    m = nc.tensor.matmul(psS[:, m_ % 2, which, 0:w], wt[:, q, c, m_ * P:(m_ + 1) * P],
                                                         xT[:, par, c, 0:w], start=(c == 0), stop=(c == DC - 1))
                                m.then_inc(N_["e", "hg_done"], 1)
                            if m_ == 1 and not (first and pos == 0):
                                pq, pblk = divmod(pos - 1, NB) if pos else (1, NB - 1)
                                outputs(t if pos else t - 1, pq, pblk, first)
                            if m_ == 4:
                                nq, nblk = divmod(pos + 1, NB)
                                if nq < 2:
                                    transposes(t, nq, nblk, first)
                                elif not last:
                                    transposes(t + 1, 0, 0, False)
                if last:
                    outputs(t, 1, NB - 1, False)

            pe.wait_ge(s_xload[0], 32)
            transposes(0, 0, 0, True)
            turns(pe, body)

        def moe_act(act):
            NB = len(BLOCKS)

            def copies(t, q, blk):
                for i in range(blk * 4, min(blk * 4 + 4, ROWT)):
                    n = t * (2 * ROWT) + (q * ROWT + i)
                    r = rows_of(i)
                    act.wait_ge(N_["e", "xT_done"], n + 1)
                    nc.scalar.copy(xT[:, (q * NB + blk) % 2, :, (i % 4) * P:(i % 4) * P + r],
                                   psT[:, i % 2, 0:DC * P].rearrange("p (c t) -> p c t", c=DC)[:, :, 0:r])\
                        .then_inc(N_["e", "xT_copied"], 1)

            def silu(n, par, m_, w, first):
                act.wait_ge(N_["e", "gated"], n + 1)
                nc.scalar.activation(st[:, par, m_, 0:w], hg[:, m_ % 2, 0:w], ACT.Silu).then_inc(N_["e", "silu_done"], 1)

            def body(t, first, last):
                for q in range(2):
                    for blk, (c0, w) in enumerate(BLOCKS):
                        pos = q * NB + blk
                        for m_ in range(HCH):
                            n = (t * 2 * NB + pos) * HCH + m_
                            act.wait_ge(N_["e", "hg_done"], 2 * n + 1)
                            if not (first and pos == 0 and m_ < 2):
                                act.wait_ge(N_["e", "gated"], n - 1)
                            nc.scalar.activation(hb[:, m_ % 2, 0:w], psS[:, m_ % 2, 0, 0:w], ACT.Identity,
                                                 bias=bcg[:, q, m_:m_ + 1]).then_inc(N_["e", "h_ready"], 1)
                            if m_ == 0:
                                if pos or not first:
                                    silu(n - 1, (pos + 1) % 2, HCH - 1, BLOCKS[(pos - 1) % NB][1], first)
                            else:
                                if m_ == 1 and not (first and pos < 2):
                                    a, b_ = divmod(pos - 2, NB) if pos >= 2 else (1, pos - 2 + NB)
                                    tt = t if pos >= 2 else t - 1
                                    act.wait_ge(N_["e", "o_done"], tt * (2 * ROWT) + (a * ROWT + min(b_ * 4 + 4, ROWT)))
                                silu(n - 1, pos % 2, m_ - 1, w, first)
                            if m_ == 4:
                                nq, nblk = divmod(pos + 1, NB)
                                if nq < 2:
                                    copies(t, nq, nblk)
                                elif not last:
                                    copies(t + 1, 0, 0)
                if last:
                    silu(EP * 2 * NB * HCH - 1, 1, HCH - 1, BLOCKS[NB - 1][1], False)

            copies(0, 0, 0)
            turns(act, body)

        def moe_dve(dve):
            NB = len(BLOCKS)

            def outputs(t, q, blk, first):
                for i in range(blk * 4, min(blk * 4 + 4, ROWT)):
                    n = t * (2 * ROWT) + (q * ROWT + i)
                    r = rows_of(i)
                    dve.wait_ge(N_["e", "o_done"], n + 1)
                    if not (first and n < YS):
                        k = (2 * t + q) * (ROWT // YS) + i // YS
                        dve.wait_ge(s_ostore[i % YS], k * 16)
                    nc.vector.tensor_tensor(out=yo[0:r, i % YS, :], in0=(psO, psM)[i % 2][0:r, 0:D], in1=bp[0:r, q, :],
                                            op=ALU.add).then_inc(N_["e", "o_copied"], 1)

            def body(t, first, last):
                for q in range(2):
                    for blk, (c0, w) in enumerate(BLOCKS):
                        pos = q * NB + blk
                        for m_ in range(HCH):
                            n = (t * 2 * NB + pos) * HCH + m_
                            dve.wait_ge(N_["e", "hg_done"], 2 * n + 2)
                            dve.wait_ge(N_["e", "h_ready"], n + 1)
                            if not (first and pos == 0 and m_ < 2):
                                dve.wait_ge(N_["e", "silu_done"], n - 1)
                            nc.vector.scalar_tensor_tensor(hg[:, m_ % 2, 0:w], psS[:, m_ % 2, 1, 0:w],
                                                           bcg[:, q, HCH + m_:HCH + m_ + 1], hb[:, m_ % 2, 0:w],
                                                           ALU.add, ALU.mult).then_inc(N_["e", "gated"], 1)
                            if m_ == 1 and not (first and pos == 0):
                                pq, pblk = divmod(pos - 1, NB) if pos else (1, NB - 1)
                                outputs(t if pos else t - 1, pq, pblk, first)
                if last:
                    outputs(t, 1, NB - 1, False)
            turns(dve, body)
            with dve.Fori(0, NT // GS) as g:
                for u in range(GS):
                    T = g * GS + u
                    dve.wait_ge(s_yload[u], 32 * (g + 1))
                    ch_fin = nc.vector.scalar_tensor_tensor(x[:, T, :], yg[:, u, 0, :], prob[:, 0, bass.ds(T, 1)], x[:, T, :],
                                                            ALU.mult, ALU.add)
                    ch_fin.then_inc(s_half, 1)
                    dve.wait_ge(s_half, T + 1)
                    nc.vector.scalar_tensor_tensor(x[:, T, :], yg[:, u, 1, :], prob[:, 1, bass.ds(T, 1)], x[:, T, :],
                                                   ALU.mult, ALU.add).then_inc(s_fin, 1)

        def moe_pool(pool):
            with pool.Fori(0, EXPERTS) as e:
                for i in range(ROWT):
                    r = rows_of(i)
                    pool.wait_ge(N_["e", "o_copied"], e * ROWT + i + 1)
                    pool.dma_start(slots_out[bass.ds(e * SLOTS + i * P, r), :], yo[0:r, i % YS, :])\
                        .then_inc(s_ostore[i % YS], 16)
            for u in range(YS):
                pool.wait_ge(s_ostore[u], 16 * EXPERTS * ROWT // YS)
            for T in range(NT):
                if T >= GS:
                    pool.wait_ge(s_fin, T - GS + 1)
                for k in range(TOPK):
                    nc.gpsimd.indirect_dma_start(
                        out=yg[:, T % GS, k, :], out_offset=None, in_=slots_out[:, :],
                        in_offset=bass.IndirectOffsetOnAxis(ap=read_i[:, k * TPB + T % TPB, T // TPB:T // TPB + 1], axis=0))\
                        .then_inc(s_yload[T % GS], 16)

        def final_sync(sp):
            with sp.Fori(0, NT // GS) as g:
                sp.wait_ge(s_fin, g * GS + GS)
                sp.dma_start(out_v[:, bass.ds(g * GS, GS), :], x[:, bass.ds(g * GS, GS), :]).then_inc(s_out, 16)
            sp.wait_ge(s_out, 16 * (NT // GS))

        block = es.enter_context(nc.Block())

        @block.sync
        def _(sp):
            prep_sync(sp)
            route_sync(sp)
            ffn_sync(sp)
            moe_sync(sp)
            final_sync(sp)

        @block.gpsimd
        def _(pool):
            prep_pool(pool)
            pool.wait_ge(s_w, 16 * N_W)
            xattn_pool(pool, "a")
            scatter_pool(pool)
            gather_pool(pool)
            xattn_pool(pool, "c")
            dispatch_pool(pool)
            moe_pool(pool)

        @block.scalar
        def _(act):
            prep_loads_act(act)
            prep_act(act)
            xattn_act(act, "a")
            route_act(act, "b")
            ffn_act(act)
            sa_act(act)
            xattn_act(act, "c")
            route_act(act, "d")
            topk_act(act)
            moe_act(act)

        @block.vector
        def _(dve):
            prep_dve(dve)
            xattn_dve(dve, "a")
            tree_dve(dve)
            ffn_dve(dve)
            sa_dve(dve)
            xattn_dve(dve, "c")
            topk_dve(dve)
            moe_dve(dve)

        @block.tensor
        def _(pe):
            prep_pe(pe)
            xattn_pe(pe, "a")
            route_pe(pe, "b", nodew, NODES3, lambda pe: pe.wait_ge(s_node, 64))
            rank_pe(pe)
            ffn_pe(pe)
            sa_pe(pe)
            xattn_pe(pe, "c")
            route_pe(pe, "d", routerw, EXPERTS, lambda pe: None)
            topk_pe(pe)
            moe_pe(pe)


def kernel(**inputs):
    import numpy as np
    import concourse.bacc as bacc
    from concourse.bass_utils import run_bass_kernel_spmd

    nc = bacc.Bacc("TRN2", target_bir_lowering=False, num_devices=1)
    arrays = {}

    def dram(name, a=None):
        a = np.ascontiguousarray(inputs[name] if a is None else a)
        arrays[f"in_{name}"] = a
        return nc.dram_tensor(f"in_{name}", a.shape, mybir.dt.from_np(a.dtype), kind="ExternalInput").ap()

    def weight(k, name, transposed=False):
        a = np.asarray(inputs[name])
        if transposed and k[0] == "w":
            a = a.T
        if k in ("bq", "bk"):
            a = a.reshape(DC, P).T
        return dram(name, a)

    xa = {
        "a": {k: weight(k, f"L0_xattn_{n}") for k, n in (("wq", "W_Q"), ("bq", "b_Q"), ("wk", "W_K"), ("bk", "b_K"),
                                                    ("wv", "W_V"), ("bv", "b_V"), ("wo", "W_O"), ("bo", "b_O"))},
        "c": {k: weight(k, f"L1_xattn_{n}", transposed=True)
              for k, n in (("wq", "q_w"), ("bq", "q_b"), ("wk", "k_w"), ("bk", "k_b"), ("wv", "v_w"), ("bv", "v_b"))},
    }
    trees = [{k: np.asarray(inputs[f"L0_ffn_{t}_{k}"]) for k in ("node_w", "node_b", "w1", "b1", "w2", "b2")} for t in "qkv"]

    def leaf_in(t):
        w = t["w1"].reshape(LEAVES, DC, P, LEAF_W).transpose(0, 2, 1, 3).reshape(LEAVES, P, DC * LEAF_W)
        b = np.zeros((LEAVES, P, 2), w.dtype)
        b[:, 0:LEAF_W, 0] = t["b1"]
        return np.concatenate([w, b], axis=2)

    ffn = {
        "node_w": dram("ffn_node_w", np.concatenate([t["node_w"] for t in trees]).T),
        "node_b": dram("ffn_node_b", np.concatenate([t["node_b"] for t in trees])),
        "w1b": dram("ffn_w1b", np.concatenate([leaf_in(t) for t in trees])),
        "w2b": dram("ffn_w2b", np.concatenate([np.concatenate([t["w2"], t["b2"][:, None, :]], axis=1) for t in trees])),
    }
    def bias_columns(name):
        return np.asarray(inputs[name]).reshape(EXPERTS, HID // P, P).transpose(0, 2, 1)

    moe = {
        "router_w": dram("L1_ffn_router_w"), "router_b": dram("L1_ffn_router_b"),
        "w_c": dram("L1_ffn_w_c_fc"), "w_g": dram("L1_ffn_w_gate"), "w_p": dram("L1_ffn_w_c_proj"),
        "b_cg": dram("moe_b_cg", np.concatenate([bias_columns("L1_ffn_b_c_fc"), bias_columns("L1_ffn_b_gate")], axis=2)),
        "b_p": dram("L1_ffn_b_c_proj", np.asarray(inputs["L1_ffn_b_c_proj"]).reshape(EXPERTS, D)),
    }
    x_in, ctx_in, mask_in = dram("x"), dram("ctx_1024"), dram("mask_BxS2_ik0")
    out = nc.dram_tensor("out", x_in.shape, F32, kind="ExternalOutput").ap()
    xattn_ffn_kernel(nc, x_in, ctx_in, mask_in, xa, ffn, moe, out)
    r = run_bass_kernel_spmd(nc, [arrays], core_ids=[0])
    return r.results[0]["out"]
```

```python
import concourse.bass as bass
from concourse import mybir
from contextlib import ExitStack

F32 = mybir.dt.float32
BF16 = mybir.dt.bfloat16
I32 = mybir.dt.int32
U32 = mybir.dt.uint32
ALU = mybir.AluOpType
ACT = mybir.ActivationFunctionType
AX = mybir.AxisListType

P = 128
B, SEQ, D = 4, 1024, 256
NT = B * SEQ // P
TPB = SEQ // P
GT = 4
DC = D // P
HEADS, DK, CTX = 16, 16, 77
HH = HEADS // 2
HQ = HH // 2
HW = HH * CTX
VW = DK + 1
EPS = 1e-5
NEG = -1e30
STEPS = 2 * TPB
DRAIN = 6

LEAVES, DEPTH, LEAF_W = 16, 4, 64
NODES = LEAVES - 1
NODES3, LEAVES3 = 3 * NODES, 3 * LEAVES
SET_TILES = NT + LEAVES
SET_ROWS = SET_TILES * P
FS = 8
GB = 2
WS = 4
IT_SET = SET_TILES // FS
W1W = DC * LEAF_W + 2
ZR = 16
SA_SCALE = D ** -0.5
EXPERTS, TOPK = 8, 2
CAP = int(1.2 * TOPK * SEQ // EXPERTS)
SLOTS = B * CAP
ROW_TRASH = EXPERTS * SLOTS
SLOT_ROWS = ROW_TRASH + TOPK * NT * P
SLOT_FILL = 10240
HID = 1024
YS = 5
GS = 4


class Link:

    def __init__(self, eng, sem):
        self.eng, self.sem, self.base, self.n = eng, sem, 0, 0

    def restart(self, base):
        self.base, self.n = base, 0

    def count(self, ins):
        self.n += 1
        ins.then_inc(self.sem, 1)

    def wait(self):
        self.eng.wait_ge(self.sem, self.base + self.n)

    def __call__(self, ins):
        self.count(ins)
        self.wait()


def xattn_ffn_kernel(nc, x_in, ctx_in, mask_in, xa, ffn, moe, out):
    es = ExitStack()
    with es:
        def sb(name, shape, dt=F32, scope=es):
            return scope.enter_context(nc.sbuf_tensor(name, shape, dt))

        def pb(name, shape, dt=F32, scope=es):
            return scope.enter_context(nc.psum_tensor(name, shape, dt))

        def sem(name):
            return es.enter_context(nc.semaphore(name))

        x = sb("x", [P, NT, D])
        ident = sb("ident", [P, P])
        stat = sb("stat", [P, TPB, 6])
        mean = sb("mean", [P, TPB])
        rstd = sb("rstd", [P, TPB])
        nw = sb("nw", [P, 2, NT])
        stat_all = sb("stat_all", [P, NT, 6])
        mean_all = sb("mean_all", [P, NT])
        rstd_all = sb("rstd_all", [P, NT])
        x_v = x_in.rearrange("b (t p) d -> p (b t) d", p=P)
        out_v = out.rearrange("b (t p) d -> p (b t) d", p=P)

        kb, vb = {}, {}
        kb["c"] = sb("kb_c", [P, B, DC, HH, CTX])
        vb["c"] = sb("vb_c", [CTX, B, HEADS, VW])
        neg = sb("neg", [P, B, CTX], BF16)
        mean128 = sb("mean128", [P, P], BF16)
        wq = {L: sb(f"wq_{L}", [P, DC, D]) for L in "ac"}
        bq = {L: sb(f"bq_{L}", [P, DC]) for L in "ac"}
        bk = {L: sb(f"bk_{L}", [P, DC]) for L in "ac"}
        wo = sb("wo", [P, DC, D])
        bo_bc = sb("bo_bc", [P, D])

        zq = sb("zq", [P, NT, D])
        nodew = sb("nodew", [P, DC, NODES3])
        nodeb = sb("nodeb", [P, NODES3])
        bits = sb("bits", [P, TPB * NODES3])
        path = [sb(f"path{l}", [P, TPB * 3, 2 ** (l + 1)]) for l in range(DEPTH - 1)]
        onehot = sb("onehot", [P, NT, LEAVES3], BF16)
        before = sb("before", [P, NT + 1, LEAVES3], BF16)
        tri = sb("tri", [P, P], BF16)
        ones_bf = sb("ones_bf", [P, P], BF16)
        ones_row = sb("ones_row", [P, LEAVES])
        set_leaf0 = sb("set_leaf0", [1, 3, SET_TILES])
        tile_row = sb("tile_row", [1, SET_TILES])
        expert_id = sb("expert_id", [P, EXPERTS])
        trash = sb("trash", [P, B, TOPK * TPB])
        scan_on = sb("scan_on", [P, EXPERTS, TOPK * TPB])
        cnt_i = sb("cnt_i", [P, LEAVES3], I32)
        padded, incl, base = (sb(n, [P, LEAVES3]) for n in ("padded", "incl", "base"))
        rowt = sb("rowt", [P, TPB, LEAVES3])
        rowf = sb("rowf", [P, 3, TPB])
        row_i = sb("row_i", [P, 3, NT], U32)
        leaff = sb("leaff", [1, 3, SET_TILES])
        leaf_i = sb("leaf_i", [1, 3 * SET_TILES], I32)

        routerw = sb("routerw", [P, DC, EXPERTS])
        routerb = sb("routerb", [P, EXPERTS])
        logit = sb("logit", [P, NT, EXPERTS])
        best = sb("best", [P, NT, 8])
        best_i = sb("best_i", [P, NT, 8], U32)
        choice = sb("choice", [P, NT, TOPK])
        prob = sb("prob", [P, TOPK, NT])
        ohs = sb("ohs", [P, B, EXPERTS, TOPK * TPB], BF16)
        ohb = sb("ohb", [P, B, EXPERTS, TOPK * TPB], BF16)
        upto = sb("upto", [P, EXPERTS, TOPK * TPB])
        xrow = sb("xrow", [P, TOPK * TPB])
        rankt = sb("rankt", [P, EXPERTS, TOPK * TPB])
        rankf = sb("rankf", [P, TOPK * TPB])
        read_i = sb("read_i", [P, B, TOPK * TPB], U32)
        write_i = sb("write_i", [P, B, TOPK * TPB], U32)

        sorted_in, sorted_out = ([nc.dram_tensor(f"sorted_{d}{s}", [SET_ROWS, D], F32, kind="Internal").ap()
                                  for s in range(3)] for d in ("in", "out"))
        slots_in = nc.dram_tensor("slots_in", [SLOT_ROWS, D], F32, kind="Internal").ap()
        slots_out = nc.dram_tensor("slots_out", [EXPERTS * SLOTS, D], F32, kind="Internal").ap()

        with ExitStack() as r1:
            kb["a"] = sb("kb_a", [P, B, DC, HH, CTX], scope=r1)
            vb["a"] = sb("vb_a", [CTX, B, HEADS, VW], scope=r1)
            ctx_sb = sb("ctx_sb", [CTX, B, D], scope=r1)
            ctxT = sb("ctxT", [P, DC, B * CTX], scope=r1)
            wk = {L: sb(f"wk_{L}", [P, DC, D], scope=r1) for L in "ac"}
            wv = {L: sb(f"wv_{L}", [P, DC, D], scope=r1) for L in "ac"}
            kT = {L: sb(f"kT_{L}", [P, DC, B * CTX], scope=r1) for L in "ac"}
            bv_bc = {L: sb(f"bv_{L}", [CTX, D], scope=r1) for L in "ac"}
            mask_sb = sb("mask_sb", [P, B * CTX], I32, scope=r1)
            headsel = sb("headsel", [P, HH], scope=r1)
            sa = {
                "y": sb("y", [P, 2, D], scope=r1),
                "yT": sb("yT", [P, DC, GT * P], scope=r1),
                "qT": sb("qT", [P, 2, DC, GT * P], scope=r1),
                "mx": sb("mx", [P, 2, HH], scope=r1),
                "pr": sb("pr", [P, 2, HH, CTX], scope=r1),
                "prT": sb("prT", [CTX, 2, HH, P], scope=r1),
                "rinv": sb("rinv", [P, 2, HH], scope=r1),
                "o": sb("o", [P, 2, D], scope=r1),
                "oT": sb("oT", [P, DC, P], scope=r1),
            }
        with ExitStack() as r2:
            kg = sb("kg", [P, TPB, D], scope=r2)
            with ExitStack() as r3:
                vg = sb("vg", [P, 2, TPB, D], scope=r3)
            with ExitStack() as r4:
                ends = sb("ends", [1, 3, SET_TILES, LEAVES], scope=r4)
            with ExitStack() as r3:
                zt = sb("zt", [P, FS, D], scope=r3)
                yt = sb("yt", [P, FS, D], scope=r3)
                with ExitStack() as r4:
                    w1_all = sb("w1_all", [P, 2, LEAVES, W1W], scope=r4)
                    w2_all = sb("w2_all", [LEAF_W + 1, 2, LEAVES, D], scope=r4)
                    w1s = sb("w1s", [P, WS, W1W], scope=r4)
                    w2s = sb("w2s", [LEAF_W + 1, WS, D], scope=r4)
                    zT = sb("zT", [P, 2, DC, P], scope=r4)
                    hT = sb("hT", [LEAF_W + 1, 2, P], scope=r4)
                kTs = sb("kTs", [P, 2, DC, SEQ], scope=r3)
                qTs = sb("qTs", [P, 2, DC, P], scope=r3)
                pg = sb("pg", [P, 2, SEQ], scope=r3)
                pgT = sb("pgT", [P, 2, TPB, P], scope=r3)
                smax, nmax, rsum = (sb(n, [P, 2], scope=r3) for n in ("smax", "nmax", "rsum"))
                psum_exp = sb("psum_exp", [P, 4], scope=r3)

        with ExitStack() as r5:
            wc = sb("wc", [P, 2, DC, HID], scope=r5)
            wg = sb("wg", [P, 2, DC, HID], scope=r5)
            wp = sb("wp", [P, 2, HID // P, D], scope=r5)
            bcg = sb("bcg", [P, 2, 2 * HID // P], scope=r5)
            bp = sb("bp", [P, 2, D], scope=r5)
            xr = sb("xr", [P, 2, -(-SLOTS // P), D], scope=r5)
            xT = sb("xT", [P, 2, DC, 512], scope=r5)
            hb = sb("hb", [P, 2, 512], scope=r5)
            hg = sb("hg", [P, 2, 512], scope=r5)
        dead = kb["c"][:].rearrange("p b j h s -> p (b j h s)")
        yo = dead[:, 0:YS * D].rearrange("p (u d) -> p u d", u=YS)
        zT_of = {"b": zT, "d": dead[:, 4096:4096 + 2 * DC * P].rearrange("p (u c t) -> p u c t", u=2, c=DC)}
        yg = dead[:, YS * D:(YS + GS * TOPK) * D].rearrange("p (u k d) -> p u k d", u=GS, k=TOPK)
        st = zq[:].rearrange("p t d -> p (t d)").rearrange("p (a m w) -> p a m w", a=2, m=HID // P)

        psS = pb("psS", [P, 2, 2, 512])
        psT = pb("psT", [P, 2, 512])
        psO = pb("psO", [P, 512])
        psM = pb("psM", [P, 512])

        s_x0 = sem("x_batch0_loaded")
        s_ctx, s_x, s_w, s_mask = sem("ctx_loaded"), sem("x_loaded"), sem("weights_loaded"), sem("mask_loaded")
        s_ident, s_const, s_hs = sem("ident_ready"), sem("consts_ready"), sem("headsel_ready")
        s_poolc = sem("pool_chain")
        p_ctxT, p_ctxTc, p_k, p_kc, p_v, p_vc = (sem(n) for n in
            ("ctxT_done", "ctxT_copied", "k_done", "k_copied", "v_done", "v_copied"))
        s_kb = {L: sem(f"kb_ready_{L}") for L in "ac"}
        s_neg = sem("neg_ready")
        s_out = sem("out_stored")
        s_dve = sem("dve_chain")

        N_ = {}
        for L in "ac":
            for n in ("yT_done", "yT_copied", "q_done", "q_copied", "scores_done", "shifted", "exp_done",
                      "prT_done", "prT_copied", "pv_done", "o_ready", "oT_done", "oT_copied", "wo_done",
                      "y_ready", "x_biased", "x_updated", "chain"):
                N_[L, n] = sem(f"{L}_{n}")

        for L in "bd":
            for n in ("z_ready", "zT_done", "zT_copied", "node_done", "scores_used", "rank_done", "chain"):
                N_[L, n] = sem(f"{L}_{n}")
        for n in ("zT_done", "zT_copied", "w_copied", "h_done", "h_copied", "y_done", "y_copied"):
            N_["f", n] = sem(f"f_{n}")
        for n in ("tr_done", "tr_copied", "scores_done", "bias_ready", "exp_done", "pT_done", "pT_copied", "pv_done",
                  "x_updated", "chain"):
            N_["g", n] = sem(f"g_{n}")
        s_node, s_zeros, s_zfill, s_tables = sem("node_loaded"), sem("zeros_ready"), sem("zero_filled"), sem("tables_ready")
        for n in ("xT_done", "xT_copied", "hg_done", "h_ready", "gated", "silu_done", "o_done", "o_copied"):
            N_["e", n] = sem(f"e_{n}")
        s_before = sem("tiles_summed")
        s_ohs, s_xrank, s_gap, s_gexp, s_disp, s_half, s_fin = (sem(n) for n in (
            "onehots_ready", "slot_ranks_done", "gap_ready", "gap_exp_done", "dispatched", "first_added", "x_final"))
        s_wload = [sem(f"expert_loaded{q}") for q in range(2)]
        s_xload = [sem(f"slots_loaded{q}") for q in range(2)]
        s_ostore = [sem(f"o_stored{u}") for u in range(YS)]
        s_yload = [sem(f"outputs_gathered{u}") for u in range(GS)]
        s_rows, s_leaf = sem("rows_ready"), sem("leaf_table_ready")
        s_scat = [sem(f"scattered{s}") for s in range(3)]
        s_qgath, s_kgath, s_vgath = sem("queries_gathered"), sem("keys_gathered"), sem("values_gathered")
        s_leafw = [sem(f"leaf_weights_loaded{s}") for s in range(3)]
        s_zload = [sem(f"tiles_loaded{g}") for g in range(FS // GB)]
        s_ystore = [sem(f"y_stored{g}") for g in range(FS // GB)]

        def prep_sync(sp):
            sp.dma_start(ctx_sb[:], ctx_in.rearrange("b s d -> s b d")).then_inc(s_ctx, 16)
            for L in "ac":
                sp.dma_start(wk[L][:], xa[L]["wk"].rearrange("(c p) n -> p c n", p=P)).then_inc(s_w, 16)
                sp.dma_start(wv[L][:], xa[L]["wv"].rearrange("(c p) n -> p c n", p=P)).then_inc(s_w, 16)
                sp.dma_start(wq[L][:], xa[L]["wq"].rearrange("(c p) n -> p c n", p=P)).then_inc(s_w, 16)
            sp.dma_start(wo[:], xa["a"]["wo"].rearrange("(c p) n -> p c n", p=P)).then_inc(s_w, 16)

        def prep_loads_act(act):
            act.dma_start(x[:, 0:TPB, :], x_v[:, 0:TPB, :]).then_inc(s_x0, 16)
            for L in "ac":
                act.dma_start(bq[L][:], xa[L]["bq"]).then_inc(s_w, 16)
                act.dma_start(bk[L][:], xa[L]["bk"]).then_inc(s_w, 16)
                act.dma_start(bv_bc[L][:], xa[L]["bv"].partition_broadcast(CTX)).then_inc(s_w, 16)
            act.dma_start(bo_bc[:], xa["a"]["bo"].partition_broadcast(P)).then_inc(s_w, 16)
            act.dma_start(mask_sb[:], mask_in.rearrange("b s -> (b s)").partition_broadcast(P)).then_inc(s_mask, 16)
            act.dma_start(x[:, TPB:NT, :], x_v[:, TPB:NT, :]).then_inc(s_x, 16)

        N_W = 14

        def prep_pool(pool):
            ch = Link(pool, s_poolc)
            ch(nc.gpsimd.memset(ident[:], 0.0))
            nc.gpsimd.affine_select(out=ident[:], in_=ident[:], compare_op=ALU.not_equal, fill=1.0, base=0,
                                    pattern=[[-1, P]], channel_multiplier=1).then_inc(s_ident, 1)
            ch(nc.gpsimd.memset(headsel[:], 1.0 / DK ** 0.5))
            ch(nc.gpsimd.affine_select(out=headsel[:], in_=headsel[:], compare_op=ALU.is_ge, fill=0.0, base=0,
                                       pattern=[[-DK, HH]], channel_multiplier=1))
            nc.gpsimd.affine_select(out=headsel[:], in_=headsel[:], compare_op=ALU.is_ge, fill=0.0, base=DK - 1,
                                    pattern=[[DK, HH]], channel_multiplier=-1).then_inc(s_hs, 1)
            nc.gpsimd.memset(mean128[:], 1.0 / P).then_inc(s_const, 1)
            for L in "ac":
                nc.gpsimd.memset(vb[L][:, :, :, DK:VW], 1.0).then_inc(s_const, 1)
            consts_pool(pool, ch)
            pool.wait_ge(s_hs, 1)
            key_blocks(pool, nc.gpsimd, "c", 2 * DC)

        def key_blocks(eng, e, L, copied):
            eng.wait_ge(p_kc, copied)
            for b in range(B):
                for j in range(DC):
                    e.tensor_tensor(
                        out=kb[L][:, b, j],
                        in0=kT[L][:, j, b * CTX:(b + 1) * CTX].unsqueeze(1).broadcast_to([P, HH, CTX]),
                        in1=headsel[:].unsqueeze(2).broadcast_to([P, HH, CTX]),
                        op=ALU.mult).then_inc(s_kb[L], 1)

        def prep_pe(pe):
            pe.wait_ge(s_ident, 1)
            pe.wait_ge(s_ctx, 16)
            for b in range(B):
                for c in range(DC):
                    i = nc.tensor.transpose(psS[:, c, 0, b * CTX:(b + 1) * CTX], ctx_sb[:, b, c * P:(c + 1) * P],
                                            ident[0:CTX, 0:CTX])
                    if b == B - 1:
                        i.then_inc(p_ctxT, 1)
            pe.wait_ge(s_w, 16 * N_W)
            pe.wait_ge(p_ctxTc, DC)
            for n, (L, j) in enumerate((L, j) for L in "ac" for j in range(DC)):
                for c in range(DC):
                    i = nc.tensor.matmul(psS[:, n // 2, n % 2, 0:B * CTX], wk[L][:, c, j * P:(j + 1) * P],
                                         ctxT[:, c, :], start=(c == 0), stop=(c == DC - 1))
                i.then_inc(p_k, 1)
            for n, (L, b) in enumerate((L, b) for L in "ac" for b in range(B)):
                if n >= 2:
                    pe.wait_ge(p_vc, n - 1)
                for c in range(DC):
                    i = nc.tensor.matmul(psT[0:CTX, n % 2, 0:D], ctxT[:, c, b * CTX:(b + 1) * CTX],
                                         wv[L][:, c, :], start=(c == 0), stop=(c == DC - 1))
                i.then_inc(p_v, 1)

        def prep_act(act):
            for c in range(DC):
                act.wait_ge(p_ctxT, c + 1)
                nc.scalar.copy(ctxT[:, c, :], psS[:, c, 0, 0:B * CTX]).then_inc(p_ctxTc, 1)
            act.wait_ge(s_w, 16 * N_W)
            for n, (L, j) in enumerate((L, j) for L in "ac" for j in range(DC)):
                act.wait_ge(p_k, n + 1)
                nc.scalar.activation(kT[L][:, j, :], psS[:, n // 2, n % 2, 0:B * CTX], ACT.Identity,
                                     bias=bk[L][:, j:j + 1]).then_inc(p_kc, 1)

        def prep_dve(dve):
            dve.wait_ge(s_mask, 16)
            nc.vector.tensor_scalar(neg[:].rearrange("p b s -> p (b s)"), mask_sb[:], 0, NEG,
                                    ALU.is_gt, ALU.mult).then_inc(s_neg, 1)
            dve.wait_ge(s_w, 16 * N_W)
            for n, (L, b) in enumerate((L, b) for L in "ac" for b in range(B)):
                dve.wait_ge(p_v, n + 1)
                nc.vector.tensor_tensor(
                    out=vb[L][:, b, :, 0:DK],
                    in0=psT[0:CTX, n % 2, 0:D].rearrange("p (h d) -> p h d", h=HEADS),
                    in1=bv_bc[L][:].rearrange("p (h d) -> p h d", h=HEADS), op=ALU.add).then_inc(p_vc, 1)
            dve.wait_ge(s_hs, 1)
            key_blocks(dve, nc.vector, "a", DC)

        def bodies(eng, step, chain=None, per=0):
            for k in range(STEPS):
                step(0, k, True, False)
            done = chain.base + chain.n if chain else 0
            with eng.Fori(1, B - 1) as b:
                if chain:
                    chain.restart(b * per + (done - per))
                for k in range(STEPS):
                    step(b, k, False, False)
                assert not chain or chain.n == per
            if chain:
                chain.restart(done + (B - 2) * per)
            for k in range(STEPS + DRAIN):
                step(B - 1, k, False, True)

        def query_piece(f):
            return f % 2, (f - GT) // 2

        def piece_copied(pe, L, G, f):
            if f < GT:
                pe.wait_ge(N_[L, "yT_copied"], GT * G + f + 1)
            else:
                pe.wait_ge(N_[L, "q_copied"], GT * G + (f - GT) + 1)

        def front_pe(pe, L, G, f, first=False):
            if f < GT:
                T = GT * G + f
                pe.wait_ge(N_[L, "y_ready"], T + 1)
                if not first:
                    piece_copied(pe, L, G if f else G - 1, (f - 1) % 8)
                for c in range(DC):
                    m = nc.tensor.transpose(psM[:, c * P:(c + 1) * P], sa["y"][:, f % 2, c * P:(c + 1) * P], ident[:])
                m.then_inc(N_[L, "yT_done"], 1)
            else:
                j, h = query_piece(f)
                piece_copied(pe, L, G, f - 1)
                for c in range(DC):
                    m = nc.tensor.matmul(psM[:, 0:2 * P], wq[L][:, c, j * P:(j + 1) * P],
                                         sa["yT"][:, c, h * 2 * P:(h + 1) * 2 * P],
                                         start=(c == 0), stop=(c == DC - 1))
                m.then_inc(N_[L, "q_done"], 1)

        def front_act(act, L, G, g2, f):
            if f < GT:
                act.wait_ge(N_[L, "yT_done"], GT * G + f + 1)
                nc.scalar.copy(sa["yT"][:, :, f * P:(f + 1) * P],
                               psM[:, 0:D].rearrange("p (c t) -> p c t", c=DC)).then_inc(N_[L, "yT_copied"], 1)
            else:
                j, h = query_piece(f)
                act.wait_ge(N_[L, "q_done"], GT * G + (f - GT) + 1)
                nc.scalar.activation(sa["qT"][:, g2, j, h * 2 * P:(h + 1) * 2 * P], psM[:, 0:2 * P], ACT.Identity,
                                     bias=bq[L][:, j:j + 1]).then_inc(N_[L, "q_copied"], 1)

        def xattn_pe(pe, L):
            def step(b, k, first, last):
                n = STEPS * b + k
                drain = k >= STEPS
                if not drain:
                    g = k // 8
                    if k % 4 == 0:
                        pe.wait_ge(N_[L, "q_copied"], GT * (2 * b + g) + (2 if k % 8 == 0 else 4))
                    if not (first and k < 2):
                        pe.wait_ge(N_[L, "shifted"], n - 1)
                    for q in range(2):
                        o = psS[:, k % 2, q, 0:HQ * CTX].rearrange("p (h s) -> p h s", h=HQ)
                        j = k % 2
                        lhs = sa["qT"][:, g, j, ((k // 2) % GT) * P:((k // 2) % GT + 1) * P]
                        m = nc.tensor.matmul(o, lhs, kb[L][:, b, j, q * HQ:(q + 1) * HQ, :],
                                             start=True, stop=(L == "a"))
                        if L == "c":
                            m = nc.tensor.matmul(o, mean128[:], neg[:, b, :].unsqueeze(1).broadcast_to([P, HQ, CTX]),
                                                 start=False, stop=True)
                    m.then_inc(N_[L, "scores_done"], 1)
                out_tile = L == "a" and k % 2 == 0 and not (first and k < 6)
                T = TPB * b + (k - 6) // 2
                if out_tile:
                    pe.wait_ge(N_[L, "o_ready"], 2 * T + 2)
                    if not (last and k >= 9):
                        piece_copied(pe, L, 2 * b + (k - 1) // 8 + 1, (k - 1) % 8)
                    else:
                        pe.wait_ge(N_[L, "x_updated"], T)
                    for c in range(DC):
                        m = nc.tensor.transpose(psM[:, c * P:(c + 1) * P],
                                                sa["o"][:, ((k - 6) // 2) % 2, c * P:(c + 1) * P], ident[:])
                    m.then_inc(N_[L, "oT_done"], 1)
                if k - 1 < STEPS and not (first and k < 1):
                    pe.wait_ge(N_[L, "exp_done"], n)
                    for q in range(2):
                        if not (first and k < 2):
                            pe.wait_ge(N_[L, "prT_copied"], 2 * (n - 2) + q + 1)
                        for h in range(HQ):
                            m = nc.tensor.transpose(psT[0:CTX, q, h * P:(h + 1) * P],
                                                    sa["pr"][:, (k - 1) % 2, q * HQ + h, :], ident[:])
                        m.then_inc(N_[L, "prT_done"], 1)
                if not (last and k >= 8):
                    if out_tile:
                        pe.wait_ge(N_[L, "oT_copied"], T + 1)
                    elif L == "a" and not (first and k < 7):
                        pe.wait_ge(N_[L, "x_updated"], TPB * b + (k - 7) // 2 + 1)
                    front_pe(pe, L, 2 * b + k // 8 + 1, k % 8)
                if k - 2 < STEPS and not (first and k < 2):
                    pe.wait_ge(N_[L, "prT_copied"], 2 * (n - 2) + 2)
                    if not (first and k < 3):
                        pe.wait_ge(N_[L, "o_ready"], n - 2)
                    bb = b if k >= 2 else b - 1
                    for h in range(HH):
                        m = nc.tensor.matmul(psO[:, h * VW:(h + 1) * VW], sa["prT"][:, k % 2, h, :],
                                             vb[L][:, bb, (k % 2) * HH + h, :], start=True, stop=True)
                    m.then_inc(N_[L, "pv_done"], 1)
                if out_tile:
                    if not (last and k >= 8):
                        piece_copied(pe, L, 2 * b + k // 8 + 1, k % 8)
                    else:
                        pe.wait_ge(N_[L, "oT_copied"], T + 1)
                    for c in range(DC):
                        m = nc.tensor.matmul(psM[:, 0:D], sa["oT"][:, c, :], wo[:, c, :],
                                             start=(c == 0), stop=(c == DC - 1))
                    m.then_inc(N_[L, "wo_done"], 1)

            if L == "a":
                pe.wait_ge(s_ident, 1)
            else:
                pe.wait_ge(N_["g", "tr_copied"], TPB + 2 * NT)
            for f in range(8):
                front_pe(pe, L, 0, f, f == 0)
            pe.wait_ge(s_kb[L], B * DC)
            pe.wait_ge(p_vc, 2 * B)
            pe.wait_ge(s_const, 3)
            pe.wait_ge(s_neg, 1)
            bodies(pe, step)

        def xattn_act(act, L):
            def step(b, k, first, last):
                n = STEPS * b + k
                if k - 1 < STEPS and not (first and k < 1):
                    act.wait_ge(N_[L, "shifted"], n)
                    pr = sa["pr"][:, (k - 1) % 2].rearrange("p h s -> p (h s)")
                    nc.scalar.activation(pr, pr, ACT.Exp).then_inc(N_[L, "exp_done"], 1)

                if L == "a" and k % 2 == 0 and not (first and k < 6):
                    act.wait_ge(N_[L, "oT_done"], TPB * b + (k - 6) // 2 + 1)
                    nc.scalar.copy(sa["oT"][:], psM[:, 0:D].rearrange("p (c t) -> p c t", c=DC))\
                        .then_inc(N_[L, "oT_copied"], 1)
                if k - 1 < STEPS and not (first and k < 1):
                    if not (first and k < 3):
                        act.wait_ge(N_[L, "pv_done"], n - 2)
                    for q in range(2):
                        act.wait_ge(N_[L, "prT_done"], 2 * (n - 1) + q + 1)
                        nc.scalar.copy(sa["prT"][:, (k - 1) % 2, q * HQ:(q + 1) * HQ, :],
                                       psT[0:CTX, q, :].rearrange("p (h t) -> p h t", h=HQ))\
                            .then_inc(N_[L, "prT_copied"], 1)
                if not (last and k >= 8):
                    front_act(act, L, 2 * b + k // 8 + 1, (k // 8 + 1) % 2, k % 8)

            act.wait_ge(s_w, 16 * N_W)
            for f in range(8):
                front_act(act, L, 0, 0, f)
            bodies(act, step)

        def tile_stats(ch, dst, T, i):
            ch.count(nc.vector.bn_stats(dst[:, i, :], x[:, T, :]))

        def tiles_rstd(ch, stat, mean, rstd):
            ch.wait()
            m_even, q_even, m_odd, q_odd = (stat[:, :, i] for i in (1, 2, 4, 5))
            n = stat.shape[1]
            v, t, r = nw[:, 0, 0:n], nw[:, 1, 0:n], rstd[:]
            ch.count(nc.vector.tensor_tensor(out=mean[:], in0=m_even, in1=m_odd, op=ALU.add))
            ch.count(nc.vector.tensor_tensor(out=t, in0=m_even, in1=m_odd, op=ALU.subtract))
            ch(nc.vector.tensor_tensor(out=v, in0=q_even, in1=q_odd, op=ALU.add))
            ch.count(nc.vector.tensor_scalar(mean[:], mean[:], 0.5, None, ALU.mult))
            ch(nc.vector.tensor_tensor(out=t, in0=t, in1=t, op=ALU.mult))
            ch(nc.vector.scalar_tensor_tensor(v, t, D / 4.0, v, ALU.mult, ALU.add))
            ch(nc.vector.tensor_scalar(v, v, 1.0 / D, EPS, ALU.mult, ALU.add))
            ch(nc.vector.tensor_scalar(r.bitcast(I32), v.bitcast(I32), -0.5, float(0x5F3759DF), ALU.mult, ALU.add))
            for _ in range(3):
                ch(nc.vector.tensor_tensor(out=t, in0=r, in1=r, op=ALU.mult))
                ch(nc.vector.scalar_tensor_tensor(t, t, -0.5, v, ALU.mult, ALU.mult))
                ch(nc.vector.scalar_tensor_tensor(r, t, 1.5, r, ALU.add, ALU.mult))
        LN_CHAIN = TPB + 8 + 9

        def normalise(dst, T, m, r):
            return nc.vector.tensor_scalar(dst, x[:, T, :], m, r, ALU.subtract, ALU.mult)

        def xattn_dve(dve, L):
            ch = Link(dve, N_[L, "chain"])

            def norm_tile(b, g, i):
                T = GT * (2 * b + g) + i
                if not (isinstance(b, int) and b == 0 and g == 0 and i < 2):
                    dve.wait_ge(N_[L, "yT_done"], T - 1)
                i8 = GT * (g % 2) + i
                normalise(sa["y"][:, i % 2, :], T, mean[:, i8:i8 + 1], rstd[:, i8:i8 + 1]).then_inc(N_[L, "y_ready"], 1)

            def step(b, k, first, last):
                n = STEPS * b + k
                if 3 <= k + (0 if first else 3) and k - 3 < STEPS:
                    par, tp, j = (k - 3) % 2, ((k - 3) // 2) % 2, (k - 3) % 2
                    dve.wait_ge(N_[L, "pv_done"], n - 2)
                    pv = psO[:, 0:HH * VW].rearrange("p (h d) -> p h d", h=HH)
                    ch(nc.vector.reciprocal(sa["rinv"][:, par, :], pv[:, :, DK]))
                    if j == 0 and not (first and k < 7):
                        dve.wait_ge(N_[L, "oT_done" if L == "a" else "x_updated"], TPB * b + (k - 3) // 2 - 1)
                    nc.vector.tensor_tensor(
                        out=sa["o"][:, tp, j * P:(j + 1) * P].rearrange("p (h d) -> p h d", h=HH),
                        in0=pv[:, :, 0:DK], in1=sa["rinv"][:, par, :].unsqueeze(2).broadcast_to([P, HH, DK]),
                        op=ALU.mult).then_inc(N_[L, "o_ready"], 1)
                if L == "a" and k % 2 == 1 and not (first and k < 7):
                    T = TPB * b + (k - 7) // 2
                    dve.wait_ge(N_[L, "wo_done"], T + 1)
                    dve.wait_ge(N_[L, "x_biased"], T + 1)
                    nc.vector.tensor_tensor(out=x[:, T, :], in0=psM[:, 0:D], in1=x[:, T, :], op=ALU.add)\
                        .then_inc(N_[L, "x_updated"], 1)
                if k < STEPS:
                    dve.wait_ge(N_[L, "scores_done"], n + 1)
                    s = psS[:, k % 2, :, 0:HQ * CTX].rearrange("p q (h s) -> p q h s", h=HQ)
                    mx = sa["mx"][:, k % 2, :].rearrange("p (q h) -> p q h", q=2)
                    ch(nc.vector.tensor_reduce(mx, s, AX.X, ALU.max))
                    if not (first and k < 2):
                        dve.wait_ge(N_[L, "prT_done"], 2 * (n - 2) + 2)
                    nc.vector.tensor_tensor(
                        out=sa["pr"][:, k % 2].rearrange("p (q h) s -> p q h s", q=2), in0=s,
                        in1=mx.unsqueeze(3).broadcast_to([P, 2, HQ, CTX]), op=ALU.subtract)\
                        .then_inc(N_[L, "shifted"], 1)
                if k < TPB and not last:
                    if L == "a" and k == 0:
                        dve.wait_ge(s_x, 16)
                    tile_stats(ch, stat, TPB * (b + 1) + k, k)
                if k == TPB - 1 and not last:
                    tiles_rstd(ch, stat, mean, rstd)
                if (k + 1) % 8 < GT and not (last and k + 1 >= 8):
                    norm_tile(b, (k + 1) // 8 + 1, (k + 1) % 8)
                if k % 2 == 1 and not (first and k < 7):
                    T = TPB * b + (k - 7) // 2
                    dve.wait_ge(N_[L, "x_updated"], T + 1)
                    tile_stats(ch, stat_all, T, T)

            if L == "a":
                dve.wait_ge(s_x0, 16)
            else:
                dve.wait_ge(N_["g", "x_updated"], NT)
            for T in range(TPB):
                tile_stats(ch, stat, T, T)
            tiles_rstd(ch, stat, mean, rstd)
            for i in range(GT):
                norm_tile(0, 0, i)
            norm_tile(0, 1, 0)
            bodies(dve, step, ch, per=2 * STEPS + TPB + LN_CHAIN)
            ch.wait()

        def xattn_pool(pool, L):
            if L == "a":
                with pool.Fori(0, NT) as T:
                    pool.wait_ge(N_["a", "y_ready"], T + 1)
                    nc.gpsimd.tensor_tensor(out=x[:, T, :], in0=x[:, T, :], in1=bo_bc[:], op=ALU.add)\
                        .then_inc(N_["a", "x_biased"], 1)
            else:
                with pool.Fori(0, NT // 2) as t2:
                    for u in range(2):
                        pool.wait_ge(N_["c", "o_ready"], 4 * t2 + 2 * u + 2)
                        nc.gpsimd.tensor_tensor(out=x[:, 2 * t2 + u, :], in0=x[:, 2 * t2 + u, :],
                                                in1=sa["o"][:, u, :], op=ALU.add).then_inc(N_["c", "x_updated"], 1)

        def route_sync(sp):
            sp.dma_start(nodew[:], ffn["node_w"].rearrange("(c p) n -> p c n", p=P)).then_inc(s_node, 16)
            sp.dma_start(nodeb[:], ffn["node_b"].partition_broadcast(P)).then_inc(s_node, 16)
            sp.dma_start(routerw[:], moe["router_w"].rearrange("(c p) n -> p c n", p=P)).then_inc(s_node, 16)
            sp.dma_start(routerb[:], moe["router_b"].partition_broadcast(P)).then_inc(s_node, 16)
            sp.wait_ge(s_zeros, 1)
            rows = zq[:, 0:ZR, :]
            n = P * ZR
            for buf in (*sorted_in, slots_in[0:SLOT_FILL, :]):
                for i in range(buf.shape[0] // n):
                    sp.dma_start(buf[i * n:(i + 1) * n, :].rearrange("(p r) d -> p r d", p=P), rows)\
                        .then_inc(s_zfill, 16)
        N_ZFILL = 16 * (3 * SET_ROWS + SLOT_FILL) // (P * ZR)

        def consts_pool(pool, ch):
            nc.gpsimd.memset(zq[:, 0:ZR, :], 0.0).then_inc(s_zeros, 1)
            ch(nc.gpsimd.memset(tri[:], 1.0))
            ch(nc.gpsimd.affine_select(out=tri[:], in_=tri[:], compare_op=ALU.is_ge, fill=0.0, base=0,
                                       pattern=[[1, P]], channel_multiplier=-1))
            ch(nc.gpsimd.memset(ones_bf[:], 1.0))
            ch(nc.gpsimd.memset(before[:, 0, :], 0.0))
            ch(nc.gpsimd.memset(ones_row[:], 1.0))
            for s in range(3):
                ch(nc.gpsimd.memset(set_leaf0[:, s, :], float(s % 2 * LEAVES)))
            ch(nc.gpsimd.iota(tile_row[:], pattern=[[P, SET_TILES]], base=0, channel_multiplier=0,
                              allow_small_or_imprecise_dtypes=True))
            ch(nc.gpsimd.memset(scan_on[:], 1.0))
            ch(nc.gpsimd.memset(scan_on[:, :, 0:1], 0.0))
            ch(nc.gpsimd.iota(expert_id[:], pattern=[[1, EXPERTS]], base=0, channel_multiplier=0,
                              allow_small_or_imprecise_dtypes=True))
            nc.gpsimd.iota(trash[:], pattern=[[P * TOPK * TPB, B], [P, TOPK * TPB]], base=ROW_TRASH, channel_multiplier=1,
                           allow_small_or_imprecise_dtypes=True).then_inc(s_tables, 1)

        def transposed_z(pe, L, T, k):
            for c in range(DC):
                m = nc.tensor.transpose(psT[:, k % 2, c * P:(c + 1) * P], zq[:, T, c * P:(c + 1) * P], ident[:])
            m.then_inc(N_[L, "zT_done"], 1)

        def score_bank(b):
            return (psO, psM)[b % 2]

        def route_pe(pe, L, w, width, after):
            def scores(b, k):
                T = TPB * b + k
                pe.wait_ge(N_[L, "zT_copied"], T + 1)
                if k == 0 and b >= 2:
                    pe.wait_ge(N_[L, "scores_used"], b - 1)
                for c in range(DC):
                    m = nc.tensor.matmul(score_bank(b)[:, k * width:(k + 1) * width], zT_of[L][:, k % 2, c, :], w[:, c, :],
                                         start=(c == 0), stop=(c == DC - 1))
                m.then_inc(N_[L, "node_done"], 1)

            pe.wait_ge(s_node, 64)
            for b in range(B):
                for k in range(TPB):
                    T = TPB * b + k
                    pe.wait_ge(N_[L, "z_ready"], T + 1)
                    if T >= 2:
                        pe.wait_ge(N_[L, "zT_copied"], T - 1)
                    transposed_z(pe, L, T, k)
                    if k:
                        scores(b, k - 1)
                scores(b, TPB - 1)
                if b:
                    after(b - 1)
            after(B - 1)

        def route_act(act, L):
            def body(b, first):
                for k in range(TPB):
                    T = TPB * b + k
                    act.wait_ge(N_[L, "zT_done"], T + 1)
                    if not (first and k < 2):
                        act.wait_ge(N_[L, "node_done"], T - 1)
                    nc.scalar.copy(zT_of[L][:, k % 2], psT[:, k % 2, 0:D].rearrange("p (c t) -> p c t", c=DC))\
                        .then_inc(N_[L, "zT_copied"], 1)
            body(0, True)
            with act.Fori(1, B) as b:
                body(b, False)

        def route_norm(L, b):
            for T in range(TPB * b, TPB * (b + 1)):
                normalise(zq[:, T, :], T, mean_all[:, T:T + 1], rstd_all[:, T:T + 1]).then_inc(N_[L, "z_ready"], 1)

        def route_dve(ch, L, batch):
            tiles_rstd(ch, stat_all, mean_all, rstd_all)
            route_norm(L, 0)
            for b in range(B):
                if b + 1 < B:
                    route_norm(L, b + 1)
                batch(b)

        def tree_dve(dve):
            ch = Link(dve, N_["b", "chain"])
            dve.wait_ge(s_node, 64)
            dve.wait_ge(s_zfill, N_ZFILL)
            dve.wait_ge(N_["a", "x_updated"], NT)
            dve.wait_ge(s_tables, 1)
            ch(nc.vector.tensor_scalar(nodeb[:], nodeb[:], -1.0, None, ALU.mult))

            def batch(b):
                dve.wait_ge(N_["b", "node_done"], TPB * (b + 1))
                i = nc.vector.tensor_tensor(
                    out=bits[:].rearrange("p (t n) -> p t n", t=TPB),
                    in0=score_bank(b)[:, 0:TPB * NODES3].rearrange("p (t n) -> p t n", t=TPB),
                    in1=nodeb[:].unsqueeze(1).broadcast_to([P, TPB, NODES3]), op=ALU.is_ge)
                i.then_inc(N_["b", "scores_used"], 1)
                dve.wait_ge(N_["b", "scores_used"], b + 1)
                bv = bits[:].rearrange("p (m n) -> p m n", n=NODES)
                p1 = path[0][:]
                ch.count(nc.vector.tensor_scalar(p1[:, :, 0], bv[:, :, 0], -1.0, 1.0, ALU.mult, ALU.add))
                ch(nc.vector.tensor_scalar(p1[:, :, 1], bv[:, :, 0], 1.0, None, ALU.mult))
                for l in range(1, DEPTH):
                    w = 2 ** l
                    src = path[l - 1][:]
                    if l < DEPTH - 1:
                        dst = path[l][:].rearrange("p m (w two) -> p m w two", two=2)
                    else:
                        dst = onehot[:, b * TPB:(b + 1) * TPB, :].rearrange("p t (m w two) -> p (t m) w two", m=3, two=2)
                    ch(nc.vector.tensor_tensor(out=dst[:, :, :, 1], in0=src, in1=bv[:, :, w - 1:2 * w - 1], op=ALU.mult))
                    ch(nc.vector.tensor_tensor(out=dst[:, :, :, 0], in0=src, in1=dst[:, :, :, 1], op=ALU.subtract))
                for T in range(TPB * b, TPB * (b + 1)):
                    i = nc.vector.tensor_tensor(out=before[:, T + 1, :], in0=before[:, T, :], in1=onehot[:, T, :], op=ALU.add)
                    i.then_inc(s_before, 1)
                    dve.wait_ge(s_before, T + 1)
            route_dve(ch, "b", batch)
            dve.wait_ge(N_["b", "rank_done"], 1)
            ch(nc.vector.tensor_scalar(cnt_i[:], psO[:, 0:LEAVES3], float(P - 1), None, ALU.add))
            ch(nc.vector.tensor_scalar(cnt_i[:], cnt_i[:], 7, 7, ALU.arith_shift_right, ALU.logical_shift_left))
            ch(nc.vector.tensor_copy(padded[:], cnt_i[:]))
            for s in range(3):
                r = slice(s * LEAVES, (s + 1) * LEAVES)
                ch(nc.vector.tensor_tensor_scan(incl[:, r], ones_row[:, 0:LEAVES], padded[:, r], 0.0, ALU.mult, ALU.add))
            ch(nc.vector.tensor_tensor(out=base[:], in0=incl[:], in1=padded[:], op=ALU.subtract))
            ch(nc.vector.tensor_scalar(base[:], base[:], -1.0, None, ALU.add))
            for b in range(B):
                dve.wait_ge(N_["b", "rank_done"], 2 + b)
                r = psS[:, b // 2, b % 2, 0:TPB * LEAVES3].rearrange("p (t m) -> p t m", t=TPB)
                ch(nc.vector.tensor_tensor(out=rowt[:], in0=r, in1=base[:].unsqueeze(1).broadcast_to([P, TPB, LEAVES3]),
                                           op=ALU.add))
                ch(nc.vector.tensor_tensor(out=rowt[:], in0=rowt[:], in1=onehot[:, b * TPB:(b + 1) * TPB, :], op=ALU.mult))
                ch(nc.vector.tensor_reduce(rowf[:], rowt[:].rearrange("p t (s l) -> p s t l", s=3), AX.X, ALU.add))
                nc.vector.tensor_copy(row_i[:, :, b * TPB:(b + 1) * TPB], rowf[:]).then_inc(s_rows, 1)
            ch(nc.vector.tensor_tensor(
                out=ends[:], in0=incl[0:1].rearrange("p (s l) -> p s l", s=3).unsqueeze(2).broadcast_to([1, 3, SET_TILES, LEAVES]),
                in1=tile_row[:].unsqueeze(1).unsqueeze(3).broadcast_to([1, 3, SET_TILES, LEAVES]), op=ALU.is_le))
            ch(nc.vector.tensor_reduce(leaff[:], ends[:], AX.X, ALU.add))
            ch(nc.vector.tensor_scalar(leaff[:], leaff[:], float(LEAVES - 1), None, ALU.min))
            nc.vector.tensor_tensor(out=leaf_i[:].rearrange("p (s t) -> p s t", s=3), in0=leaff[:],
                                    in1=set_leaf0[:], op=ALU.add).then_inc(s_leaf, 1)

        def rank_pe(pe):
            pe.wait_ge(s_before, NT)
            nc.tensor.matmul(psO[:, 0:LEAVES3], ones_bf[:], before[:, NT, :], start=True, stop=True)\
                .then_inc(N_["b", "rank_done"], 1)
            for b in range(B):
                o = psS[:, b // 2, b % 2, 0:TPB * LEAVES3]
                r = slice(b * TPB, (b + 1) * TPB)
                nc.tensor.matmul(o, tri[:], onehot[:, r, :].rearrange("p t m -> p (t m)"), start=True, stop=False)
                nc.tensor.matmul(o, ones_bf[:], before[:, r, :].rearrange("p t m -> p (t m)"), start=False, stop=True)\
                    .then_inc(N_["b", "rank_done"], 1)

        def scatter_pool(pool):
            pool.wait_ge(s_zfill, N_ZFILL)
            pool.wait_ge(N_["b", "z_ready"], NT)
            for s in range(3):
                for T in range(NT):
                    if s == 0 and T % TPB == 0:
                        pool.wait_ge(s_rows, T // TPB + 1)
                    nc.gpsimd.indirect_dma_start(
                        out=sorted_in[s][:, :], out_offset=bass.IndirectOffsetOnAxis(ap=row_i[:, s, T:T + 1], axis=0),
                        in_=zq[:, T, :], in_offset=None).then_inc(s_scat[s], 16)

        def gather(pool, dst, s, T, done):
            nc.gpsimd.indirect_dma_start(
                out=dst, out_offset=None, in_=sorted_out[s][:, :],
                in_offset=bass.IndirectOffsetOnAxis(ap=row_i[:, s, T:T + 1], axis=0)).then_inc(done, 16)

        def gather_pool(pool):
            for s in range(3):
                pool.wait_ge(s_scat[s], 16 * NT)

            def rows_stored(s):
                for g in range(FS // GB):
                    pool.wait_ge(s_ystore[g], 16 * IT_SET * (s + 1))

            def query(b, k):
                gather(pool, zq[:, k, :], 0, b * TPB + k, s_qgath)

            def key(b, k):
                gather(pool, kg[:, k, :], 1, b * TPB + k, s_kgath)

            def values(b):
                for k in range(TPB):
                    gather(pool, vg[:, b % 2, k, :], 2, b * TPB + k, s_vgath)

            rows_stored(0)
            for k in range(TPB):
                query(0, k)
            rows_stored(1)
            for k in range(TPB):
                key(0, k)
            rows_stored(2)
            pool.wait_ge(N_["f", "y_done"], 3 * SET_TILES)
            values(0)
            for k in range(TPB):
                pool.wait_ge(N_["g", "tr_done"], k + 1)
                key(1, k)
            pool.wait_ge(s_vgath, 16 * TPB)
            values(1)
            for b in range(B - 1):
                for k in range(TPB):
                    pool.wait_ge(N_["g", "tr_done"], TPB + 1 + 2 * (TPB * b + k) + 1)
                    if b + 2 < B:
                        key(b + 2, k)
                    query(b + 1, k)
                if b + 2 < B:
                    pool.wait_ge(N_["g", "pv_done"], TPB * (b + 1))
                    pool.wait_ge(s_vgath, 16 * TPB * (b + 2))
                    values(b + 2)

        def leaf_weights_sync(sp, s):
            r = slice(s * LEAVES, (s + 1) * LEAVES)
            sp.dma_start(w1_all[:, s % 2], ffn["w1b"][r].rearrange("l p n -> p l n")).then_inc(s_leafw[s], 16)
            sp.dma_start(w2_all[:, s % 2], ffn["w2b"][r].rearrange("l p n -> p l n")).then_inc(s_leafw[s], 16)

        def ffn_sync(sp):
            def rows(buf, it, g):
                return buf[bass.ds((it * FS + g * GB) * P, GB * P), :].rearrange("(u p) d -> p u d", p=P)

            def load(s, it, g):
                sp.dma_start(zt[:, g * GB:(g + 1) * GB, :], rows(sorted_in[s], it, g)).then_inc(s_zload[g], 16)

            def store(s, it, g):
                sp.wait_ge(N_["f", "y_copied"], s * SET_TILES + (it * FS + (g + 1) * GB))
                sp.dma_start(rows(sorted_out[s], it, g), yt[:, g * GB:(g + 1) * GB, :]).then_inc(s_ystore[g], 16)

            sp.wait_ge(N_["a", "x_updated"], NT)
            leaf_weights_sync(sp, 0)
            leaf_weights_sync(sp, 1)
            sp.wait_ge(s_leaf, 1)
            for s in range(3):
                sp.wait_ge(s_leafw[s], 32)
                sp.wait_ge(s_scat[s], 16 * NT)
                for g in range(FS // GB):
                    if s:
                        sp.wait_ge(N_["f", "zT_done"], s * SET_TILES - FS + (g + 1) * GB)
                    load(s, 0, g)
                    if s:
                        store(s - 1, IT_SET - 1, g)
                if s == 1:
                    leaf_weights_sync(sp, 2)
                with sp.Fori(1, IT_SET) as it:
                    for g in range(FS // GB):
                        sp.wait_ge(N_["f", "zT_done"], it * FS + (s * SET_TILES - FS + (g + 1) * GB))
                        load(s, it, g)
                        store(s, it - 1, g)
            for g in range(FS // GB):
                store(2, IT_SET - 1, g)

        def ffn_turns(eng, step):
            for it in range(2):
                for u in range(FS):
                    step(it, u, it == 0, False)
            with eng.Fori(2, 3 * IT_SET - 1) as it:
                for u in range(FS):
                    step(it, u, False, False)
            for u in range(FS + 2):
                step(3 * IT_SET - 1, u, False, True)

        def ffn_pe(pe):
            def step(it, u, first, last):
                i = it * FS + u
                if u < FS:
                    if u % GB == 0:
                        pe.wait_ge(s_zload[u // GB], 16 * (it + 1))
                    if not (first and u < 2):
                        pe.wait_ge(N_["f", "zT_copied"], i - 1)
                    for c in range(DC):
                        m = nc.tensor.transpose(psT[:, u % 2, c * P:(c + 1) * P], zt[:, u, c * P:(c + 1) * P], ident[:])
                    m.then_inc(N_["f", "zT_done"], 1)
                if u - 1 < FS and not (first and u < 1):
                    v = (u - 1) % WS
                    pe.wait_ge(N_["f", "w_copied"], i)
                    if not (first and u < 3):
                        pe.wait_ge(N_["f", "h_copied"], i - 2)
                    for c in range(DC):
                        m = nc.tensor.matmul(psS[0:LEAF_W, 0, (u - 1) % 2, 0:P], w1s[:, v, c * LEAF_W:(c + 1) * LEAF_W],
                                             zT[:, (u - 1) % 2, c, :], start=(c == 0), stop=(c == DC - 1))
                    m.then_inc(N_["f", "h_done"], 1)
                if u - 2 < FS and not (first and u < 2):
                    v = (u - 2) % WS
                    pe.wait_ge(N_["f", "h_copied"], i - 1)
                    if not (first and u < 4):
                        pe.wait_ge(N_["f", "y_copied"], i - 3)
                    nc.tensor.matmul(psS[:, 1, u % 2, 0:D], hT[:, u % 2, :], w2s[:, v, :], start=True, stop=True)\
                        .then_inc(N_["f", "y_done"], 1)
            ffn_turns(pe, step)

        def ffn_act(act):
            def step(it, u, first, last):
                i = it * FS + u
                if u < FS:
                    act.wait_ge(N_["f", "zT_done"], i + 1)
                    if not (first and u < 2):
                        act.wait_ge(N_["f", "h_done"], i - 1)
                    nc.scalar.copy(zT[:, u % 2], psT[:, u % 2, 0:D].rearrange("p (c t) -> p c t", c=DC))\
                        .then_inc(N_["f", "zT_copied"], 1)
                    if not (first and u < WS):
                        act.wait_ge(N_["f", "y_done"], i - WS + 1)
                    r = act.value_load(leaf_i[0:1, bass.ds(i, 1)], min_val=0, max_val=2 * LEAVES - 1)
                    nc.scalar.copy(w1s[:, u % WS, :], w1_of[:, bass.ds(r, 1), :].rearrange("p o n -> p (o n)"))
                    nc.scalar.copy(w2s[:, u % WS, :], w2_of[:, bass.ds(r, 1), :].rearrange("p o n -> p (o n)"))\
                        .then_inc(N_["f", "w_copied"], 1)
            w1_of = w1_all[:].rearrange("p s l n -> p (s l) n")
            w2_of = w2_all[:].rearrange("p s l n -> p (s l) n")
            act.wait_ge(s_leaf, 1)
            ffn_turns(act, step)

        def ffn_dve(dve):
            def step(it, u, first, last):
                i = it * FS + u
                if u - 1 < FS and not (first and u < 1):
                    v = (u - 1) % WS
                    dve.wait_ge(N_["f", "h_done"], i)
                    if not (first and u < 3):
                        dve.wait_ge(N_["f", "y_done"], i - 2)
                    nc.vector.tensor_scalar(hT[0:LEAF_W, (u - 1) % 2, :], psS[0:LEAF_W, 0, (u - 1) % 2, 0:P],
                                            w1s[0:LEAF_W, v, DC * LEAF_W:DC * LEAF_W + 1], 0.0, ALU.add, ALU.max)\
                        .then_inc(N_["f", "h_copied"], 1)
                if u - 2 < FS and not (first and u < 2):
                    v = (u - 2) % FS
                    dve.wait_ge(N_["f", "y_done"], i - 1)
                    n = it if u >= 2 else it - 1
                    if not (isinstance(n, int) and n == 0):
                        dve.wait_ge(s_ystore[v // GB], 16 * n)
                    nc.vector.tensor_copy(yt[:, v, :], psS[:, 1, u % 2, 0:D]).then_inc(N_["f", "y_copied"], 1)
            nc.vector.memset(hT[LEAF_W:LEAF_W + 1, :, :], 1.0)
            ffn_turns(dve, step)

        def sa_bodies(eng, step, chain=None, per=0):
            for k in range(TPB):
                step(0, k, True, False)
            done = chain.base + chain.n if chain else 0
            with eng.Fori(1, B - 1) as b:
                if chain:
                    chain.restart(b * per + (done - per))
                for k in range(TPB):
                    step(b, k, False, False)
                assert not chain or chain.n == per
            if chain:
                chain.restart(done + (B - 2) * per)
            for k in range(TPB + 2):
                step(B - 1, k, False, True)

        def sa_pe(pe):
            def transpose_tile(src, count_free):
                if count_free is not None:
                    pe.wait_ge(N_["g", "tr_copied"], count_free)
                for c in range(DC):
                    m = nc.tensor.transpose(psM[:, c * P:(c + 1) * P], src[:, c * P:(c + 1) * P], ident[:])
                m.then_inc(N_["g", "tr_done"], 1)

            def step(b, k, first, last):
                n = TPB * b + k
                if k < TPB:
                    pe.wait_ge(N_["g", "tr_copied"], 2 * n + TPB + 1)
                    if not (first and k < 2):
                        pe.wait_ge(N_["g", "exp_done"], n - 1)
                    for h in range(2):
                        for c in range(DC):
                            m = nc.tensor.matmul(psS[:, k % 2, h, :], qTs[:, k % 2, c, :],
                                                 kTs[:, b % 2, c, h * 512:(h + 1) * 512],
                                                 start=(c == 0), stop=(c == DC - 1))
                    m.then_inc(N_["g", "scores_done"], 1)
                    if k == 0 and not last:
                        pe.wait_ge(s_kgath, 16 * TPB * (b + 2))
                    transpose_tile(kg[:, k, :], 2 * n + TPB + 1)
                    if not (last and k == TPB - 1):
                        if k == TPB - 1:
                            pe.wait_ge(s_qgath, 16 * TPB * (b + 2))
                        transpose_tile(zq[:, (k + 1) % TPB, :], 2 * n + TPB + 2)
                if k - 1 < TPB and not (first and k < 1):
                    pe.wait_ge(N_["g", "exp_done"], n)
                    for h in range(2):
                        if not (first and k < 2):
                            pe.wait_ge(N_["g", "pT_copied"], 2 * (n - 2) + h + 1)
                        for q in range(4):
                            m = nc.tensor.transpose(psT[:, h, q * P:(q + 1) * P],
                                                    pg[:, (k - 1) % 2, (4 * h + q) * P:(4 * h + q + 1) * P], ident[:])
                        m.then_inc(N_["g", "pT_done"], 1)
                if k - 2 < TPB and not (first and k < 2):
                    pe.wait_ge(N_["g", "pT_copied"], 2 * (n - 2) + 2)
                    if not (first and k < 3):
                        pe.wait_ge(N_["g", "x_updated"], n - 2)
                    bb = b if k >= 2 else b - 1
                    if k == 2:
                        pe.wait_ge(s_vgath, 16 * TPB * (b + 1))
                    for q in range(8):
                        m = nc.tensor.matmul(psO[:, 0:D], pgT[:, k % 2, q, :], vg[:, bb % 2, q, :],
                                             start=(q == 0), stop=(q == 7))
                    m.then_inc(N_["g", "pv_done"], 1)

            pe.wait_ge(s_kgath, 16 * TPB)
            pe.wait_ge(s_qgath, 16 * TPB)
            for k in range(TPB):
                transpose_tile(kg[:, k, :], k if k else None)
            transpose_tile(zq[:, 0, :], TPB)
            sa_bodies(pe, step)

        def sa_act(act):
            def copy_key(b, k, n):
                act.wait_ge(N_["g", "tr_done"], n)
                nc.scalar.copy(kTs[:, b % 2, :, k * P:(k + 1) * P],
                               psM[:, 0:D].rearrange("p (c t) -> p c t", c=DC)).then_inc(N_["g", "tr_copied"], 1)

            def copy_query(par, n):
                act.wait_ge(N_["g", "tr_done"], n)
                nc.scalar.copy(qTs[:, par], psM[:, 0:D].rearrange("p (c t) -> p c t", c=DC))\
                    .then_inc(N_["g", "tr_copied"], 1)

            def step(b, k, first, last):
                n = TPB * b + k
                if k - 1 < TPB and not (first and k < 1):
                    act.wait_ge(N_["g", "bias_ready"], n)
                    if not (first and k < 3):
                        act.wait_ge(N_["g", "pT_done"], 2 * (n - 3) + 2)
                    nc.scalar.activation(pg[:, (k - 1) % 2, :], psS[:, (k - 1) % 2].rearrange("p h s -> p (h s)"),
                                         ACT.Exp, bias=nmax[:, (k - 1) % 2:(k - 1) % 2 + 1], scale=SA_SCALE,
                                         accum_out=psum_exp[:, (k - 1) % 4:(k - 1) % 4 + 1])\
                        .then_inc(N_["g", "exp_done"], 1)
                if k < TPB:
                    copy_key(b + 1, k, 2 * n + TPB + 2)
                    if not (last and k == TPB - 1):
                        copy_query((k + 1) % 2, 2 * n + TPB + 3)
                if k - 1 < TPB and not (first and k < 1):
                    if not (first and k < 3):
                        act.wait_ge(N_["g", "pv_done"], n - 2)
                    for h in range(2):
                        act.wait_ge(N_["g", "pT_done"], 2 * (n - 1) + h + 1)
                        nc.scalar.copy(pgT[:, (k - 1) % 2, 4 * h:4 * h + 4, :],
                                       psT[:, h, :].rearrange("p (q t) -> p q t", q=4)).then_inc(N_["g", "pT_copied"], 1)

            for k in range(TPB):
                copy_key(0, k, k + 1)
            copy_query(0, TPB + 1)
            sa_bodies(act, step)

        def sa_dve(dve):
            ch = Link(dve, N_["g", "chain"])

            def step(b, k, first, last):
                n = TPB * b + k
                if k < TPB:
                    dve.wait_ge(N_["g", "scores_done"], n + 1)
                    par = k % 2
                    ch(nc.vector.tensor_reduce(smax[:, par:par + 1], psS[:, par].rearrange("p h s -> p (h s)"),
                                               AX.X, ALU.max))
                    if not (first and k < 2):
                        dve.wait_ge(N_["g", "exp_done"], n - 1)
                    nc.vector.tensor_scalar(nmax[:, par:par + 1], smax[:, par:par + 1], -SA_SCALE, None, ALU.mult)\
                        .then_inc(N_["g", "bias_ready"], 1)
                if k - 2 < TPB and not (first and k < 2):
                    T = TPB * b + k - 2
                    dve.wait_ge(N_["g", "pv_done"], n - 1)
                    ch(nc.vector.reciprocal(rsum[:, k % 2:k % 2 + 1], psum_exp[:, (k - 2) % 4:(k - 2) % 4 + 1]))
                    nc.vector.scalar_tensor_tensor(x[:, T, :], psO[:, 0:D], rsum[:, k % 2:k % 2 + 1], x[:, T, :],
                                                   ALU.mult, ALU.add).then_inc(N_["g", "x_updated"], 1)
            sa_bodies(dve, step, ch, per=2 * TPB)

        def topk_pe(pe, b):
            pe.wait_ge(s_ohs, b + 1)
            o = psS[:, b // 2, b % 2, 0:EXPERTS * TOPK * TPB]
            nc.tensor.matmul(o, tri[:], ohs[:, b].rearrange("p e q -> p (e q)"), start=True, stop=False)
            nc.tensor.matmul(o, ones_bf[:], ohb[:, b].rearrange("p e q -> p (e q)"), start=False, stop=True)\
                .then_inc(s_xrank, 1)

        def topk_act(act):
            act.wait_ge(s_gap, B)
            nc.scalar.activation(prob[:, 1, :], prob[:, 1, :], ACT.Exp).then_inc(s_gexp, 1)

        def topk_dve(dve):
            ch = Link(dve, N_["d", "chain"])
            dve.wait_ge(N_["c", "x_updated"], NT)
            dve.wait_ge(s_node, 16 * 4)

            def batch(b):
                tiles = slice(TPB * b, TPB * (b + 1))
                dve.wait_ge(N_["d", "node_done"], TPB * (b + 1))
                nc.vector.tensor_tensor(
                    out=logit[:, tiles, :],
                    in0=score_bank(b)[:, 0:TPB * EXPERTS].rearrange("p (t e) -> p t e", t=TPB),
                    in1=routerb[:].unsqueeze(1).broadcast_to([P, TPB, EXPERTS]), op=ALU.add)\
                    .then_inc(N_["d", "scores_used"], 1)
                dve.wait_ge(N_["d", "scores_used"], b + 1)
                for T in range(TPB * b, TPB * (b + 1)):
                    ch.count(nc.vector.max(best[:, T, :], logit[:, T, :]))
                ch.wait()
                for T in range(TPB * b, TPB * (b + 1)):
                    ch.count(nc.vector.max_index(best_i[:, T, :], best[:, T, :], logit[:, T, :]))
                nc.vector.tensor_tensor(out=prob[:, 1, tiles], in0=best[:, tiles, 1], in1=best[:, tiles, 0], op=ALU.subtract)\
                    .then_inc(s_gap, 1)
                ch.wait()
                ch(nc.vector.tensor_copy(choice[:, tiles, :], best_i[:, tiles, 0:TOPK]))
                for k in range(TOPK):
                    ch.count(nc.vector.tensor_tensor(
                        out=ohs[:, b, :, k * TPB:(k + 1) * TPB],
                        in0=choice[:, tiles, k].unsqueeze(1).broadcast_to([P, EXPERTS, TPB]),
                        in1=expert_id[:].unsqueeze(2).broadcast_to([P, EXPERTS, TPB]), op=ALU.is_equal))
                ch.wait()
                ch(nc.vector.tensor_tensor_scan(upto[:].rearrange("p e q -> p (e q)"), scan_on[:].rearrange("p e q -> p (e q)"),
                                                ohs[:, b].rearrange("p e q -> p (e q)"), 0.0, ALU.mult, ALU.add))
                nc.vector.tensor_tensor(out=ohb[:, b], in0=upto[:], in1=ohs[:, b], op=ALU.subtract).then_inc(s_ohs, 1)
                for k in range(TOPK):
                    ch.count(nc.vector.tensor_scalar(xrow[:, k * TPB:(k + 1) * TPB], choice[:, tiles, k],
                                                     float(SLOTS), float(b * CAP - 1), ALU.mult, ALU.add))
                dve.wait_ge(s_xrank, b + 1)
                ch(nc.vector.tensor_tensor(
                    out=rankt[:], in0=psS[:, b // 2, b % 2, 0:EXPERTS * TOPK * TPB].rearrange("p (e q) -> p e q", e=EXPERTS),
                    in1=ohs[:, b], op=ALU.mult))
                ch(nc.vector.tensor_reduce(rankf[:], rankt[:].rearrange("p e q -> p q e"), AX.X, ALU.add))
                ch(nc.vector.scalar_tensor_tensor(xrow[:], rankf[:], float(CAP), xrow[:], ALU.min, ALU.add))
                nc.vector.tensor_copy(read_i[:, b, :], xrow[:]).then_inc(s_rows, 1)
                ch(nc.vector.tensor_scalar(rankf[:], rankf[:], float(CAP), None, ALU.is_le))
                ch(nc.vector.tensor_tensor(out=xrow[:], in0=xrow[:], in1=trash[:, b, :], op=ALU.subtract))
                ch(nc.vector.tensor_tensor(out=xrow[:], in0=xrow[:], in1=rankf[:], op=ALU.mult))
                nc.vector.tensor_tensor(out=write_i[:, b, :], in0=xrow[:], in1=trash[:, b, :], op=ALU.add).then_inc(s_rows, 1)
            route_dve(ch, "d", batch)
            dve.wait_ge(s_gexp, 1)
            ch(nc.vector.tensor_scalar(prob[:, 0, :], prob[:, 1, :], 1.0, None, ALU.add))
            ch(nc.vector.reciprocal(prob[:, 0, :], prob[:, 0, :]))
            ch(nc.vector.tensor_tensor(out=prob[:, 1, :], in0=prob[:, 1, :], in1=prob[:, 0, :], op=ALU.mult))

        def dispatch_pool(pool):
            for b in range(B):
                pool.wait_ge(s_rows, B + 2 * (b + 1))
                for k in range(TOPK):
                    for t in range(TPB):
                        nc.gpsimd.indirect_dma_start(
                            out=slots_in[:, :],
                            out_offset=bass.IndirectOffsetOnAxis(ap=write_i[:, b, k * TPB + t:k * TPB + t + 1], axis=0),
                            in_=zq[:, b * TPB + t, :], in_offset=None).then_inc(s_disp, 16)

        EP = EXPERTS // 2
        ROWT = -(-SLOTS // P)
        BLOCKS = [(c, min(512, SLOTS - c)) for c in range(0, SLOTS, 512)]
        HCH = HID // P

        def rows_of(i):
            return min(P, SLOTS - i * P)

        def turns(eng, body):
            body(0, True, False)
            with eng.Fori(1, EP - 1) as t:
                body(t, False, False)
            body(EP - 1, False, True)

        def moe_sync(sp):
            def load(e, q):
                sp.dma_start(wc[:, q], moe["w_c"][e].rearrange("(c p) h -> p c h", p=P)).then_inc(s_wload[q], 16)
                sp.dma_start(wg[:, q], moe["w_g"][e].rearrange("(c p) h -> p c h", p=P)).then_inc(s_wload[q], 16)
                sp.dma_start(bcg[:, q], moe["b_cg"][e]).then_inc(s_wload[q], 16)
                sp.dma_start(wp[:, q], moe["w_p"][e].rearrange("(m p) n -> p m n", p=P)).then_inc(s_wload[q], 16)
                sp.dma_start(bp[:, q], moe["b_p"][e].partition_broadcast(P)).then_inc(s_wload[q], 16)

            def load_x(e, q):
                n = (ROWT - 1) * P
                sp.dma_start(xr[:, q, 0:ROWT - 1, :], slots_in[bass.ds(e * SLOTS, n), :].rearrange("(i p) d -> p i d", p=P))\
                    .then_inc(s_xload[q], 16)
                sp.dma_start(xr[0:SLOTS - n, q, ROWT - 1, :], slots_in[bass.ds(e * SLOTS + n, SLOTS - n), :])\
                    .then_inc(s_xload[q], 16)

            sp.wait_ge(N_["c", "x_updated"], NT)
            for q in range(2):
                load(q, q)
            sp.wait_ge(s_disp, 16 * TOPK * NT)
            for q in range(2):
                load_x(q, q)
            with sp.Fori(1, EP) as t:
                for q in range(2):
                    sp.wait_ge(N_["e", "o_copied"], t * (2 * ROWT) + (q - 1) * ROWT)
                    load(2 * t + q, q)
                    load_x(2 * t + q, q)

        def moe_pe(pe):
            NB = len(BLOCKS)

            def transposes(t, q, blk, first):
                if blk == 0:
                    pe.wait_ge(s_xload[q], 32 * (t + 1))
                for i in range(blk * 4, min(blk * 4 + 4, ROWT)):
                    n = t * (2 * ROWT) + (q * ROWT + i)
                    if not (first and n < 2):
                        pe.wait_ge(N_["e", "xT_copied"], n - 1)
                    r = rows_of(i)
                    for c in range(DC):
                        m = nc.tensor.transpose(psT[:, i % 2, c * P:c * P + r], xr[0:r, q, i, c * P:(c + 1) * P], ident[0:r, 0:r])
                    m.then_inc(N_["e", "xT_done"], 1)

            def outputs(t, q, blk, first):
                for i in range(blk * 4, min(blk * 4 + 4, ROWT)):
                    n = t * (2 * ROWT) + (q * ROWT + i)
                    r = rows_of(i)
                    if i == blk * 4:
                        pe.wait_ge(N_["e", "silu_done"], ((t * 2 + q) * NB + blk + 1) * HCH)
                    if not (first and n < 2):
                        pe.wait_ge(N_["e", "o_copied"], n - 1)
                    par = (q * NB + blk) % 2
                    po = (psO, psM)[i % 2]
                    for m_ in range(HCH):
                        m = nc.tensor.matmul(po[0:r, 0:D], st[:, par, m_, (i % 4) * P:(i % 4) * P + r], wp[:, q, m_, :],
                                             start=(m_ == 0), stop=(m_ == HCH - 1))
                    m.then_inc(N_["e", "o_done"], 1)

            def body(t, first, last):
                for q in range(2):
                    for blk, (c0, w) in enumerate(BLOCKS):
                        pos = q * NB + blk
                        par = pos % 2
                        if blk == 0:
                            pe.wait_ge(s_wload[q], 80 * (t + 1))
                        pe.wait_ge(N_["e", "xT_copied"], t * (2 * ROWT) + (q * ROWT + min(blk * 4 + 4, ROWT)))
                        for m_ in range(HCH):
                            n = (t * 2 * NB + pos) * HCH + m_
                            if not (first and pos == 0 and m_ < 2):
                                pe.wait_ge(N_["e", "gated"], n - 1)
                            for which, wt in enumerate((wc, wg)):
                                for c in range(DC):
                                    m = nc.tensor.matmul(psS[:, m_ % 2, which, 0:w], wt[:, q, c, m_ * P:(m_ + 1) * P],
                                                         xT[:, par, c, 0:w], start=(c == 0), stop=(c == DC - 1))
                                m.then_inc(N_["e", "hg_done"], 1)
                            if m_ == 1 and not (first and pos == 0):
                                pq, pblk = divmod(pos - 1, NB) if pos else (1, NB - 1)
                                outputs(t if pos else t - 1, pq, pblk, first)
                            if m_ == 4:
                                nq, nblk = divmod(pos + 1, NB)
                                if nq < 2:
                                    transposes(t, nq, nblk, first)
                                elif not last:
                                    transposes(t + 1, 0, 0, False)
                if last:
                    outputs(t, 1, NB - 1, False)

            pe.wait_ge(s_xload[0], 32)
            transposes(0, 0, 0, True)
            turns(pe, body)

        def moe_act(act):
            NB = len(BLOCKS)

            def copies(t, q, blk):
                for i in range(blk * 4, min(blk * 4 + 4, ROWT)):
                    n = t * (2 * ROWT) + (q * ROWT + i)
                    r = rows_of(i)
                    act.wait_ge(N_["e", "xT_done"], n + 1)
                    nc.scalar.copy(xT[:, (q * NB + blk) % 2, :, (i % 4) * P:(i % 4) * P + r],
                                   psT[:, i % 2, 0:DC * P].rearrange("p (c t) -> p c t", c=DC)[:, :, 0:r])\
                        .then_inc(N_["e", "xT_copied"], 1)

            def silu(n, par, m_, w, first):
                act.wait_ge(N_["e", "gated"], n + 1)
                nc.scalar.activation(st[:, par, m_, 0:w], hg[:, m_ % 2, 0:w], ACT.Silu).then_inc(N_["e", "silu_done"], 1)

            def body(t, first, last):
                for q in range(2):
                    for blk, (c0, w) in enumerate(BLOCKS):
                        pos = q * NB + blk
                        for m_ in range(HCH):
                            n = (t * 2 * NB + pos) * HCH + m_
                            act.wait_ge(N_["e", "hg_done"], 2 * n + 1)
                            if not (first and pos == 0 and m_ < 2):
                                act.wait_ge(N_["e", "gated"], n - 1)
                            nc.scalar.activation(hb[:, m_ % 2, 0:w], psS[:, m_ % 2, 0, 0:w], ACT.Identity,
                                                 bias=bcg[:, q, m_:m_ + 1]).then_inc(N_["e", "h_ready"], 1)
                            if m_ == 0:
                                if pos or not first:
                                    silu(n - 1, (pos + 1) % 2, HCH - 1, BLOCKS[(pos - 1) % NB][1], first)
                            else:
                                if m_ == 1 and not (first and pos < 2):
                                    a, b_ = divmod(pos - 2, NB) if pos >= 2 else (1, pos - 2 + NB)
                                    tt = t if pos >= 2 else t - 1
                                    act.wait_ge(N_["e", "o_done"], tt * (2 * ROWT) + (a * ROWT + min(b_ * 4 + 4, ROWT)))
                                silu(n - 1, pos % 2, m_ - 1, w, first)
                            if m_ == 4:
                                nq, nblk = divmod(pos + 1, NB)
                                if nq < 2:
                                    copies(t, nq, nblk)
                                elif not last:
                                    copies(t + 1, 0, 0)
                if last:
                    silu(EP * 2 * NB * HCH - 1, 1, HCH - 1, BLOCKS[NB - 1][1], False)

            copies(0, 0, 0)
            turns(act, body)

        def moe_dve(dve):
            NB = len(BLOCKS)

            def outputs(t, q, blk, first):
                for i in range(blk * 4, min(blk * 4 + 4, ROWT)):
                    n = t * (2 * ROWT) + (q * ROWT + i)
                    r = rows_of(i)
                    dve.wait_ge(N_["e", "o_done"], n + 1)
                    if not (first and n < YS):
                        k = (2 * t + q) * (ROWT // YS) + i // YS
                        dve.wait_ge(s_ostore[i % YS], k * 16)
                    nc.vector.tensor_tensor(out=yo[0:r, i % YS, :], in0=(psO, psM)[i % 2][0:r, 0:D], in1=bp[0:r, q, :],
                                            op=ALU.add).then_inc(N_["e", "o_copied"], 1)

            def body(t, first, last):
                for q in range(2):
                    for blk, (c0, w) in enumerate(BLOCKS):
                        pos = q * NB + blk
                        for m_ in range(HCH):
                            n = (t * 2 * NB + pos) * HCH + m_
                            dve.wait_ge(N_["e", "hg_done"], 2 * n + 2)
                            dve.wait_ge(N_["e", "h_ready"], n + 1)
                            if not (first and pos == 0 and m_ < 2):
                                dve.wait_ge(N_["e", "silu_done"], n - 1)
                            nc.vector.scalar_tensor_tensor(hg[:, m_ % 2, 0:w], psS[:, m_ % 2, 1, 0:w],
                                                           bcg[:, q, HCH + m_:HCH + m_ + 1], hb[:, m_ % 2, 0:w],
                                                           ALU.add, ALU.mult).then_inc(N_["e", "gated"], 1)
                            if m_ == 1 and not (first and pos == 0):
                                pq, pblk = divmod(pos - 1, NB) if pos else (1, NB - 1)
                                outputs(t if pos else t - 1, pq, pblk, first)
                if last:
                    outputs(t, 1, NB - 1, False)
            turns(dve, body)
            with dve.Fori(0, NT // GS) as g:
                for u in range(GS):
                    T = g * GS + u
                    dve.wait_ge(s_yload[u], 32 * (g + 1))
                    ch_fin = nc.vector.scalar_tensor_tensor(x[:, T, :], yg[:, u, 0, :], prob[:, 0, bass.ds(T, 1)], x[:, T, :],
                                                            ALU.mult, ALU.add)
                    ch_fin.then_inc(s_half, 1)
                    dve.wait_ge(s_half, T + 1)
                    nc.vector.scalar_tensor_tensor(x[:, T, :], yg[:, u, 1, :], prob[:, 1, bass.ds(T, 1)], x[:, T, :],
                                                   ALU.mult, ALU.add).then_inc(s_fin, 1)

        def moe_pool(pool):
            with pool.Fori(0, EXPERTS) as e:
                for i in range(ROWT):
                    r = rows_of(i)
                    pool.wait_ge(N_["e", "o_copied"], e * ROWT + i + 1)
                    pool.dma_start(slots_out[bass.ds(e * SLOTS + i * P, r), :], yo[0:r, i % YS, :])\
                        .then_inc(s_ostore[i % YS], 16)
            for u in range(YS):
                pool.wait_ge(s_ostore[u], 16 * EXPERTS * ROWT // YS)
            for T in range(NT):
                if T >= GS:
                    pool.wait_ge(s_fin, T - GS + 1)
                for k in range(TOPK):
                    nc.gpsimd.indirect_dma_start(
                        out=yg[:, T % GS, k, :], out_offset=None, in_=slots_out[:, :],
                        in_offset=bass.IndirectOffsetOnAxis(ap=read_i[:, T // TPB, k * TPB + T % TPB:k * TPB + T % TPB + 1], axis=0))\
                        .then_inc(s_yload[T % GS], 16)

        def final_sync(sp):
            with sp.Fori(0, NT // GS) as g:
                sp.wait_ge(s_fin, g * GS + GS)
                sp.dma_start(out_v[:, bass.ds(g * GS, GS), :], x[:, bass.ds(g * GS, GS), :]).then_inc(s_out, 16)
            sp.wait_ge(s_out, 16 * (NT // GS))

        block = es.enter_context(nc.Block())

        @block.sync
        def _(sp):
            prep_sync(sp)
            route_sync(sp)
            ffn_sync(sp)
            moe_sync(sp)
            final_sync(sp)

        @block.gpsimd
        def _(pool):
            prep_pool(pool)
            pool.wait_ge(s_w, 16 * N_W)
            xattn_pool(pool, "a")
            scatter_pool(pool)
            gather_pool(pool)
            xattn_pool(pool, "c")
            dispatch_pool(pool)
            moe_pool(pool)

        @block.scalar
        def _(act):
            prep_loads_act(act)
            prep_act(act)
            xattn_act(act, "a")
            route_act(act, "b")
            ffn_act(act)
            sa_act(act)
            xattn_act(act, "c")
            route_act(act, "d")
            topk_act(act)
            moe_act(act)

        @block.vector
        def _(dve):
            prep_dve(dve)
            xattn_dve(dve, "a")
            tree_dve(dve)
            ffn_dve(dve)
            sa_dve(dve)
            xattn_dve(dve, "c")
            topk_dve(dve)
            moe_dve(dve)

        @block.tensor
        def _(pe):
            prep_pe(pe)
            xattn_pe(pe, "a")
            route_pe(pe, "b", nodew, NODES3, lambda b: None)
            rank_pe(pe)
            ffn_pe(pe)
            sa_pe(pe)
            xattn_pe(pe, "c")
            route_pe(pe, "d", routerw, EXPERTS, lambda b: topk_pe(pe, b))
            moe_pe(pe)


def kernel(**inputs):
    import numpy as np
    import concourse.bacc as bacc
    from concourse.bass_utils import run_bass_kernel_spmd

    nc = bacc.Bacc("TRN2", target_bir_lowering=False, num_devices=1)
    arrays = {}

    def dram(name, a=None):
        a = np.ascontiguousarray(inputs[name] if a is None else a)
        arrays[f"in_{name}"] = a
        return nc.dram_tensor(f"in_{name}", a.shape, mybir.dt.from_np(a.dtype), kind="ExternalInput").ap()

    def weight(k, name, transposed=False):
        a = np.asarray(inputs[name])
        if transposed and k[0] == "w":
            a = a.T
        if k in ("bq", "bk"):
            a = a.reshape(DC, P).T
        return dram(name, a)

    xa = {
        "a": {k: weight(k, f"L0_xattn_{n}") for k, n in (("wq", "W_Q"), ("bq", "b_Q"), ("wk", "W_K"), ("bk", "b_K"),
                                                    ("wv", "W_V"), ("bv", "b_V"), ("wo", "W_O"), ("bo", "b_O"))},
        "c": {k: weight(k, f"L1_xattn_{n}", transposed=True)
              for k, n in (("wq", "q_w"), ("bq", "q_b"), ("wk", "k_w"), ("bk", "k_b"), ("wv", "v_w"), ("bv", "v_b"))},
    }
    trees = [{k: np.asarray(inputs[f"L0_ffn_{t}_{k}"]) for k in ("node_w", "node_b", "w1", "b1", "w2", "b2")} for t in "qkv"]

    def leaf_in(t):
        w = t["w1"].reshape(LEAVES, DC, P, LEAF_W).transpose(0, 2, 1, 3).reshape(LEAVES, P, DC * LEAF_W)
        b = np.zeros((LEAVES, P, 2), w.dtype)
        b[:, 0:LEAF_W, 0] = t["b1"]
        return np.concatenate([w, b], axis=2)

    ffn = {
        "node_w": dram("ffn_node_w", np.concatenate([t["node_w"] for t in trees]).T),
        "node_b": dram("ffn_node_b", np.concatenate([t["node_b"] for t in trees])),
        "w1b": dram("ffn_w1b", np.concatenate([leaf_in(t) for t in trees])),
        "w2b": dram("ffn_w2b", np.concatenate([np.concatenate([t["w2"], t["b2"][:, None, :]], axis=1) for t in trees])),
    }
    def bias_columns(name):
        return np.asarray(inputs[name]).reshape(EXPERTS, HID // P, P).transpose(0, 2, 1)

    moe = {
        "router_w": dram("L1_ffn_router_w"), "router_b": dram("L1_ffn_router_b"),
        "w_c": dram("L1_ffn_w_c_fc"), "w_g": dram("L1_ffn_w_gate"), "w_p": dram("L1_ffn_w_c_proj"),
        "b_cg": dram("moe_b_cg", np.concatenate([bias_columns("L1_ffn_b_c_fc"), bias_columns("L1_ffn_b_gate")], axis=2)),
        "b_p": dram("L1_ffn_b_c_proj", np.asarray(inputs["L1_ffn_b_c_proj"]).reshape(EXPERTS, D)),
    }
    x_in, ctx_in, mask_in = dram("x"), dram("ctx_1024"), dram("mask_BxS2_ik0")
    out = nc.dram_tensor("out", x_in.shape, F32, kind="ExternalOutput").ap()
    xattn_ffn_kernel(nc, x_in, ctx_in, mask_in, xa, ffn, moe, out)
    r = run_bass_kernel_spmd(nc, [arrays], core_ids=[0])
    return r.results[0]["out"]
```

```python
import concourse.bass as bass
from concourse import mybir
from contextlib import ExitStack

F32 = mybir.dt.float32
BF16 = mybir.dt.bfloat16
I32 = mybir.dt.int32
F32R = mybir.dt.float32r
U32 = mybir.dt.uint32
ALU = mybir.AluOpType
ACT = mybir.ActivationFunctionType
AX = mybir.AxisListType

P = 128
B, SEQ, D = 4, 1024, 256
NT = B * SEQ // P
TPB = SEQ // P
GT = 4
DC = D // P
HEADS, DK, CTX = 16, 16, 77
HH = HEADS // 2
HQ = HH // 2
VW = DK + 1
EPS = 1e-5
NEG = -1e30
STEPS = 2 * TPB
DRAIN = 6

LEAVES, DEPTH, LEAF_W = 16, 4, 64
NODES = LEAVES - 1
NODES3, LEAVES3 = 3 * NODES, 3 * LEAVES
SET_TILES = NT + LEAVES
SET_ROWS = SET_TILES * P
FS = 8
GB = 2
WS = 4
IT_SET = SET_TILES // FS
W1W = DC * LEAF_W + 2
ZR = 16
SA_SCALE = D ** -0.5
EXPERTS, TOPK = 8, 2
CAP = int(1.2 * TOPK * SEQ // EXPERTS)
PASSES = 2
BP = B // PASSES
NTP = NT // PASSES
SLOTS = BP * CAP
ROW_TRASH = EXPERTS * SLOTS
SLOT_ROWS = ROW_TRASH + TOPK * NTP * P
SLOT_FILL = 6144
HID = 1024
HIGH_BITS = -1 << 12
BT = 3
YS = 5
GS = 4


class Link:

    def __init__(self, eng, sem):
        self.eng, self.sem, self.base, self.n = eng, sem, 0, 0

    def restart(self, base):
        self.base, self.n = base, 0

    def count(self, ins):
        self.n += 1
        ins.then_inc(self.sem, 1)

    def wait(self):
        self.eng.wait_ge(self.sem, self.base + self.n)

    def __call__(self, ins):
        self.count(ins)
        self.wait()


def xattn_ffn_kernel(nc, x_in, ctx_in, mask_in, xa, ffn, moe, out):
    es = ExitStack()
    with es:
        def sb(name, shape, dt=F32, scope=es):
            return scope.enter_context(nc.sbuf_tensor(name, shape, dt))

        def pb(name, shape, dt=F32, scope=es):
            return scope.enter_context(nc.psum_tensor(name, shape, dt))

        def sem(name):
            return es.enter_context(nc.semaphore(name))

        x = sb("x", [P, NT, D])
        ident = sb("ident", [P, P])
        stat = sb("stat", [P, TPB, 6])
        mean = sb("mean", [P, TPB])
        rstd = sb("rstd", [P, TPB])
        nw = sb("nw", [P, 2, NT])
        stat_all = sb("stat_all", [P, NT, 6])
        mean_all = sb("mean_all", [P, NT])
        rstd_all = sb("rstd_all", [P, NT])
        x_v = x_in.rearrange("b (t p) d -> p (b t) d", p=P)
        out_v = out.rearrange("b (t p) d -> p (b t) d", p=P)

        kb, vb = {}, {}
        kb["c"] = sb("kb_c", [P, B, DC, HH, CTX])
        vb["c"] = sb("vb_c", [CTX, B, HEADS, VW])
        neg = sb("neg", [P, B, CTX], BF16)
        mean128 = sb("mean128", [P, P], BF16)
        wq = {L: sb(f"wq_{L}", [P, DC, D]) for L in "ac"}
        bq = {L: sb(f"bq_{L}", [P, DC]) for L in "ac"}
        bk = {L: sb(f"bk_{L}", [P, DC]) for L in "ac"}
        wo = sb("wo", [P, DC, D])
        bo_bc = sb("bo_bc", [P, D])

        zq = sb("zq", [P, NT, D])
        nodew = sb("nodew", [P, DC, NODES3])
        nodeb = sb("nodeb", [P, NODES3])
        bits = sb("bits", [P, TPB * NODES3])
        path = [sb(f"path{l}", [P, TPB * 3, 2 ** (l + 1)]) for l in range(DEPTH - 1)]
        onehot = sb("onehot", [P, NT, LEAVES3], BF16)
        before = sb("before", [P, NT + 1, LEAVES3], BF16)
        tri = sb("tri", [P, P], BF16)
        ones_bf = sb("ones_bf", [P, P], BF16)
        ones_row = sb("ones_row", [P, LEAVES])
        set_leaf0 = sb("set_leaf0", [1, 3, SET_TILES])
        tile_row = sb("tile_row", [1, SET_TILES])
        expert_id = sb("expert_id", [P, EXPERTS])
        trash = sb("trash", [P, B, TOPK * TPB])
        scan_on = sb("scan_on", [P, EXPERTS, TOPK * TPB])
        cnt_i = sb("cnt_i", [P, LEAVES3], I32)
        padded, incl, base = (sb(n, [P, LEAVES3]) for n in ("padded", "incl", "base"))
        rowt = sb("rowt", [P, TPB, LEAVES3])
        rowf = sb("rowf", [P, 3, TPB])
        row_i = sb("row_i", [P, 3, NT], U32)
        leaff = sb("leaff", [1, 3, SET_TILES])
        leaf_i = sb("leaf_i", [1, 3 * SET_TILES], I32)

        routerw = sb("routerw", [P, DC, EXPERTS])
        routerb = sb("routerb", [P, EXPERTS])
        logit = sb("logit", [P, NT, EXPERTS])
        best = sb("best", [P, NT, 8])
        best_i = sb("best_i", [P, NT, 8], U32)
        choice = sb("choice", [P, NT, TOPK])
        prob = sb("prob", [P, TOPK, NT])
        ohs = sb("ohs", [P, B, EXPERTS, TOPK * TPB], BF16)
        ohb = sb("ohb", [P, B, EXPERTS, TOPK * TPB], BF16)
        upto = sb("upto", [P, EXPERTS, TOPK * TPB])
        xrow = sb("xrow", [P, TOPK * TPB])
        rankt = sb("rankt", [P, EXPERTS, TOPK * TPB])
        rankf = sb("rankf", [P, TOPK * TPB])
        read_i = sb("read_i", [P, B, TOPK * TPB], U32)
        write_i = sb("write_i", [P, B, TOPK * TPB], U32)

        sorted_in, sorted_out = ([nc.dram_tensor(f"sorted_{d}{s}", [SET_ROWS, D], F32, kind="Internal").ap()
                                  for s in range(3)] for d in ("in", "out"))
        slots_in, slots_out = ([nc.dram_tensor(f"slots_{d}{p}", [rows, D], F32, kind="Internal").ap()
                                for p in range(PASSES)] for d, rows in (("in", SLOT_ROWS), ("out", EXPERTS * SLOTS)))

        with ExitStack() as r1:
            kb["a"] = sb("kb_a", [P, B, DC, HH, CTX], scope=r1)
            vb["a"] = sb("vb_a", [CTX, B, HEADS, VW], scope=r1)
            ctx_sb = sb("ctx_sb", [CTX, B, D], scope=r1)
            ctxT = sb("ctxT", [P, DC, B * CTX], scope=r1)
            wk = {L: sb(f"wk_{L}", [P, DC, D], scope=r1) for L in "ac"}
            wv = {L: sb(f"wv_{L}", [P, DC, D], scope=r1) for L in "ac"}
            kT = {L: sb(f"kT_{L}", [P, DC, B * CTX], scope=r1) for L in "ac"}
            bv_bc = {L: sb(f"bv_{L}", [CTX, D], scope=r1) for L in "ac"}
            mask_sb = sb("mask_sb", [P, B * CTX], I32, scope=r1)
            headsel = sb("headsel", [P, HH], scope=r1)
            sa = {
                "y": sb("y", [P, 2, D], scope=r1),
                "yT": sb("yT", [P, DC, GT * P], scope=r1),
                "qT": sb("qT", [P, 2, DC, GT * P], scope=r1),
                "mx": sb("mx", [P, 2, HH], scope=r1),
                "pr": sb("pr", [P, 2, HH, CTX], scope=r1),
                "prT": sb("prT", [CTX, 2, HH, P], scope=r1),
                "rinv": sb("rinv", [P, 2, HH], scope=r1),
                "o": sb("o", [P, 2, D], scope=r1),
                "oT": sb("oT", [P, DC, P], scope=r1),
            }
        with ExitStack() as r2:
            kg = sb("kg", [P, TPB, D], scope=r2)
            with ExitStack() as r3:
                vg = sb("vg", [P, 2, TPB, D], scope=r3)
            with ExitStack() as r4:
                ends = sb("ends", [1, 3, SET_TILES, LEAVES], scope=r4)
            with ExitStack() as r3:
                zt = sb("zt", [P, FS, D], scope=r3)
                yt = sb("yt", [P, FS, D], scope=r3)
                with ExitStack() as r4:
                    w1_all = sb("w1_all", [P, 2, LEAVES, W1W], scope=r4)
                    w2_all = sb("w2_all", [LEAF_W + 1, 2, LEAVES, D], scope=r4)
                    w1s = sb("w1s", [P, WS, W1W], scope=r4)
                    w2s = sb("w2s", [LEAF_W + 1, WS, D], scope=r4)
                    zT = sb("zT", [P, 2, DC, P], scope=r4)
                    hT = sb("hT", [LEAF_W + 1, 2, P], scope=r4)
                k_hi = sb("k_hi", [P, 2, DC, SEQ], F32R, scope=r3)
                k_lo = sb("k_lo", [P, 2, DC, SEQ], F32R, scope=r3)
                q_hi = sb("q_hi", [P, 2, DC, P], F32R, scope=r3)
                q_lo = sb("q_lo", [P, 2, DC, P], F32R, scope=r3)
                t_tmp = sb("t_tmp", [P, 2, DC, P], scope=r3)
                pg = sb("pg", [P, 2, SEQ], scope=r3)
                pgT = sb("pgT", [P, 2, TPB, P], scope=r3)
                smax, nmax, rsum = (sb(n, [P, 2], scope=r3) for n in ("smax", "nmax", "rsum"))
                psum_exp = sb("psum_exp", [P, 4], scope=r3)

        with ExitStack() as r5:
            w_raw = sb("w_raw", [P, 2, DC, HID], scope=r5)
            w_hi = sb("w_hi", [P, 2, DC, HID], F32R, scope=r5)
            w_lo = sb("w_lo", [P, 2, DC, HID], F32R, scope=r5)
            wp = sb("wp", [P, HID // P, D], scope=r5)
            bcg = sb("bcg", [P, 2, 2 * HID // P], scope=r5)
            bp = sb("bp", [P, 2, D], scope=r5)
            xr = sb("xr", [P, 2, -(-SLOTS // P), D], scope=r5)
            x_hi = sb("x_hi", [P, 2, DC, BT * P], F32R, scope=r5)
            x_lo = sb("x_lo", [P, 2, DC, BT * P], F32R, scope=r5)
            hb = sb("hb", [P, 2, BT * P], scope=r5)
            hg = sb("hg", [P, 2, BT * P], scope=r5)
        dead = kb["c"][:].rearrange("p b j h s -> p (b j h s)")
        yo = dead[:, 0:YS * D].rearrange("p (u d) -> p u d", u=YS)
        BLOCK = HID // P * BT * P
        st1 = dead[:, YS * D:YS * D + BLOCK]
        x_tmp = dead[:, YS * D + BLOCK:YS * D + BLOCK + 2 * DC * P].rearrange("p (u c t) -> p u c t", u=2, c=DC)
        zT_of = {"b": zT, "d": x_tmp}
        tokens = zq[:].rearrange("p t d -> p (t d)")
        st = [a.rearrange("p (m w) -> p m w", m=HID // P) for a in (tokens[:, 0:BLOCK], st1)]
        w_tmp = tokens[:, BLOCK:BLOCK + 4 * DC * P].rearrange("p (u g c n) -> p u g c n", u=2, g=2, c=DC)
        yg = tokens[:, NTP * D:(NTP + GS * TOPK) * D].rearrange("p (u k d) -> p u k d", u=GS, k=TOPK)

        psS = pb("psS", [P, 2, 2, 512])
        psT = pb("psT", [P, 2, 512])
        psO = pb("psO", [P, 512])
        psM = pb("psM", [P, 512])

        s_x0 = sem("x_batch0_loaded")
        s_ctx, s_x, s_w, s_mask = sem("ctx_loaded"), sem("x_loaded"), sem("weights_loaded"), sem("mask_loaded")
        s_ident, s_const, s_hs = sem("ident_ready"), sem("consts_ready"), sem("headsel_ready")
        s_poolc = sem("pool_chain")
        p_ctxT, p_ctxTc, p_k, p_kc, p_v, p_vc = (sem(n) for n in
            ("ctxT_done", "ctxT_copied", "k_done", "k_copied", "v_done", "v_copied"))
        s_kb = {L: sem(f"kb_ready_{L}") for L in "ac"}
        s_neg = sem("neg_ready")
        s_out = sem("out_stored")

        N_ = {}
        for L in "ac":
            for n in ("yT_done", "yT_copied", "q_done", "q_copied", "scores_done", "shifted", "exp_done",
                      "prT_done", "prT_copied", "pv_done", "o_ready", "oT_done", "oT_copied", "wo_done",
                      "y_ready", "x_biased", "x_updated", "chain"):
                N_[L, n] = sem(f"{L}_{n}")

        for L in "bd":
            for n in ("z_ready", "zT_done", "zT_copied", "node_done", "scores_used", "rank_done", "chain"):
                N_[L, n] = sem(f"{L}_{n}")
        for n in ("zT_done", "zT_copied", "w1_copied", "w2_copied", "h_done", "h_copied", "y_done", "y_copied"):
            N_["f", n] = sem(f"f_{n}")
        for n in ("tr_done", "tr_masked", "hi_ready", "lo_ready", "scores_done", "bias_ready", "exp_done", "pT_done", "pT_copied", "pv_done",
                  "x_updated", "chain"):
            N_["g", n] = sem(f"g_{n}")
        s_node, s_zeros, s_zfill, s_tables = sem("node_loaded"), sem("zeros_ready"), sem("zero_filled"), sem("tables_ready")
        for n in ("w_masked", "w_hi_ready", "w_lo_ready", "x_masked", "x_hi_ready", "x_lo_ready", "xT_done", "hg_done", "h_ready", "gated", "silu_done", "o_done", "o_copied"):
            N_["e", n] = sem(f"e_{n}")
        s_before = sem("tiles_summed")
        s_ohs, s_xrank, s_gap, s_gexp, s_half, s_fin = (sem(n) for n in (
            "onehots_ready", "slot_ranks_done", "gap_ready", "gap_exp_done", "first_added", "x_final"))
        s_disp = [sem(f"dispatched{p}") for p in range(PASSES)]
        s_rawload, s_wpload = sem("expert_raw_loaded"), sem("expert_proj_loaded")
        s_wload = [sem(f"expert_biases_loaded{q}") for q in range(2)]
        s_xload = [sem(f"slots_loaded{q}") for q in range(2)]
        s_ostore = [sem(f"o_stored{u}") for u in range(YS)]
        s_yload = [sem(f"outputs_gathered{u}") for u in range(GS)]
        s_rows, s_leaf = sem("rows_ready"), sem("leaf_table_ready")
        s_scat = [sem(f"scattered{s}") for s in range(3)]
        s_qgath, s_kgath, s_vgath = sem("queries_gathered"), sem("keys_gathered"), sem("values_gathered")
        s_leafw = [sem(f"leaf_weights_loaded{s}") for s in range(3)]
        s_zload = [sem(f"tiles_loaded{g}") for g in range(FS // GB)]
        s_ystore = [sem(f"y_stored{g}") for g in range(FS // GB)]

        def prep_sync(sp):
            sp.dma_start(ctx_sb[:], ctx_in.rearrange("b s d -> s b d")).then_inc(s_ctx, 16)
            for L in "ac":
                sp.dma_start(wk[L][:], xa[L]["wk"].rearrange("(c p) n -> p c n", p=P)).then_inc(s_w, 16)
                sp.dma_start(wv[L][:], xa[L]["wv"].rearrange("(c p) n -> p c n", p=P)).then_inc(s_w, 16)
                sp.dma_start(wq[L][:], xa[L]["wq"].rearrange("(c p) n -> p c n", p=P)).then_inc(s_w, 16)
            sp.dma_start(wo[:], xa["a"]["wo"].rearrange("(c p) n -> p c n", p=P)).then_inc(s_w, 16)

        def prep_loads_act(act):
            act.dma_start(x[:, 0:TPB, :], x_v[:, 0:TPB, :]).then_inc(s_x0, 16)
            for L in "ac":
                act.dma_start(bq[L][:], xa[L]["bq"]).then_inc(s_w, 16)
                act.dma_start(bk[L][:], xa[L]["bk"]).then_inc(s_w, 16)
                act.dma_start(bv_bc[L][:], xa[L]["bv"].partition_broadcast(CTX)).then_inc(s_w, 16)
            act.dma_start(bo_bc[:], xa["a"]["bo"].partition_broadcast(P)).then_inc(s_w, 16)
            act.dma_start(mask_sb[:], mask_in.rearrange("b s -> (b s)").partition_broadcast(P)).then_inc(s_mask, 16)
            act.dma_start(x[:, TPB:NT, :], x_v[:, TPB:NT, :]).then_inc(s_x, 16)

        N_W = 14

        def prep_pool(pool):
            ch = Link(pool, s_poolc)
            ch(nc.gpsimd.memset(ident[:], 0.0))
            nc.gpsimd.affine_select(out=ident[:], in_=ident[:], compare_op=ALU.not_equal, fill=1.0, base=0,
                                    pattern=[[-1, P]], channel_multiplier=1).then_inc(s_ident, 1)
            ch(nc.gpsimd.memset(headsel[:], 1.0 / DK ** 0.5))
            ch(nc.gpsimd.affine_select(out=headsel[:], in_=headsel[:], compare_op=ALU.is_ge, fill=0.0, base=0,
                                       pattern=[[-DK, HH]], channel_multiplier=1))
            nc.gpsimd.affine_select(out=headsel[:], in_=headsel[:], compare_op=ALU.is_ge, fill=0.0, base=DK - 1,
                                    pattern=[[DK, HH]], channel_multiplier=-1).then_inc(s_hs, 1)
            nc.gpsimd.memset(mean128[:], 1.0 / P).then_inc(s_const, 1)
            for L in "ac":
                nc.gpsimd.memset(vb[L][:, :, :, DK:VW], 1.0).then_inc(s_const, 1)
            consts_pool(pool, ch)
            pool.wait_ge(s_hs, 1)
            key_blocks(pool, nc.gpsimd, "c", 2 * DC)

        def key_blocks(eng, e, L, copied):
            eng.wait_ge(p_kc, copied)
            for b in range(B):
                for j in range(DC):
                    e.tensor_tensor(
                        out=kb[L][:, b, j],
                        in0=kT[L][:, j, b * CTX:(b + 1) * CTX].unsqueeze(1).broadcast_to([P, HH, CTX]),
                        in1=headsel[:].unsqueeze(2).broadcast_to([P, HH, CTX]),
                        op=ALU.mult).then_inc(s_kb[L], 1)

        def prep_pe(pe):
            pe.wait_ge(s_ident, 1)
            pe.wait_ge(s_ctx, 16)
            for b in range(B):
                for c in range(DC):
                    i = nc.tensor.transpose(psS[:, c, 0, b * CTX:(b + 1) * CTX], ctx_sb[:, b, c * P:(c + 1) * P],
                                            ident[0:CTX, 0:CTX])
                    if b == B - 1:
                        i.then_inc(p_ctxT, 1)
            pe.wait_ge(s_w, 16 * N_W)
            pe.wait_ge(p_ctxTc, DC)
            for j in range(DC):
                prep_pe_keys("a", j)
            for b in range(B):
                prep_pe_values(pe, "a", b)

        def prep_pe_keys(L, j):
            n = "ac".index(L) * DC + j
            for c in range(DC):
                i = nc.tensor.matmul(psS[:, n // 2, n % 2, 0:B * CTX], wk[L][:, c, j * P:(j + 1) * P],
                                     ctxT[:, c, :], start=(c == 0), stop=(c == DC - 1))
            i.then_inc(p_k, 1)

        def prep_pe_values(pe, L, b):
            n = "ac".index(L) * B + b
            if n >= 2:
                pe.wait_ge(p_vc, n - 1)
            for c in range(DC):
                i = nc.tensor.matmul(psT[0:CTX, n % 2, 0:D], ctxT[:, c, b * CTX:(b + 1) * CTX],
                                     wv[L][:, c, :], start=(c == 0), stop=(c == DC - 1))
            i.then_inc(p_v, 1)

        def prep_act(act):
            for c in range(DC):
                act.wait_ge(p_ctxT, c + 1)
                nc.scalar.copy(ctxT[:, c, :], psS[:, c, 0, 0:B * CTX]).then_inc(p_ctxTc, 1)
            act.wait_ge(s_w, 16 * N_W)
            for j in range(DC):
                prep_act_keys(act, "a", j)

        def prep_act_keys(act, L, j):
            n = "ac".index(L) * DC + j
            act.wait_ge(p_k, n + 1)
            nc.scalar.activation(kT[L][:, j, :], psS[:, n // 2, n % 2, 0:B * CTX], ACT.Identity,
                                 bias=bk[L][:, j:j + 1]).then_inc(p_kc, 1)

        def prep_dve_mask(dve):
            dve.wait_ge(s_mask, 16)
            nc.vector.tensor_scalar(neg[:].rearrange("p b s -> p (b s)"), mask_sb[:], 0, NEG,
                                    ALU.is_gt, ALU.mult).then_inc(s_neg, 1)

        def prep_dve_values(dve, L):
            for b in range(B):
                n = "ac".index(L) * B + b
                dve.wait_ge(p_v, n + 1)
                nc.vector.tensor_tensor(
                    out=vb[L][:, b, :, 0:DK],
                    in0=psT[0:CTX, n % 2, 0:D].rearrange("p (h d) -> p h d", h=HEADS),
                    in1=bv_bc[L][:].rearrange("p (h d) -> p h d", h=HEADS), op=ALU.add).then_inc(p_vc, 1)

        def bodies(eng, step, chain=None, per=0):
            for k in range(STEPS):
                step(0, k, True, False)
            done = chain.base + chain.n if chain else 0
            with eng.Fori(1, B - 1) as b:
                if chain:
                    chain.restart(b * per + (done - per))
                for k in range(STEPS):
                    step(b, k, False, False)
                assert not chain or chain.n == per
            if chain:
                chain.restart(done + (B - 2) * per)
            for k in range(STEPS + DRAIN):
                step(B - 1, k, False, True)

        def query_piece(f):
            return f % 2, (f - GT) // 2

        def piece_copied(pe, L, G, f):
            if f < GT:
                pe.wait_ge(N_[L, "yT_copied"], GT * G + f + 1)
            else:
                pe.wait_ge(N_[L, "q_copied"], GT * G + (f - GT) + 1)

        def front_pe(pe, L, G, f, first=False):
            if f < GT:
                T = GT * G + f
                pe.wait_ge(N_[L, "y_ready"], T + 1)
                if not first:
                    piece_copied(pe, L, G if f else G - 1, (f - 1) % 8)
                for c in range(DC):
                    m = nc.tensor.transpose(psM[:, c * P:(c + 1) * P], sa["y"][:, f % 2, c * P:(c + 1) * P], ident[:])
                m.then_inc(N_[L, "yT_done"], 1)
            else:
                j, h = query_piece(f)
                piece_copied(pe, L, G, f - 1)
                for c in range(DC):
                    m = nc.tensor.matmul(psM[:, 0:2 * P], wq[L][:, c, j * P:(j + 1) * P],
                                         sa["yT"][:, c, h * 2 * P:(h + 1) * 2 * P],
                                         start=(c == 0), stop=(c == DC - 1))
                m.then_inc(N_[L, "q_done"], 1)

        def front_act(act, L, G, g2, f):
            if f < GT:
                act.wait_ge(N_[L, "yT_done"], GT * G + f + 1)
                nc.scalar.copy(sa["yT"][:, :, f * P:(f + 1) * P],
                               psM[:, 0:D].rearrange("p (c t) -> p c t", c=DC)).then_inc(N_[L, "yT_copied"], 1)
            else:
                j, h = query_piece(f)
                act.wait_ge(N_[L, "q_done"], GT * G + (f - GT) + 1)
                nc.scalar.activation(sa["qT"][:, g2, j, h * 2 * P:(h + 1) * 2 * P], psM[:, 0:2 * P], ACT.Identity,
                                     bias=bq[L][:, j:j + 1]).then_inc(N_[L, "q_copied"], 1)

        def xattn_pe(pe, L):
            def step(b, k, first, last):
                n = STEPS * b + k
                drain = k >= STEPS
                if not drain:
                    g = k // 8
                    if k % 4 == 0:
                        pe.wait_ge(N_[L, "q_copied"], GT * (2 * b + g) + (2 if k % 8 == 0 else 4))
                    if not (first and k < 2):
                        pe.wait_ge(N_[L, "shifted"], n - 1)
                    for q in range(2):
                        o = psS[:, k % 2, q, 0:HQ * CTX].rearrange("p (h s) -> p h s", h=HQ)
                        j = k % 2
                        lhs = sa["qT"][:, g, j, ((k // 2) % GT) * P:((k // 2) % GT + 1) * P]
                        m = nc.tensor.matmul(o, lhs, kb[L][:, b, j, q * HQ:(q + 1) * HQ, :],
                                             start=True, stop=(L == "a"))
                        if L == "c":
                            m = nc.tensor.matmul(o, mean128[:], neg[:, b, :].unsqueeze(1).broadcast_to([P, HQ, CTX]),
                                                 start=False, stop=True)
                    m.then_inc(N_[L, "scores_done"], 1)
                out_tile = L == "a" and k % 2 == 0 and not (first and k < 6)
                T = TPB * b + (k - 6) // 2
                if out_tile:
                    pe.wait_ge(N_[L, "o_ready"], 2 * T + 2)
                    if not (last and k >= 9):
                        piece_copied(pe, L, 2 * b + (k - 1) // 8 + 1, (k - 1) % 8)
                    else:
                        pe.wait_ge(N_[L, "x_updated"], T)
                    for c in range(DC):
                        m = nc.tensor.transpose(psM[:, c * P:(c + 1) * P],
                                                sa["o"][:, ((k - 6) // 2) % 2, c * P:(c + 1) * P], ident[:])
                    m.then_inc(N_[L, "oT_done"], 1)
                if k - 1 < STEPS and not (first and k < 1):
                    pe.wait_ge(N_[L, "exp_done"], n)
                    for q in range(2):
                        if not (first and k < 2):
                            pe.wait_ge(N_[L, "prT_copied"], 2 * (n - 2) + q + 1)
                        for h in range(HQ):
                            m = nc.tensor.transpose(psT[0:CTX, q, h * P:(h + 1) * P],
                                                    sa["pr"][:, (k - 1) % 2, q * HQ + h, :], ident[:])
                        m.then_inc(N_[L, "prT_done"], 1)
                if not (last and k >= 8):
                    if out_tile:
                        pe.wait_ge(N_[L, "oT_copied"], T + 1)
                    elif L == "a" and not (first and k < 7):
                        pe.wait_ge(N_[L, "x_updated"], TPB * b + (k - 7) // 2 + 1)
                    front_pe(pe, L, 2 * b + k // 8 + 1, k % 8)
                if k - 2 < STEPS and not (first and k < 2):
                    pe.wait_ge(N_[L, "prT_copied"], 2 * (n - 2) + 2)
                    if not (first and k < 3):
                        pe.wait_ge(N_[L, "o_ready"], n - 2)
                    bb = b if k >= 2 else b - 1
                    for h in range(HH):
                        m = nc.tensor.matmul(psO[:, h * VW:(h + 1) * VW], sa["prT"][:, k % 2, h, :],
                                             vb[L][:, bb, (k % 2) * HH + h, :], start=True, stop=True)
                    m.then_inc(N_[L, "pv_done"], 1)
                if out_tile:
                    if not (last and k >= 8):
                        piece_copied(pe, L, 2 * b + k // 8 + 1, k % 8)
                    else:
                        pe.wait_ge(N_[L, "oT_copied"], T + 1)
                    for c in range(DC):
                        m = nc.tensor.matmul(psM[:, 0:D], sa["oT"][:, c, :], wo[:, c, :],
                                             start=(c == 0), stop=(c == DC - 1))
                    m.then_inc(N_[L, "wo_done"], 1)

            if L == "a":
                pe.wait_ge(s_ident, 1)
            else:
                pe.wait_ge(N_["g", "lo_ready"], TPB + 2 * NT)
            for f in range(8):
                front_pe(pe, L, 0, f, f == 0)
                if L == "a" and 1 <= f < 3:
                    prep_pe_keys("c", f - 1)
                elif L == "a" and 3 <= f < 7:
                    prep_pe_values(pe, "c", f - 3)
            pe.wait_ge(s_kb[L], B * DC)
            pe.wait_ge(p_vc, 2 * B)
            pe.wait_ge(s_const, 3)
            pe.wait_ge(s_neg, 1)
            bodies(pe, step)

        def xattn_act(act, L):
            def step(b, k, first, last):
                n = STEPS * b + k
                if k - 1 < STEPS and not (first and k < 1):
                    act.wait_ge(N_[L, "shifted"], n)
                    pr = sa["pr"][:, (k - 1) % 2].rearrange("p h s -> p (h s)")
                    nc.scalar.activation(pr, pr, ACT.Exp).then_inc(N_[L, "exp_done"], 1)

                if L == "a" and k % 2 == 0 and not (first and k < 6):
                    act.wait_ge(N_[L, "oT_done"], TPB * b + (k - 6) // 2 + 1)
                    nc.scalar.copy(sa["oT"][:], psM[:, 0:D].rearrange("p (c t) -> p c t", c=DC))\
                        .then_inc(N_[L, "oT_copied"], 1)
                if k - 1 < STEPS and not (first and k < 1):
                    if not (first and k < 3):
                        act.wait_ge(N_[L, "pv_done"], n - 2)
                    for q in range(2):
                        act.wait_ge(N_[L, "prT_done"], 2 * (n - 1) + q + 1)
                        nc.scalar.copy(sa["prT"][:, (k - 1) % 2, q * HQ:(q + 1) * HQ, :],
                                       psT[0:CTX, q, :].rearrange("p (h t) -> p h t", h=HQ))\
                            .then_inc(N_[L, "prT_copied"], 1)
                if not (last and k >= 8):
                    front_act(act, L, 2 * b + k // 8 + 1, (k // 8 + 1) % 2, k % 8)

            act.wait_ge(s_w, 16 * N_W)
            for f in range(8):
                front_act(act, L, 0, 0, f)
                if L == "a" and 1 <= f < 3:
                    prep_act_keys(act, "c", f - 1)
            bodies(act, step)

        def tile_stats(ch, dst, T, i):
            ch.count(nc.vector.bn_stats(dst[:, i, :], x[:, T, :]))

        def tiles_rstd(ch, stat, mean, rstd):
            ch.wait()
            m_even, q_even, m_odd, q_odd = (stat[:, :, i] for i in (1, 2, 4, 5))
            n = stat.shape[1]
            v, t, r = nw[:, 0, 0:n], nw[:, 1, 0:n], rstd[:]
            ch.count(nc.vector.tensor_tensor(out=mean[:], in0=m_even, in1=m_odd, op=ALU.add))
            ch.count(nc.vector.tensor_tensor(out=t, in0=m_even, in1=m_odd, op=ALU.subtract))
            ch(nc.vector.tensor_tensor(out=v, in0=q_even, in1=q_odd, op=ALU.add))
            ch.count(nc.vector.tensor_scalar(mean[:], mean[:], 0.5, None, ALU.mult))
            ch(nc.vector.tensor_tensor(out=t, in0=t, in1=t, op=ALU.mult))
            ch(nc.vector.scalar_tensor_tensor(v, t, D / 4.0, v, ALU.mult, ALU.add))
            ch(nc.vector.tensor_scalar(v, v, 1.0 / D, EPS, ALU.mult, ALU.add))
            ch(nc.vector.tensor_scalar(r.bitcast(I32), v.bitcast(I32), -0.5, float(0x5F3759DF), ALU.mult, ALU.add))
            for _ in range(3):
                ch(nc.vector.tensor_tensor(out=t, in0=r, in1=r, op=ALU.mult))
                ch(nc.vector.scalar_tensor_tensor(t, t, -0.5, v, ALU.mult, ALU.mult))
                ch(nc.vector.scalar_tensor_tensor(r, t, 1.5, r, ALU.add, ALU.mult))
        LN_CHAIN = TPB + 8 + 9

        def normalise(dst, T, m, r):
            return nc.vector.tensor_scalar(dst, x[:, T, :], m, r, ALU.subtract, ALU.mult)

        def route_tile(L, T):
            normalise(zq[:, T, :], T, mean_all[:, T:T + 1], rstd_all[:, T:T + 1]).then_inc(N_[L, "z_ready"], 1)

        def xattn_dve(dve, L):
            ch = Link(dve, N_[L, "chain"])
            routed = {"a": "b", "c": "d"}[L]

            def norm_tile(b, g, i):
                T = GT * (2 * b + g) + i
                if not (isinstance(b, int) and b == 0 and g == 0 and i < 2):
                    dve.wait_ge(N_[L, "yT_done"], T - 1)
                i8 = GT * (g % 2) + i
                normalise(sa["y"][:, i % 2, :], T, mean[:, i8:i8 + 1], rstd[:, i8:i8 + 1]).then_inc(N_[L, "y_ready"], 1)

            def step(b, k, first, last):
                n = STEPS * b + k
                if 3 <= k + (0 if first else 3) and k - 3 < STEPS:
                    par, tp, j = (k - 3) % 2, ((k - 3) // 2) % 2, (k - 3) % 2
                    dve.wait_ge(N_[L, "pv_done"], n - 2)
                    pv = psO[:, 0:HH * VW].rearrange("p (h d) -> p h d", h=HH)
                    ch(nc.vector.reciprocal(sa["rinv"][:, par, :], pv[:, :, DK]))
                    if j == 0 and not (first and k < 7):
                        dve.wait_ge(N_[L, "oT_done" if L == "a" else "x_updated"], TPB * b + (k - 3) // 2 - 1)
                    nc.vector.tensor_tensor(
                        out=sa["o"][:, tp, j * P:(j + 1) * P].rearrange("p (h d) -> p h d", h=HH),
                        in0=pv[:, :, 0:DK], in1=sa["rinv"][:, par, :].unsqueeze(2).broadcast_to([P, HH, DK]),
                        op=ALU.mult).then_inc(N_[L, "o_ready"], 1)
                if L == "a" and k % 2 == 1 and not (first and k < 7):
                    T = TPB * b + (k - 7) // 2
                    dve.wait_ge(N_[L, "wo_done"], T + 1)
                    dve.wait_ge(N_[L, "x_biased"], T + 1)
                    nc.vector.tensor_tensor(out=x[:, T, :], in0=psM[:, 0:D], in1=x[:, T, :], op=ALU.add)\
                        .then_inc(N_[L, "x_updated"], 1)
                if k < STEPS:
                    dve.wait_ge(N_[L, "scores_done"], n + 1)
                    s = psS[:, k % 2, :, 0:HQ * CTX].rearrange("p q (h s) -> p q h s", h=HQ)
                    mx = sa["mx"][:, k % 2, :].rearrange("p (q h) -> p q h", q=2)
                    ch(nc.vector.tensor_reduce(mx, s, AX.X, ALU.max))
                    if not (first and k < 2):
                        dve.wait_ge(N_[L, "prT_done"], 2 * (n - 2) + 2)
                    nc.vector.tensor_tensor(
                        out=sa["pr"][:, k % 2].rearrange("p (q h) s -> p q h s", q=2), in0=s,
                        in1=mx.unsqueeze(3).broadcast_to([P, 2, HQ, CTX]), op=ALU.subtract)\
                        .then_inc(N_[L, "shifted"], 1)
                if k < TPB and not last:
                    if L == "a" and k == 0:
                        dve.wait_ge(s_x, 16)
                    tile_stats(ch, stat, TPB * (b + 1) + k, k)
                if k == TPB - 1 and not last:
                    tiles_rstd(ch, stat, mean, rstd)
                if (k + 1) % 8 < GT and not (last and k + 1 >= 8):
                    norm_tile(b, (k + 1) // 8 + 1, (k + 1) % 8)
                if k % 2 == 1 and not (first and k < 7):
                    T = TPB * b + (k - 7) // 2
                    dve.wait_ge(N_[L, "x_updated"], T + 1)
                    tile_stats(ch, stat_all, T, T)
                if last and k == 9:
                    tiles_rstd(ch, *(a[:, 0:3 * TPB] for a in (stat_all, mean_all, rstd_all)))
                    if L == "a":
                        dve.wait_ge(s_zfill, N_ZFILL)
                if last and 10 <= k < 10 + TPB:
                    for T in (2 * (k - 10), 2 * (k - 10) + 1):
                        route_tile(routed, T)

            if L == "a":
                dve.wait_ge(s_x0, 16)
            else:
                dve.wait_ge(N_["g", "x_updated"], NT)
            if L == "a":
                for T in range(TPB):
                    tile_stats(ch, stat, T, T)
                tiles_rstd(ch, stat, mean, rstd)
            else:
                ch.restart(LN_CHAIN)
            for i in range(2):
                norm_tile(0, 0, i)
            if L == "a":
                dve.wait_ge(s_w, 16 * N_W)
                prep_dve_values(dve, "a")
            for i in range(2, GT):
                norm_tile(0, 0, i)
            norm_tile(0, 1, 0)
            if L == "a":
                dve.wait_ge(s_hs, 1)
                key_blocks(dve, nc.vector, "a", DC)
                prep_dve_values(dve, "c")
            bodies(dve, step, ch, per=2 * STEPS + TPB + LN_CHAIN)
            ch.wait()

        def xattn_pool(pool, L):
            if L == "a":
                with pool.Fori(0, NT) as T:
                    pool.wait_ge(N_["a", "y_ready"], T + 1)
                    nc.gpsimd.tensor_tensor(out=x[:, T, :], in0=x[:, T, :], in1=bo_bc[:], op=ALU.add)\
                        .then_inc(N_["a", "x_biased"], 1)
            else:
                with pool.Fori(0, NT // 2) as t2:
                    for u in range(2):
                        pool.wait_ge(N_["c", "o_ready"], 4 * t2 + 2 * u + 2)
                        nc.gpsimd.tensor_tensor(out=x[:, 2 * t2 + u, :], in0=x[:, 2 * t2 + u, :],
                                                in1=sa["o"][:, u, :], op=ALU.add).then_inc(N_["c", "x_updated"], 1)

        def route_sync(sp):
            sp.dma_start(nodew[:], ffn["node_w"].rearrange("(c p) n -> p c n", p=P)).then_inc(s_node, 16)
            sp.dma_start(nodeb[:], ffn["node_b"].partition_broadcast(P)).then_inc(s_node, 16)
            sp.dma_start(routerw[:], moe["router_w"].rearrange("(c p) n -> p c n", p=P)).then_inc(s_node, 16)
            sp.dma_start(routerb[:], moe["router_b"].partition_broadcast(P)).then_inc(s_node, 16)
            sp.wait_ge(s_zeros, 1)
            rows = zq[:, 0:ZR, :]
            n = P * ZR
            for buf in (*sorted_in, *(s[0:SLOT_FILL, :] for s in slots_in)):
                for i in range(buf.shape[0] // n):
                    sp.dma_start(buf[i * n:(i + 1) * n, :].rearrange("(p r) d -> p r d", p=P), rows)\
                        .then_inc(s_zfill, 16)
        N_ZFILL = 16 * (3 * SET_ROWS + PASSES * SLOT_FILL) // (P * ZR)

        def consts_pool(pool, ch):
            nc.gpsimd.memset(zq[:, 0:ZR, :], 0.0).then_inc(s_zeros, 1)
            ch(nc.gpsimd.memset(tri[:], 1.0))
            ch(nc.gpsimd.affine_select(out=tri[:], in_=tri[:], compare_op=ALU.is_ge, fill=0.0, base=0,
                                       pattern=[[1, P]], channel_multiplier=-1))
            ch(nc.gpsimd.memset(ones_bf[:], 1.0))
            ch(nc.gpsimd.memset(before[:, 0, :], 0.0))
            ch(nc.gpsimd.memset(ones_row[:], 1.0))
            for s in range(3):
                ch(nc.gpsimd.memset(set_leaf0[:, s, :], float(s % 2 * LEAVES)))
            ch(nc.gpsimd.iota(tile_row[:], pattern=[[P, SET_TILES]], base=0, channel_multiplier=0,
                              allow_small_or_imprecise_dtypes=True))
            ch(nc.gpsimd.memset(scan_on[:], 1.0))
            ch(nc.gpsimd.memset(scan_on[:, :, 0:1], 0.0))
            ch(nc.gpsimd.iota(expert_id[:], pattern=[[1, EXPERTS]], base=0, channel_multiplier=0,
                              allow_small_or_imprecise_dtypes=True))
            nc.gpsimd.iota(trash[:].rearrange("p (h b) q -> p h b q", h=PASSES),
                           pattern=[[0, PASSES], [P * TOPK * TPB, BP], [P, TOPK * TPB]], base=ROW_TRASH, channel_multiplier=1,
                           allow_small_or_imprecise_dtypes=True).then_inc(s_tables, 1)

        def transposed_z(pe, L, T, k):
            for c in range(DC):
                m = nc.tensor.transpose(psT[:, k % 2, c * P:(c + 1) * P], zq[:, T, c * P:(c + 1) * P], ident[:])
            m.then_inc(N_[L, "zT_done"], 1)

        def score_bank(b):
            return (psO, psM)[b % 2]

        def route_pe(pe, L, w, width, after):
            def scores(b, k):
                T = TPB * b + k
                pe.wait_ge(N_[L, "zT_copied"], T + 1)
                if k == 0 and b == 0:
                    pe.wait_ge(*((N_["a", "x_updated"], NT) if L == "b" else (N_["c", "o_ready"], 2 * NT)))
                if k == 0 and b >= 2:
                    pe.wait_ge(N_[L, "scores_used"], b - 1)
                for c in range(DC):
                    m = nc.tensor.matmul(score_bank(b)[:, k * width:(k + 1) * width], zT_of[L][:, k % 2, c, :], w[:, c, :],
                                         start=(c == 0), stop=(c == DC - 1))
                m.then_inc(N_[L, "node_done"], 1)

            pe.wait_ge(s_node, 64)
            for b in range(B):
                for k in range(TPB):
                    T = TPB * b + k
                    pe.wait_ge(N_[L, "z_ready"], T + 1)
                    if T >= 2:
                        pe.wait_ge(N_[L, "zT_copied"], T - 1)
                    transposed_z(pe, L, T, k)
                    if k:
                        scores(b, k - 1)
                    if b and k == TPB // 2:
                        after(b - 1)
                scores(b, TPB - 1)
            after(B - 1)

        def route_act(act, L):
            def body(b, first):
                for k in range(TPB):
                    T = TPB * b + k
                    act.wait_ge(N_[L, "zT_done"], T + 1)
                    if not (first and k < 2):
                        act.wait_ge(N_[L, "node_done"], T - 1)
                    nc.scalar.copy(zT_of[L][:, k % 2], psT[:, k % 2, 0:D].rearrange("p (c t) -> p c t", c=DC))\
                        .then_inc(N_[L, "zT_copied"], 1)
            body(0, True)
            with act.Fori(1, B) as b:
                body(b, False)

        def route_norm(L, b):
            for T in range(TPB * b, TPB * (b + 1)):
                route_tile(L, T)

        def route_dve(ch, L, batch):
            route_norm(L, 2)
            tiles_rstd(ch, *(a[:, 3 * TPB:NT] for a in (stat_all, mean_all, rstd_all)))
            batch(0)
            route_norm(L, 3)
            for b in range(1, B):
                batch(b)

        def tree_dve(dve):
            ch = Link(dve, N_["b", "chain"])
            dve.wait_ge(s_node, 64)
            dve.wait_ge(N_["a", "x_updated"], NT)
            dve.wait_ge(s_tables, 1)
            ch(nc.vector.tensor_scalar(nodeb[:], nodeb[:], -1.0, None, ALU.mult))

            def batch(b):
                dve.wait_ge(N_["b", "node_done"], TPB * (b + 1))
                i = nc.vector.tensor_tensor(
                    out=bits[:].rearrange("p (t n) -> p t n", t=TPB),
                    in0=score_bank(b)[:, 0:TPB * NODES3].rearrange("p (t n) -> p t n", t=TPB),
                    in1=nodeb[:].unsqueeze(1).broadcast_to([P, TPB, NODES3]), op=ALU.is_ge)
                i.then_inc(N_["b", "scores_used"], 1)
                dve.wait_ge(N_["b", "scores_used"], b + 1)
                bv = bits[:].rearrange("p (m n) -> p m n", n=NODES)
                p1 = path[0][:]
                ch.count(nc.vector.tensor_scalar(p1[:, :, 0], bv[:, :, 0], -1.0, 1.0, ALU.mult, ALU.add))
                ch(nc.vector.tensor_scalar(p1[:, :, 1], bv[:, :, 0], 1.0, None, ALU.mult))
                for l in range(1, DEPTH):
                    w = 2 ** l
                    src = path[l - 1][:]
                    if l < DEPTH - 1:
                        dst = path[l][:].rearrange("p m (w two) -> p m w two", two=2)
                    else:
                        dst = onehot[:, b * TPB:(b + 1) * TPB, :].rearrange("p t (m w two) -> p (t m) w two", m=3, two=2)
                    ch(nc.vector.tensor_tensor(out=dst[:, :, :, 1], in0=src, in1=bv[:, :, w - 1:2 * w - 1], op=ALU.mult))
                    ch(nc.vector.tensor_tensor(out=dst[:, :, :, 0], in0=src, in1=dst[:, :, :, 1], op=ALU.subtract))
                for T in range(TPB * b, TPB * (b + 1)):
                    i = nc.vector.tensor_tensor(out=before[:, T + 1, :], in0=before[:, T, :], in1=onehot[:, T, :], op=ALU.add)
                    i.then_inc(s_before, 1)
                    dve.wait_ge(s_before, T + 1)
            route_dve(ch, "b", batch)
            dve.wait_ge(N_["b", "rank_done"], 1)
            ch(nc.vector.tensor_scalar(cnt_i[:], psO[:, 0:LEAVES3], float(P - 1), None, ALU.add))
            ch(nc.vector.tensor_scalar(cnt_i[:], cnt_i[:], 7, 7, ALU.arith_shift_right, ALU.logical_shift_left))
            ch(nc.vector.tensor_copy(padded[:], cnt_i[:]))
            for s in range(3):
                r = slice(s * LEAVES, (s + 1) * LEAVES)
                ch(nc.vector.tensor_tensor_scan(incl[:, r], ones_row[:, 0:LEAVES], padded[:, r], 0.0, ALU.mult, ALU.add))
            ch(nc.vector.tensor_tensor(out=base[:], in0=incl[:], in1=padded[:], op=ALU.subtract))
            ch(nc.vector.tensor_scalar(base[:], base[:], -1.0, None, ALU.add))
            for b in range(B):
                dve.wait_ge(N_["b", "rank_done"], 2 + b)
                r = psS[:, b // 2, b % 2, 0:TPB * LEAVES3].rearrange("p (t m) -> p t m", t=TPB)
                ch(nc.vector.tensor_tensor(out=rowt[:], in0=r, in1=base[:].unsqueeze(1).broadcast_to([P, TPB, LEAVES3]),
                                           op=ALU.add))
                ch(nc.vector.tensor_tensor(out=rowt[:], in0=rowt[:], in1=onehot[:, b * TPB:(b + 1) * TPB, :], op=ALU.mult))
                ch(nc.vector.tensor_reduce(rowf[:], rowt[:].rearrange("p t (s l) -> p s t l", s=3), AX.X, ALU.add))
                nc.vector.tensor_copy(row_i[:, :, b * TPB:(b + 1) * TPB], rowf[:]).then_inc(s_rows, 1)
            ch(nc.vector.tensor_tensor(
                out=ends[:], in0=incl[0:1].rearrange("p (s l) -> p s l", s=3).unsqueeze(2).broadcast_to([1, 3, SET_TILES, LEAVES]),
                in1=tile_row[:].unsqueeze(1).unsqueeze(3).broadcast_to([1, 3, SET_TILES, LEAVES]), op=ALU.is_le))
            ch(nc.vector.tensor_reduce(leaff[:], ends[:], AX.X, ALU.add))
            ch(nc.vector.tensor_scalar(leaff[:], leaff[:], float(LEAVES - 1), None, ALU.min))
            nc.vector.tensor_tensor(out=leaf_i[:].rearrange("p (s t) -> p s t", s=3), in0=leaff[:],
                                    in1=set_leaf0[:], op=ALU.add).then_inc(s_leaf, 1)

        def rank_pe(pe):
            pe.wait_ge(s_before, NT)
            nc.tensor.matmul(psO[:, 0:LEAVES3], ones_bf[:], before[:, NT, :], start=True, stop=True)\
                .then_inc(N_["b", "rank_done"], 1)
            for b in range(B):
                o = psS[:, b // 2, b % 2, 0:TPB * LEAVES3]
                r = slice(b * TPB, (b + 1) * TPB)
                nc.tensor.matmul(o, tri[:], onehot[:, r, :].rearrange("p t m -> p (t m)"), start=True, stop=False)
                nc.tensor.matmul(o, ones_bf[:], before[:, r, :].rearrange("p t m -> p (t m)"), start=False, stop=True)\
                    .then_inc(N_["b", "rank_done"], 1)

        def scatter_pool(pool):
            pool.wait_ge(s_zfill, N_ZFILL)
            pool.wait_ge(N_["b", "z_ready"], NT)
            for s in range(3):
                for T in range(NT):
                    if s == 0 and T % TPB == 0:
                        pool.wait_ge(s_rows, T // TPB + 1)
                    nc.gpsimd.indirect_dma_start(
                        out=sorted_in[s][:, :], out_offset=bass.IndirectOffsetOnAxis(ap=row_i[:, s, T:T + 1], axis=0),
                        in_=zq[:, T, :], in_offset=None).then_inc(s_scat[s], 16)

        def gather(pool, dst, s, T, done):
            nc.gpsimd.indirect_dma_start(
                out=dst, out_offset=None, in_=sorted_out[s][:, :],
                in_offset=bass.IndirectOffsetOnAxis(ap=row_i[:, s, T:T + 1], axis=0)).then_inc(done, 16)

        def gather_pool(pool):
            for s in range(3):
                pool.wait_ge(s_scat[s], 16 * NT)

            def rows_stored(s):
                for g in range(FS // GB):
                    pool.wait_ge(s_ystore[g], 16 * IT_SET * (s + 1))

            def query(b, k):
                gather(pool, zq[:, k, :], 0, b * TPB + k, s_qgath)

            def key(b, k):
                gather(pool, kg[:, k, :], 1, b * TPB + k, s_kgath)

            def values(b):
                for k in range(TPB):
                    gather(pool, vg[:, b % 2, k, :], 2, b * TPB + k, s_vgath)

            rows_stored(0)
            for k in range(TPB):
                query(0, k)
            rows_stored(1)
            for k in range(TPB):
                key(0, k)
            rows_stored(2)
            pool.wait_ge(N_["f", "y_done"], 3 * SET_TILES)
            for k in range(TPB):
                pool.wait_ge(N_["g", "tr_done"], k + 1)
                key(1, k)
            values(0)
            pool.wait_ge(s_vgath, 16 * TPB)
            values(1)
            for b in range(B - 1):
                for k in range(TPB):
                    pool.wait_ge(N_["g", "tr_done"], TPB + 1 + 2 * (TPB * b + k) + 1)
                    if b + 2 < B:
                        key(b + 2, k)
                    query(b + 1, k)
                if b + 2 < B:
                    pool.wait_ge(N_["g", "pv_done"], TPB * (b + 1))
                    pool.wait_ge(s_vgath, 16 * TPB * (b + 2))
                    values(b + 2)

        def leaf_weights_sync(sp, s):
            r = slice(s * LEAVES, (s + 1) * LEAVES)
            sp.dma_start(w1_all[:, s % 2], ffn["w1b"][r].rearrange("l p n -> p l n")).then_inc(s_leafw[s], 16)
            sp.dma_start(w2_all[:, s % 2], ffn["w2b"][r].rearrange("l p n -> p l n")).then_inc(s_leafw[s], 16)

        def ffn_sync(sp):
            def rows(buf, it, g):
                return buf[bass.ds((it * FS + g * GB) * P, GB * P), :].rearrange("(u p) d -> p u d", p=P)

            def load(s, it, g):
                sp.dma_start(zt[:, g * GB:(g + 1) * GB, :], rows(sorted_in[s], it, g)).then_inc(s_zload[g], 16)

            def store(s, it, g):
                sp.wait_ge(N_["f", "y_copied"], s * SET_TILES + (it * FS + (g + 1) * GB))
                sp.dma_start(rows(sorted_out[s], it, g), yt[:, g * GB:(g + 1) * GB, :]).then_inc(s_ystore[g], 16)

            sp.wait_ge(N_["a", "x_updated"], NT)
            leaf_weights_sync(sp, 0)
            leaf_weights_sync(sp, 1)
            sp.wait_ge(s_leaf, 1)
            for s in range(3):
                sp.wait_ge(s_leafw[s], 32)
                sp.wait_ge(s_scat[s], 16 * NT)
                for g in range(FS // GB):
                    if s:
                        sp.wait_ge(N_["f", "zT_done"], s * SET_TILES - FS + (g + 1) * GB)
                    load(s, 0, g)
                    if s:
                        store(s - 1, IT_SET - 1, g)
                if s == 1:
                    leaf_weights_sync(sp, 2)
                with sp.Fori(1, IT_SET) as it:
                    for g in range(FS // GB):
                        sp.wait_ge(N_["f", "zT_done"], it * FS + (s * SET_TILES - FS + (g + 1) * GB))
                        load(s, it, g)
                        store(s, it - 1, g)
            for g in range(FS // GB):
                store(2, IT_SET - 1, g)

        def ffn_turns(eng, step):
            for it in range(2):
                for u in range(FS):
                    step(it, u, it == 0, False)
            with eng.Fori(2, 3 * IT_SET - 1) as it:
                for u in range(FS):
                    step(it, u, False, False)
            for u in range(FS + 2):
                step(3 * IT_SET - 1, u, False, True)

        def ffn_pe(pe):
            def step(it, u, first, last):
                i = it * FS + u
                if u < FS:
                    if u % GB == 0:
                        pe.wait_ge(s_zload[u // GB], 16 * (it + 1))
                    if not (first and u < 2):
                        pe.wait_ge(N_["f", "zT_copied"], i - 1)
                    for c in range(DC):
                        m = nc.tensor.transpose(psT[:, u % 2, c * P:(c + 1) * P], zt[:, u, c * P:(c + 1) * P], ident[:])
                    m.then_inc(N_["f", "zT_done"], 1)
                if u - 1 < FS and not (first and u < 1):
                    v = (u - 1) % WS
                    pe.wait_ge(N_["f", "w1_copied"], i)
                    if not (first and u < 3):
                        pe.wait_ge(N_["f", "h_copied"], i - 2)
                    for c in range(DC):
                        m = nc.tensor.matmul(psS[0:LEAF_W, 0, (u - 1) % 2, 0:P], w1s[:, v, c * LEAF_W:(c + 1) * LEAF_W],
                                             zT[:, (u - 1) % 2, c, :], start=(c == 0), stop=(c == DC - 1))
                    m.then_inc(N_["f", "h_done"], 1)
                if u - 2 < FS and not (first and u < 2):
                    v = (u - 2) % WS
                    pe.wait_ge(N_["f", "h_copied"], i - 1)
                    pe.wait_ge(N_["f", "w2_copied"], i - 1)
                    if not (first and u < 4):
                        pe.wait_ge(N_["f", "y_copied"], i - 3)
                    nc.tensor.matmul(psS[:, 1, u % 2, 0:D], hT[:, u % 2, :], w2s[:, v, :], start=True, stop=True)\
                        .then_inc(N_["f", "y_done"], 1)
            ffn_turns(pe, step)

        def ffn_act(act):
            def step(it, u, first, last):
                i = it * FS + u
                if u < FS:
                    act.wait_ge(N_["f", "zT_done"], i + 1)
                    if not (first and u < 2):
                        act.wait_ge(N_["f", "h_done"], i - 1)
                    nc.scalar.copy(zT[:, u % 2], psT[:, u % 2, 0:D].rearrange("p (c t) -> p c t", c=DC))\
                        .then_inc(N_["f", "zT_copied"], 1)
                    if not (first and u < WS):
                        act.wait_ge(N_["f", "y_done"], i - WS + 1)
                    r = act.value_load(leaf_i[0:1, bass.ds(i, 1)], min_val=0, max_val=2 * LEAVES - 1)
                    nc.scalar.copy(w1s[:, u % WS, :], w1_of[:, bass.ds(r, 1), :].rearrange("p o n -> p (o n)"))\
                        .then_inc(N_["f", "w1_copied"], 1)
                    nc.scalar.copy(w2s[:, u % WS, :], w2_of[:, bass.ds(r, 1), :].rearrange("p o n -> p (o n)"))\
                        .then_inc(N_["f", "w2_copied"], 1)
            w1_of = w1_all[:].rearrange("p s l n -> p (s l) n")
            w2_of = w2_all[:].rearrange("p s l n -> p (s l) n")
            act.wait_ge(s_leaf, 1)
            ffn_turns(act, step)

        def ffn_dve(dve):
            def step(it, u, first, last):
                i = it * FS + u
                if u - 1 < FS and not (first and u < 1):
                    v = (u - 1) % WS
                    dve.wait_ge(N_["f", "h_done"], i)
                    if not (first and u < 3):
                        dve.wait_ge(N_["f", "y_done"], i - 2)
                    nc.vector.tensor_scalar(hT[0:LEAF_W, (u - 1) % 2, :], psS[0:LEAF_W, 0, (u - 1) % 2, 0:P],
                                            w1s[0:LEAF_W, v, DC * LEAF_W:DC * LEAF_W + 1], 0.0, ALU.add, ALU.max)\
                        .then_inc(N_["f", "h_copied"], 1)
                if u - 2 < FS and not (first and u < 2):
                    v = (u - 2) % FS
                    dve.wait_ge(N_["f", "y_done"], i - 1)
                    n = it if u >= 2 else it - 1
                    if not (isinstance(n, int) and n == 0):
                        dve.wait_ge(s_ystore[v // GB], 16 * n)
                    nc.vector.tensor_copy(yt[:, v, :], psS[:, 1, u % 2, 0:D]).then_inc(N_["f", "y_copied"], 1)
            nc.vector.memset(hT[LEAF_W:LEAF_W + 1, :, :], 1.0)
            ffn_turns(dve, step)

        def sa_bodies(eng, step, chain=None, per=0):
            for k in range(TPB):
                step(0, k, True, False)
            done = chain.base + chain.n if chain else 0
            with eng.Fori(1, B - 1) as b:
                if chain:
                    chain.restart(b * per + (done - per))
                for k in range(TPB):
                    step(b, k, False, False)
                assert not chain or chain.n == per
            if chain:
                chain.restart(done + (B - 2) * per)
            for k in range(TPB + 2):
                step(B - 1, k, False, True)

        def sa_pe(pe):
            def transpose_tile(src, count_free):
                if count_free is not None:
                    pe.wait_ge(N_["g", "lo_ready"], count_free)
                for c in range(DC):
                    m = nc.tensor.transpose(psM[:, c * P:(c + 1) * P], src[:, c * P:(c + 1) * P], ident[:])
                m.then_inc(N_["g", "tr_done"], 1)

            def step(b, k, first, last):
                n = TPB * b + k
                if k < TPB:
                    if k == 0 and not last:
                        pe.wait_ge(s_kgath, 16 * TPB * (b + 2))
                    transpose_tile(kg[:, k, :], 2 * n + TPB + 1)
                    pe.wait_ge(N_["g", "hi_ready"], 2 * n + TPB + 1)
                    if not (first and k < 2):
                        pe.wait_ge(N_["g", "exp_done"], n - 1)
                    parts = [(qt, kt, c) for c in range(DC) for qt, kt in ((q_hi, k_hi), (q_hi, k_lo), (q_lo, k_hi))]
                    for h in range(2):
                        for i, (qt, kt, c) in enumerate(parts):
                            m = nc.tensor.matmul(psS[:, k % 2, h, :], qt[:, k % 2, c, :],
                                                 kt[:, b % 2, c, h * 512:(h + 1) * 512],
                                                 start=(i == 0), stop=(i == len(parts) - 1))
                    m.then_inc(N_["g", "scores_done"], 1)
                    if not (last and k == TPB - 1):
                        if k == TPB - 1:
                            pe.wait_ge(s_qgath, 16 * TPB * (b + 2))
                        transpose_tile(zq[:, (k + 1) % TPB, :], 2 * n + TPB + 2)
                if k - 1 < TPB and not (first and k < 1):
                    pe.wait_ge(N_["g", "exp_done"], n)
                    for h in range(2):
                        if not (first and k < 2):
                            pe.wait_ge(N_["g", "pT_copied"], 2 * (n - 2) + h + 1)
                        for q in range(4):
                            m = nc.tensor.transpose(psT[:, h, q * P:(q + 1) * P],
                                                    pg[:, (k - 1) % 2, (4 * h + q) * P:(4 * h + q + 1) * P], ident[:])
                        m.then_inc(N_["g", "pT_done"], 1)
                if k - 2 < TPB and not (first and k < 2):
                    pe.wait_ge(N_["g", "pT_copied"], 2 * (n - 2) + 2)
                    if not (first and k < 3):
                        pe.wait_ge(N_["g", "x_updated"], n - 2)
                    bb = b if k >= 2 else b - 1
                    if k == 2:
                        pe.wait_ge(s_vgath, 16 * TPB * (b + 1))
                    for q in range(8):
                        m = nc.tensor.matmul(psO[:, 0:D], pgT[:, k % 2, q, :], vg[:, bb % 2, q, :],
                                             start=(q == 0), stop=(q == 7))
                    m.then_inc(N_["g", "pv_done"], 1)

            pe.wait_ge(s_kgath, 16 * TPB)
            pe.wait_ge(s_qgath, 16 * TPB)
            for k in range(TPB):
                transpose_tile(kg[:, k, :], k if k else None)
            transpose_tile(zq[:, 0, :], TPB)
            sa_bodies(pe, step)

        def sa_act(act):
            def upper(dst, n, par):
                act.wait_ge(N_["g", "tr_masked"], n + 1)
                nc.scalar.copy(dst, t_tmp[:, par]).then_inc(N_["g", "hi_ready"], 1)

            def key_upper(b, k, n, par):
                upper(k_hi[:, b % 2, :, k * P:(k + 1) * P], n, par)

            def step(b, k, first, last):
                n = TPB * b + k
                if k - 1 < TPB and not (first and k < 1):
                    act.wait_ge(N_["g", "bias_ready"], n)
                    if not (first and k < 3):
                        act.wait_ge(N_["g", "pT_done"], 2 * (n - 3) + 2)
                    nc.scalar.activation(pg[:, (k - 1) % 2, :], psS[:, (k - 1) % 2].rearrange("p h s -> p (h s)"),
                                         ACT.Exp, bias=nmax[:, (k - 1) % 2:(k - 1) % 2 + 1], scale=SA_SCALE,
                                         accum_out=psum_exp[:, (k - 1) % 4:(k - 1) % 4 + 1])\
                        .then_inc(N_["g", "exp_done"], 1)
                if k < TPB:
                    key_upper(b + 1, k, 2 * n + TPB + 1, 1)
                    if not (last and k == TPB - 1):
                        upper(q_hi[:, (k + 1) % 2], 2 * n + TPB + 2, 0)
                if k - 1 < TPB and not (first and k < 1):
                    if not (first and k < 3):
                        act.wait_ge(N_["g", "pv_done"], n - 2)
                    for h in range(2):
                        act.wait_ge(N_["g", "pT_done"], 2 * (n - 1) + h + 1)
                        nc.scalar.copy(pgT[:, (k - 1) % 2, 4 * h:4 * h + 4, :],
                                       psT[:, h, :].rearrange("p (q t) -> p q t", q=4)).then_inc(N_["g", "pT_copied"], 1)

            for k in range(TPB):
                key_upper(0, k, k, k % 2)
            upper(q_hi[:, 0], TPB, 0)
            sa_bodies(act, step)

        def sa_dve(dve):
            ch = Link(dve, N_["g", "chain"])
            ch_c = Link(dve, N_["c", "chain"])

            def split(lo, n, par):
                dve.wait_ge(N_["g", "tr_done"], n + 1)
                if not (isinstance(n, int) and n < 2):
                    dve.wait_ge(N_["g", "hi_ready"], n - 1)
                    dve.wait_ge(N_["g", "lo_ready"], n - 1)
                src = psM[:, 0:D].rearrange("p (c t) -> p c t", c=DC)
                nc.vector.tensor_scalar(t_tmp[:, par].bitcast(I32), src.bitcast(I32), HIGH_BITS, None, ALU.bitwise_and)\
                    .then_inc(N_["g", "tr_masked"], 1)
                dve.wait_ge(N_["g", "tr_masked"], n + 1)
                nc.vector.tensor_tensor(out=lo, in0=src, in1=t_tmp[:, par], op=ALU.subtract).then_inc(N_["g", "lo_ready"], 1)

            def step(b, k, first, last):
                n = TPB * b + k
                if k < TPB:
                    split(k_lo[:, (b + 1) % 2, :, k * P:(k + 1) * P], 2 * n + TPB + 1, 1)
                    dve.wait_ge(N_["g", "scores_done"], n + 1)
                    par = k % 2
                    ch(nc.vector.tensor_reduce(smax[:, par:par + 1], psS[:, par].rearrange("p h s -> p (h s)"),
                                               AX.X, ALU.max))
                    if not (first and k < 2):
                        dve.wait_ge(N_["g", "exp_done"], n - 1)
                    nc.vector.tensor_scalar(nmax[:, par:par + 1], smax[:, par:par + 1], -SA_SCALE, None, ALU.mult)\
                        .then_inc(N_["g", "bias_ready"], 1)
                    if not (last and k == TPB - 1):
                        split(q_lo[:, (k + 1) % 2], 2 * n + TPB + 2, 0)
                if k - 2 < TPB and not (first and k < 2):
                    T = TPB * b + k - 2
                    dve.wait_ge(N_["g", "pv_done"], n - 1)
                    ch(nc.vector.reciprocal(rsum[:, k % 2:k % 2 + 1], psum_exp[:, (k - 2) % 4:(k - 2) % 4 + 1]))
                    nc.vector.scalar_tensor_tensor(x[:, T, :], psO[:, 0:D], rsum[:, k % 2:k % 2 + 1], x[:, T, :],
                                                   ALU.mult, ALU.add).then_inc(N_["g", "x_updated"], 1)
                if last and k < TPB:
                    tile_stats(ch_c, stat, k, k)
                if last and k == TPB:
                    tiles_rstd(ch_c, stat, mean, rstd)
            for k in range(TPB):
                split(k_lo[:, 0, :, k * P:(k + 1) * P], k, k % 2)
            split(q_lo[:, 0], TPB, 0)
            sa_bodies(dve, step, ch, per=2 * TPB)

        def topk_pe(pe, b):
            pe.wait_ge(s_ohs, b + 1)
            o = psS[:, b // 2, b % 2, 0:EXPERTS * TOPK * TPB]
            nc.tensor.matmul(o, tri[:], ohs[:, b].rearrange("p e q -> p (e q)"), start=True, stop=False)
            nc.tensor.matmul(o, ones_bf[:], ohb[:, b].rearrange("p e q -> p (e q)"), start=False, stop=True)\
                .then_inc(s_xrank, 1)

        def topk_act(act):
            act.wait_ge(s_gap, B)
            nc.scalar.activation(prob[:, 1, :], prob[:, 1, :], ACT.Exp).then_inc(s_gexp, 1)

        def topk_dve(dve):
            ch = Link(dve, N_["d", "chain"])
            dve.wait_ge(N_["c", "x_updated"], NT)
            dve.wait_ge(s_node, 16 * 4)

            def batch(b):
                tiles = slice(TPB * b, TPB * (b + 1))
                dve.wait_ge(N_["d", "node_done"], TPB * (b + 1))
                nc.vector.tensor_tensor(
                    out=logit[:, tiles, :],
                    in0=score_bank(b)[:, 0:TPB * EXPERTS].rearrange("p (t e) -> p t e", t=TPB),
                    in1=routerb[:].unsqueeze(1).broadcast_to([P, TPB, EXPERTS]), op=ALU.add)\
                    .then_inc(N_["d", "scores_used"], 1)
                dve.wait_ge(N_["d", "scores_used"], b + 1)
                for T in range(TPB * b, TPB * (b + 1)):
                    ch.count(nc.vector.max(best[:, T, :], logit[:, T, :]))
                ch.wait()
                for T in range(TPB * b, TPB * (b + 1)):
                    ch.count(nc.vector.max_index(best_i[:, T, :], best[:, T, :], logit[:, T, :]))
                nc.vector.tensor_tensor(out=prob[:, 1, tiles], in0=best[:, tiles, 1], in1=best[:, tiles, 0], op=ALU.subtract)\
                    .then_inc(s_gap, 1)
                ch.wait()
                ch(nc.vector.tensor_copy(choice[:, tiles, :], best_i[:, tiles, 0:TOPK]))
                for k in range(TOPK):
                    ch.count(nc.vector.tensor_tensor(
                        out=ohs[:, b, :, k * TPB:(k + 1) * TPB],
                        in0=choice[:, tiles, k].unsqueeze(1).broadcast_to([P, EXPERTS, TPB]),
                        in1=expert_id[:].unsqueeze(2).broadcast_to([P, EXPERTS, TPB]), op=ALU.is_equal))
                ch.wait()
                ch(nc.vector.tensor_tensor_scan(upto[:].rearrange("p e q -> p (e q)"), scan_on[:].rearrange("p e q -> p (e q)"),
                                                ohs[:, b].rearrange("p e q -> p (e q)"), 0.0, ALU.mult, ALU.add))
                nc.vector.tensor_tensor(out=ohb[:, b], in0=upto[:], in1=ohs[:, b], op=ALU.subtract).then_inc(s_ohs, 1)
                for k in range(TOPK):
                    ch.count(nc.vector.tensor_scalar(xrow[:, k * TPB:(k + 1) * TPB], choice[:, tiles, k],
                                                     float(SLOTS), float(b % BP * CAP - 1), ALU.mult, ALU.add))
                dve.wait_ge(s_xrank, b + 1)
                ch(nc.vector.tensor_tensor(
                    out=rankt[:], in0=psS[:, b // 2, b % 2, 0:EXPERTS * TOPK * TPB].rearrange("p (e q) -> p e q", e=EXPERTS),
                    in1=ohs[:, b], op=ALU.mult))
                ch(nc.vector.tensor_reduce(rankf[:], rankt[:].rearrange("p e q -> p q e"), AX.X, ALU.add))
                ch(nc.vector.scalar_tensor_tensor(xrow[:], rankf[:], float(CAP), xrow[:], ALU.min, ALU.add))
                nc.vector.tensor_copy(read_i[:, b, :], xrow[:]).then_inc(s_rows, 1)
                ch(nc.vector.tensor_scalar(rankf[:], rankf[:], float(CAP), None, ALU.is_le))
                ch(nc.vector.tensor_tensor(out=xrow[:], in0=xrow[:], in1=trash[:, b, :], op=ALU.subtract))
                ch(nc.vector.tensor_tensor(out=xrow[:], in0=xrow[:], in1=rankf[:], op=ALU.mult))
                nc.vector.tensor_tensor(out=write_i[:, b, :], in0=xrow[:], in1=trash[:, b, :], op=ALU.add).then_inc(s_rows, 1)
            route_dve(ch, "d", batch)
            dve.wait_ge(s_gexp, 1)
            ch(nc.vector.tensor_scalar(prob[:, 0, :], prob[:, 1, :], 1.0, None, ALU.add))
            ch(nc.vector.reciprocal(prob[:, 0, :], prob[:, 0, :]))
            ch(nc.vector.tensor_tensor(out=prob[:, 1, :], in0=prob[:, 1, :], in1=prob[:, 0, :], op=ALU.mult))

        def dispatch_pool(pool):
            for b in range(B):
                pool.wait_ge(s_rows, B + 2 * (b + 1))
                for k in range(TOPK):
                    for t in range(TPB):
                        nc.gpsimd.indirect_dma_start(
                            out=slots_in[b // BP][:, :],
                            out_offset=bass.IndirectOffsetOnAxis(ap=write_i[:, b, k * TPB + t:k * TPB + t + 1], axis=0),
                            in_=zq[:, b * TPB + t, :], in_offset=None).then_inc(s_disp[b // BP], 16)

        EP = PASSES * EXPERTS // 2
        ROWT = -(-SLOTS // P)
        FROM = [0, ROWT - BT, ROWT]
        BLOCKS = [min(b * P, SLOTS) - a * P for a, b in zip(FROM, FROM[1:])]
        HCH = HID // P

        def rows_of(i):
            return min(P, SLOTS - i * P)

        def turns(eng, body):
            body(0, True, False)
            with eng.Fori(1, EP - 1) as t:
                body(t, False, False)
            body(EP - 1, False, True)

        def moe_sync(sp):
            def load_projection(e, n):
                if not (isinstance(n, int) and n == 0):
                    sp.wait_ge(N_["e", "o_done"], n * ROWT)
                sp.dma_start(wp[:], moe["w_p"][e].rearrange("(m p) n -> p m n", p=P)).then_inc(s_wpload, 16)

            def load(p, e, n, q, first=False, before=None):
                if not (isinstance(n, int) and n == 0):
                    sp.wait_ge(N_["e", "w_hi_ready"], n * HCH)
                    sp.wait_ge(N_["e", "w_lo_ready"], n * HCH)
                for which, name in enumerate(("w_c", "w_g")):
                    sp.dma_start(w_raw[:, which], moe[name][e].rearrange("(c p) h -> p c h", p=P)).then_inc(s_rawload, 16)
                if before is not None:
                    load_projection(before, n - 1)
                if not first:
                    sp.wait_ge(N_["e", "o_copied"], (n - 1) * ROWT)
                sp.dma_start(bcg[:, q], moe["b_cg"][e]).then_inc(s_wload[q], 16)
                sp.dma_start(bp[:, q], moe["b_p"][e].partition_broadcast(P)).then_inc(s_wload[q], 16)
                sp.wait_ge(s_disp[p], 16 * TOPK * NTP)
                r = (ROWT - 1) * P
                sp.dma_start(xr[:, q, 0:ROWT - 1, :], slots_in[p][bass.ds(e * SLOTS, r), :].rearrange("(i p) d -> p i d", p=P))\
                    .then_inc(s_xload[q], 16)
                sp.dma_start(xr[0:SLOTS - r, q, ROWT - 1, :], slots_in[p][bass.ds(e * SLOTS + r, SLOTS - r), :])\
                    .then_inc(s_xload[q], 16)

            sp.wait_ge(N_["c", "x_updated"], NT)
            load(0, 0, 0, 0, True)
            load(0, 1, 1, 1, True, before=0)
            with sp.Fori(1, EP // 2) as t:
                for q in range(2):
                    load(0, 2 * t + q, 2 * t + q, q, before=2 * t + (q - 1))
            for q in range(2):
                load(1, q, EXPERTS + q, q, before=(q - 1) % EXPERTS)
            with sp.Fori(1, EP // 2) as t:
                for q in range(2):
                    load(1, 2 * t + q, 2 * t + (EXPERTS + q), q, before=2 * t + (q - 1))
            load_projection(EXPERTS - 1, 2 * EXPERTS - 1)

        NB = len(BLOCKS)

        def tile_ahead(fn, t, pos, j, last):
            q, blk = divmod(pos + 1, NB)
            if q == 2:
                if last:
                    return
                t, q, blk = t + 1, 0, 0
            if FROM[blk] + j < FROM[blk + 1]:
                fn(t, q, blk, FROM[blk] + j)

        def tile_behind(fn, t, pos, j, first):
            if pos == 0 and first:
                return
            q, blk = divmod(pos - 1, NB) if pos else (1, NB - 1)
            if FROM[blk] + j < FROM[blk + 1]:
                fn(t if pos else t - 1, q, blk, FROM[blk] + j, first)

        def moe_pe(pe):
            def transpose_tile(t, q, blk, i):
                if i == 0:
                    pe.wait_ge(s_xload[q], 32 * (t + 1))
                n = t * (2 * ROWT) + (q * ROWT + i)
                if not (isinstance(n, int) and n < 2):
                    pe.wait_ge(N_["e", "x_lo_ready"], n - 1)
                r = rows_of(i)
                for c in range(DC):
                    m = nc.tensor.transpose(psT[:, (q * ROWT + i) % 2, c * P:c * P + r], xr[0:r, q, i, c * P:(c + 1) * P], ident[0:r, 0:r])
                m.then_inc(N_["e", "xT_done"], 1)

            def output_tile(t, q, blk, i, first):
                n = t * (2 * ROWT) + (q * ROWT + i)
                r = rows_of(i)
                if i == 0:
                    pe.wait_ge(s_wpload, t * 32 + 16 * (q + 1))
                if i == FROM[blk]:
                    pe.wait_ge(N_["e", "silu_done"], ((t * 2 + q) * NB + blk + 1) * HCH)
                if not (first and n < 2):
                    pe.wait_ge(N_["e", "o_copied"], n - 1)
                par = (q * NB + blk) % 2
                po = (psO, psM)[(q * ROWT + i) % 2]
                for m_ in range(HCH):
                    m = nc.tensor.matmul(po[0:r, 0:D], st[par][:, m_, (i - FROM[blk]) * P:(i - FROM[blk]) * P + r], wp[:, m_, :],
                                         start=(m_ == 0), stop=(m_ == HCH - 1))
                m.then_inc(N_["e", "o_done"], 1)

            def body(t, first, last):
                for q in range(2):
                    for blk, w in enumerate(BLOCKS):
                        pos = q * NB + blk
                        par = pos % 2
                        if blk == 0:
                            pe.wait_ge(s_wload[q], 32 * (t + 1))
                        for half in ("x_hi_ready", "x_lo_ready"):
                            pe.wait_ge(N_["e", half], t * (2 * ROWT) + (q * ROWT + FROM[blk + 1]))
                        for m_ in range(HCH):
                            n = (t * 2 * NB + pos) * HCH + m_
                            if not (first and pos == 0 and m_ < 2):
                                pe.wait_ge(N_["e", "gated"], n - 1)
                            if blk == 0:
                                for half in ("w_hi_ready", "w_lo_ready"):
                                    pe.wait_ge(N_["e", half], t * (2 * HCH) + (q * HCH + m_ + 1))
                            parts = [(wt, xt, c) for c in range(DC) for wt, xt in ((w_hi, x_hi), (w_lo, x_hi), (w_hi, x_lo))]
                            for which in range(2):
                                for k, (wt, xt, c) in enumerate(parts):
                                    m = nc.tensor.matmul(psS[:, m_ % 2, which, 0:w], wt[:, which, c, m_ * P:(m_ + 1) * P],
                                                         xt[:, par, c, 0:w], start=(k == 0), stop=(k == len(parts) - 1))
                                m.then_inc(N_["e", "hg_done"], 1)
                            if m_ == 1:
                                for j in range(BT):
                                    tile_ahead(transpose_tile, t, pos, j, last)
                                    tile_behind(output_tile, t, pos, j, first)
                if last:
                    for i in range(FROM[NB - 1], ROWT):
                        output_tile(t, 1, NB - 1, i, False)

            for i in range(FROM[1]):
                transpose_tile(0, 0, 0, i)
            pe.wait_ge(s_rows, 3 * B)
            turns(pe, body)

        def moe_act(act):
            def tile_upper(t, q, blk, i):
                n = t * (2 * ROWT) + (q * ROWT + i)
                r = rows_of(i)
                act.wait_ge(N_["e", "x_masked"], n + 1)
                nc.scalar.copy(x_hi[:, (q * NB + blk) % 2, :, (i - FROM[blk]) * P:(i - FROM[blk]) * P + r], x_tmp[:, (q * ROWT + i) % 2, :, 0:r])\
                    .then_inc(N_["e", "x_hi_ready"], 1)

            def weights_upper(n, m_):
                act.wait_ge(N_["e", "w_masked"], n + 1)
                nc.scalar.copy(w_hi[:, :, :, m_ * P:(m_ + 1) * P], w_tmp[:, m_ % 2]).then_inc(N_["e", "w_hi_ready"], 1)

            def silu(n, par, m_, w, first):
                act.wait_ge(N_["e", "gated"], n + 1)
                nc.scalar.activation(st[par][:, m_, 0:w], hg[:, m_ % 2, 0:w], ACT.Silu).then_inc(N_["e", "silu_done"], 1)

            def body(t, first, last):
                for q in range(2):
                    for blk, w in enumerate(BLOCKS):
                        pos = q * NB + blk
                        for m_ in range(HCH):
                            n = (t * 2 * NB + pos) * HCH + m_
                            act.wait_ge(N_["e", "hg_done"], 2 * n + 1)
                            if not (first and pos == 0 and m_ < 2):
                                act.wait_ge(N_["e", "gated"], n - 1)
                            nc.scalar.activation(hb[:, m_ % 2, 0:w], psS[:, m_ % 2, 0, 0:w], ACT.Identity,
                                                 bias=bcg[:, q, m_:m_ + 1]).then_inc(N_["e", "h_ready"], 1)
                            if m_ == 0:
                                if pos or not first:
                                    silu(n - 1, (pos + 1) % 2, HCH - 1, BLOCKS[(pos - 1) % NB], first)
                            else:
                                if m_ == 1 and not (first and pos < 2):
                                    a, b_ = divmod(pos - 2, NB) if pos >= 2 else (1, pos - 2 + NB)
                                    tt = t if pos >= 2 else t - 1
                                    act.wait_ge(N_["e", "o_done"], tt * (2 * ROWT) + (a * ROWT + FROM[b_ + 1]))
                                silu(n - 1, pos % 2, m_ - 1, w, first)
                            if m_ == 1:
                                for j in range(BT):
                                    tile_ahead(tile_upper, t, pos, j, last)
                            if blk == NB - 1 and m_ and not (last and q == 1):
                                weights_upper(t * (2 * HCH) + ((q + 1) * HCH + m_ - 1), m_ - 1)
                            if blk == 0 and m_ == 0 and not (first and q == 0):
                                weights_upper(t * (2 * HCH) + (q * HCH + HCH - 1), HCH - 1)
                if last:
                    silu(EP * 2 * NB * HCH - 1, 1, HCH - 1, BLOCKS[NB - 1], False)

            for m_ in range(HCH):
                if m_ == 3:
                    for i in range(FROM[1]):
                        tile_upper(0, 0, 0, i)
                weights_upper(m_, m_)
            turns(act, body)

        def moe_dve(dve):
            def split_tile(t, q, blk, i):
                n = t * (2 * ROWT) + (q * ROWT + i)
                r, k = rows_of(i), (q * ROWT + i) % 2
                dve.wait_ge(N_["e", "xT_done"], n + 1)
                if not (isinstance(n, int) and n < 2):
                    dve.wait_ge(N_["e", "x_hi_ready"], n - 1)
                    dve.wait_ge(N_["e", "x_lo_ready"], n - 1)
                src = psT[:, k, 0:DC * P].rearrange("p (c t) -> p c t", c=DC)[:, :, 0:r]
                tmp = x_tmp[:, k, :, 0:r]
                nc.vector.tensor_scalar(tmp.bitcast(I32), src.bitcast(I32), HIGH_BITS, None, ALU.bitwise_and)\
                    .then_inc(N_["e", "x_masked"], 1)
                dve.wait_ge(N_["e", "x_masked"], n + 1)
                nc.vector.tensor_tensor(out=x_lo[:, (q * NB + blk) % 2, :, (i - FROM[blk]) * P:(i - FROM[blk]) * P + r], in0=src, in1=tmp,
                                        op=ALU.subtract).then_inc(N_["e", "x_lo_ready"], 1)

            def split_weights(n, m_):
                src = w_raw[:, :, :, m_ * P:(m_ + 1) * P]
                tmp = w_tmp[:, m_ % 2]
                if not (isinstance(n, int) and n < 2):
                    dve.wait_ge(N_["e", "w_hi_ready"], n - 1)
                    dve.wait_ge(N_["e", "w_lo_ready"], n - 1)
                nc.vector.tensor_scalar(tmp.bitcast(I32), src.bitcast(I32), HIGH_BITS, None, ALU.bitwise_and)\
                    .then_inc(N_["e", "w_masked"], 1)
                dve.wait_ge(N_["e", "w_masked"], n + 1)
                nc.vector.tensor_tensor(out=w_lo[:, :, :, m_ * P:(m_ + 1) * P], in0=src, in1=tmp, op=ALU.subtract)\
                    .then_inc(N_["e", "w_lo_ready"], 1)

            def output_tile(t, q, blk, i, first):
                n = t * (2 * ROWT) + (q * ROWT + i)
                r = rows_of(i)
                dve.wait_ge(N_["e", "o_done"], n + 1)
                if not (first and n < YS):
                    k = (2 * t + q) * (ROWT // YS) + i // YS
                    dve.wait_ge(s_ostore[i % YS], k * 16)
                nc.vector.tensor_tensor(out=yo[0:r, i % YS, :], in0=(psO, psM)[(q * ROWT + i) % 2][0:r, 0:D], in1=bp[0:r, q, :],
                                        op=ALU.add).then_inc(N_["e", "o_copied"], 1)

            def body(t, first, last):
                for q in range(2):
                    for blk, w in enumerate(BLOCKS):
                        pos = q * NB + blk
                        for m_ in range(HCH):
                            n = (t * 2 * NB + pos) * HCH + m_
                            dve.wait_ge(N_["e", "hg_done"], 2 * n + 2)
                            dve.wait_ge(N_["e", "h_ready"], n + 1)
                            if not (first and pos == 0 and m_ < 2):
                                dve.wait_ge(N_["e", "silu_done"], n - 1)
                            nc.vector.scalar_tensor_tensor(hg[:, m_ % 2, 0:w], psS[:, m_ % 2, 1, 0:w],
                                                           bcg[:, q, HCH + m_:HCH + m_ + 1], hb[:, m_ % 2, 0:w],
                                                           ALU.add, ALU.mult).then_inc(N_["e", "gated"], 1)
                            if m_ == 1:
                                for j in range(BT):
                                    tile_ahead(split_tile, t, pos, j, last)
                                    tile_behind(output_tile, t, pos, j, first)
                            if blk == NB - 1 and not (last and q == 1):
                                if m_ == 0:
                                    dve.wait_ge(s_rawload, t * 64 + 32 * (q + 2))
                                split_weights(t * (2 * HCH) + ((q + 1) * HCH + m_), m_)
                if last:
                    for i in range(FROM[NB - 1], ROWT):
                        output_tile(t, 1, NB - 1, i, False)

            def combine(T, g, u):
                dve.wait_ge(s_yload[u], 32 * (g + 1))
                nc.vector.scalar_tensor_tensor(x[:, T, :], yg[:, u, 0, :], prob[:, 0, bass.ds(T, 1)], x[:, T, :],
                                               ALU.mult, ALU.add).then_inc(s_half, 1)
                dve.wait_ge(s_half, T + 1)
                nc.vector.scalar_tensor_tensor(x[:, T, :], yg[:, u, 1, :], prob[:, 1, bass.ds(T, 1)], x[:, T, :],
                                               ALU.mult, ALU.add).then_inc(s_fin, 1)

            dve.wait_ge(s_disp[0], 16 * TOPK * NTP)
            dve.wait_ge(s_rawload, 32)
            for m_ in range(HCH):
                if m_ == 3:
                    for i in range(FROM[1]):
                        split_tile(0, 0, 0, i)
                split_weights(m_, m_)
            body(0, True, False)
            with dve.Fori(1, EP // 2 + 1) as t:
                body(t, False, False)
            with dve.Fori(EP // 2 + 1, EP - 1) as t:
                body(t, False, False)
                for u in range(GS):
                    combine((t - EP // 2 - 1) * GS + u, t - EP // 2 - 1, u)
            body(EP - 1, False, True)
            for u in range(GS):
                combine((EP // 2 - 2) * GS + u, EP // 2 - 2, u)
            with dve.Fori(EP // 2 - 1, NT // GS) as g:
                for u in range(GS):
                    combine(g * GS + u, g, u)

        def moe_pool(pool):
            def store(p, e, n):
                for i in range(ROWT):
                    r = rows_of(i)
                    pool.wait_ge(N_["e", "o_copied"], n * ROWT + i + 1)
                    pool.dma_start(slots_out[p][bass.ds(e * SLOTS + i * P, r), :], yo[0:r, i % YS, :])\
                        .then_inc(s_ostore[i % YS], 16)

            def pass_stored(p):
                for u in range(YS):
                    pool.wait_ge(s_ostore[u], 16 * (p + 1) * EXPERTS * ROWT // YS)

            def gathers(T):
                if T >= GS:
                    pool.wait_ge(s_fin, T - GS + 1)
                for k in range(TOPK):
                    nc.gpsimd.indirect_dma_start(
                        out=yg[:, T % GS, k, :], out_offset=None, in_=slots_out[T // NTP][:, :],
                        in_offset=bass.IndirectOffsetOnAxis(ap=read_i[:, T // TPB, k * TPB + T % TPB:k * TPB + T % TPB + 1], axis=0))\
                        .then_inc(s_yload[T % GS], 16)

            with pool.Fori(0, EXPERTS) as e:
                store(0, e, e)
            pass_stored(0)
            pool.wait_ge(s_disp[1], 16 * TOPK * NTP)
            for e in range(EXPERTS):
                store(1, e, EXPERTS + e)
                if e % 2:
                    for u in range(GS):
                        gathers(e // 2 * GS + u)
            pass_stored(1)
            for T in range(NTP, NT):
                gathers(T)

        def final_sync(sp):
            with sp.Fori(0, NT // GS) as g:
                sp.wait_ge(s_fin, g * GS + GS)
                sp.dma_start(out_v[:, bass.ds(g * GS, GS), :], x[:, bass.ds(g * GS, GS), :]).then_inc(s_out, 16)
            sp.wait_ge(s_out, 16 * (NT // GS))

        block = es.enter_context(nc.Block())

        @block.sync
        def _(sp):
            prep_sync(sp)
            route_sync(sp)
            ffn_sync(sp)
            moe_sync(sp)
            final_sync(sp)

        @block.gpsimd
        def _(pool):
            prep_pool(pool)
            pool.wait_ge(s_w, 16 * N_W)
            xattn_pool(pool, "a")
            scatter_pool(pool)
            gather_pool(pool)
            xattn_pool(pool, "c")
            dispatch_pool(pool)
            moe_pool(pool)

        @block.scalar
        def _(act):
            prep_loads_act(act)
            prep_act(act)
            xattn_act(act, "a")
            route_act(act, "b")
            ffn_act(act)
            sa_act(act)
            xattn_act(act, "c")
            route_act(act, "d")
            topk_act(act)
            moe_act(act)

        @block.vector
        def _(dve):
            prep_dve_mask(dve)
            xattn_dve(dve, "a")
            tree_dve(dve)
            ffn_dve(dve)
            sa_dve(dve)
            xattn_dve(dve, "c")
            topk_dve(dve)
            moe_dve(dve)

        @block.tensor
        def _(pe):
            prep_pe(pe)
            xattn_pe(pe, "a")
            route_pe(pe, "b", nodew, NODES3, lambda b: None)
            rank_pe(pe)
            ffn_pe(pe)
            sa_pe(pe)
            xattn_pe(pe, "c")
            route_pe(pe, "d", routerw, EXPERTS, lambda b: topk_pe(pe, b))
            moe_pe(pe)


def kernel(**inputs):
    import numpy as np
    import concourse.bacc as bacc
    from concourse.bass_utils import run_bass_kernel_spmd

    nc = bacc.Bacc("TRN2", target_bir_lowering=False, num_devices=1)
    arrays = {}

    def dram(name, a=None):
        a = np.ascontiguousarray(inputs[name] if a is None else a)
        arrays[f"in_{name}"] = a
        return nc.dram_tensor(f"in_{name}", a.shape, mybir.dt.from_np(a.dtype), kind="ExternalInput").ap()

    def weight(k, name, transposed=False):
        a = np.asarray(inputs[name])
        if transposed and k[0] == "w":
            a = a.T
        if k in ("bq", "bk"):
            a = a.reshape(DC, P).T
        return dram(name, a)

    xa = {
        "a": {k: weight(k, f"L0_xattn_{n}") for k, n in (("wq", "W_Q"), ("bq", "b_Q"), ("wk", "W_K"), ("bk", "b_K"),
                                                    ("wv", "W_V"), ("bv", "b_V"), ("wo", "W_O"), ("bo", "b_O"))},
        "c": {k: weight(k, f"L1_xattn_{n}", transposed=True)
              for k, n in (("wq", "q_w"), ("bq", "q_b"), ("wk", "k_w"), ("bk", "k_b"), ("wv", "v_w"), ("bv", "v_b"))},
    }
    trees = [{k: np.asarray(inputs[f"L0_ffn_{t}_{k}"]) for k in ("node_w", "node_b", "w1", "b1", "w2", "b2")} for t in "qkv"]

    def leaf_in(t):
        w = t["w1"].reshape(LEAVES, DC, P, LEAF_W).transpose(0, 2, 1, 3).reshape(LEAVES, P, DC * LEAF_W)
        b = np.zeros((LEAVES, P, 2), w.dtype)
        b[:, 0:LEAF_W, 0] = t["b1"]
        return np.concatenate([w, b], axis=2)

    ffn = {
        "node_w": dram("ffn_node_w", np.concatenate([t["node_w"] for t in trees]).T),
        "node_b": dram("ffn_node_b", np.concatenate([t["node_b"] for t in trees])),
        "w1b": dram("ffn_w1b", np.concatenate([leaf_in(t) for t in trees])),
        "w2b": dram("ffn_w2b", np.concatenate([np.concatenate([t["w2"], t["b2"][:, None, :]], axis=1) for t in trees])),
    }
    def bias_columns(name):
        return np.asarray(inputs[name]).reshape(EXPERTS, HID // P, P).transpose(0, 2, 1)

    moe = {
        "router_w": dram("L1_ffn_router_w"), "router_b": dram("L1_ffn_router_b"),
        "w_c": dram("L1_ffn_w_c_fc"), "w_g": dram("L1_ffn_w_gate"), "w_p": dram("L1_ffn_w_c_proj"),
        "b_cg": dram("moe_b_cg", np.concatenate([bias_columns("L1_ffn_b_c_fc"), bias_columns("L1_ffn_b_gate")], axis=2)),
        "b_p": dram("L1_ffn_b_c_proj", np.asarray(inputs["L1_ffn_b_c_proj"]).reshape(EXPERTS, D)),
    }
    x_in, ctx_in, mask_in = dram("x"), dram("ctx_1024"), dram("mask_BxS2_ik0")
    out = nc.dram_tensor("out", x_in.shape, F32, kind="ExternalOutput").ap()
    xattn_ffn_kernel(nc, x_in, ctx_in, mask_in, xa, ffn, moe, out)
    r = run_bass_kernel_spmd(nc, [arrays], core_ids=[0])
    return r.results[0]["out"]
```
